# Optimizing a Trainium2 kernel written in Bass

```python
import numpy as np
import jax
import jax.numpy as jnp

def _softmax(x, axis=-1):
    return jax.nn.softmax(x, axis=axis)

def _gelu(x):
    return jax.nn.gelu(x, approximate=True)

def _silu(x):
    return jax.nn.silu(x)

def _sigmoid(x):
    return jax.nn.sigmoid(x)

def _layernorm(x, axis=-1, eps=1e-05):
    m = jnp.mean(x, axis=axis, keepdims=True)
    v = jnp.var(x, axis=axis, keepdims=True)
    return (x - m) / jnp.sqrt(v + eps)

def _scatter_add(tgt, idx, src, axis=0):
    return tgt.at[idx].add(src)

def _segment_sum(src, seg, n):
    return jax.ops.segment_sum(src, seg, n)
kernel_name = 'mk_decoder_preln_d4_seqx_r8_21dc7b'

def setup_inputs(seed: int=0):
    np.random.seed(seed)
    _w = jnp.asarray

    def _rec_inputs():
        import jax
        import jax.numpy as jnp
        _rk = jax.random.key(seed)
        x = -0.0002928 + 1 * jax.random.normal(jax.random.fold_in(_rk, 1), (2, 512, 128), jnp.float32)
        _lenS = 512 - jax.random.randint(jax.random.fold_in(_rk, 7), (2,), 0, max(1, 512 // 4) + 1, jnp.int32)
        _lenS2 = 77 - jax.random.randint(jax.random.fold_in(_rk, 8), (2,), 0, max(1, 77 // 4) + 1, jnp.int32)
        _ctx_768P = jax.random.normal(jax.random.fold_in(_rk, 11), (2, 16, 96), jnp.float32)
        _ctx_768c = jax.random.dirichlet(jax.random.fold_in(_rk, 511), 0.3 * jnp.ones((16,), jnp.float32), (2, 77))
        _ctx_768t = jnp.einsum('bsk,bkd->bsd', _ctx_768c, _ctx_768P)
        _ctx_768t = _ctx_768t * jax.lax.rsqrt(jnp.mean(jnp.square(_ctx_768t)) + 1e-12) * 0.953939
        ctx_768 = 2.09791e-05 + 1.00001 * (_ctx_768t + 0.3 * jax.random.normal(jax.random.fold_in(_rk, 611), (2, 77, 96), jnp.float32))
        _validS = jnp.arange(512)[None, :] < _lenS[:, None]
        _validS2 = jnp.arange(77)[None, :] < _lenS2[:, None]
        _causal = jnp.tril(jnp.ones((512, 512), dtype=bool))
        mask_BxS2_bf1 = jnp.ones((2, 77), dtype=bool)
        mask_BxS2_bk0 = jnp.logical_not(jnp.broadcast_to(_validS2[:, :], (2, 77)))
        return (x, ctx_768, mask_BxS2_bf1, mask_BxS2_bk0)
    x, ctx_768, mask_BxS2_bf1, mask_BxS2_bk0 = _rec_inputs()

    def _L0_attn_setup():
        import jax, jax.numpy as jnp
        import numpy as np
        B, S, D, H = (2, 256, 128, 16)
        HD = D // H
        key = jax.random.key(seed)
        k1, k2, k3 = jax.random.split(key, 3)
        x = jax.random.normal(k1, (B, S, D), dtype=jnp.float32)
        c_attn_kernel = 0.02 * jax.random.normal(k2, (3 * D, D), dtype=jnp.float32)
        c_attn_bias = jnp.zeros((3 * D,), dtype=jnp.float32)
        c_proj_kernel = 0.02 * jax.random.normal(k3, (D, D), dtype=jnp.float32)
        c_proj_bias = jnp.zeros((D,), dtype=jnp.float32)
        return {'hidden_states': x, 'c_attn_kernel': c_attn_kernel, 'c_attn_bias': c_attn_bias, 'c_proj_kernel': c_proj_kernel, 'c_proj_bias': c_proj_bias}
    _L0_attn_all = _L0_attn_setup()
    _L0_attn_in = {k: v for k, v in _L0_attn_all.items() if k in ('c_attn_kernel', 'c_attn_bias', 'c_proj_kernel', 'c_proj_bias')}
    del _L0_attn_all

    def _L0_xattn_setup():
        import jax, jax.numpy as jnp
        import numpy as np
        import math
        B, N, M = (4, 128, 128)
        DIM, CTX_DIM = (128, 96)
        HEADS, DIM_HEAD = (16, 64)
        INNER = HEADS * DIM_HEAD

        def layer_norm(t, g, eps=1e-05):
            mean = jnp.mean(t, axis=-1, keepdims=True)
            var = jnp.mean((t - mean) ** 2, axis=-1, keepdims=True)
            return (t - mean) * jax.lax.rsqrt(var + eps) * g
        key = jax.random.key(seed)
        ks = jax.random.split(key, 8)
        return {'x': jax.random.normal(ks[0], (B, N, DIM), jnp.float32), 'context': jax.random.normal(ks[1], (B, M, CTX_DIM), jnp.float32), 'mask': jnp.ones((B, M), dtype=bool), 'g_norm': jnp.ones((DIM,), jnp.float32), 'null_kv': jax.random.normal(ks[2], (2, DIM_HEAD), jnp.float32), 'Wq': jax.random.normal(ks[3], (DIM, INNER), jnp.float32) * DIM ** (-0.5), 'Wkv': jax.random.normal(ks[4], (CTX_DIM, 2 * INNER), jnp.float32) * CTX_DIM ** (-0.5), 'Wout': jax.random.normal(ks[5], (INNER, DIM), jnp.float32) * INNER ** (-0.5), 'g_out': jnp.ones((DIM,), jnp.float32)}
    _L0_xattn_all = _L0_xattn_setup()
    _L0_xattn_in = {k: v for k, v in _L0_xattn_all.items() if k in ('g_norm', 'null_kv', 'Wq', 'Wkv', 'Wout', 'g_out')}
    del _L0_xattn_all

    def _L0_ffn_setup():
        import jax, jax.numpy as jnp
        import numpy as np
        TOP_P = 0.8
        B, T, H, F, E = (2, 256, 128, 512, 8)
        key = jax.random.key(seed)
        k0, k1, k2, k3 = jax.random.split(key, 4)
        x = jax.random.normal(k0, (B, T, H), jnp.float32)
        Wr = jax.random.normal(k1, (H, E), jnp.float32) * 0.02
        br = jnp.zeros((E,), jnp.float32)
        W1 = jax.random.normal(k2, (E, H, F), jnp.float32) * 0.02
        b1 = jnp.zeros((E, F), jnp.float32)
        W2 = jax.random.normal(k3, (E, F, H), jnp.float32) * 0.02
        b2 = jnp.zeros((E, H), jnp.float32)
        return {'x': x, 'Wr': Wr, 'br': br, 'W1': W1, 'b1': b1, 'W2': W2, 'b2': b2}
    _L0_ffn_all = _L0_ffn_setup()
    _L0_ffn_in = {k: v for k, v in _L0_ffn_all.items() if k in ('Wr', 'br', 'W1', 'b1', 'W2', 'b2')}
    del _L0_ffn_all

    def _L1_attn_setup():
        import jax, jax.numpy as jnp
        import numpy as np
        B, L, D = (2, 256, 128)
        H, HD = (16, 64)
        LD = 32
        key = jax.random.key(seed)
        ks = jax.random.split(key, 6)
        s = lambda fan_in: 1.0 / np.sqrt(fan_in)
        x_bld = jax.random.normal(ks[0], (B, L, D), dtype=jnp.float32)
        Wq = jax.random.normal(ks[1], (D, H, HD), dtype=jnp.float32) * s(D)
        Wkv_down = jax.random.normal(ks[2], (D, LD), dtype=jnp.float32) * s(D)
        Wk_up = jax.random.normal(ks[3], (LD, H, HD), dtype=jnp.float32) * s(LD)
        Wv_up = jax.random.normal(ks[4], (LD, H, HD), dtype=jnp.float32) * s(LD)
        Wout = jax.random.normal(ks[5], (H, HD, D), dtype=jnp.float32) * s(H * HD)
        return {'x_bld': x_bld, 'Wq': Wq, 'Wkv_down': Wkv_down, 'Wk_up': Wk_up, 'Wv_up': Wv_up, 'Wout': Wout}
    _L1_attn_all = _L1_attn_setup()
    _L1_attn_in = {k: v for k, v in _L1_attn_all.items() if k in ('Wq', 'Wkv_down', 'Wk_up', 'Wv_up', 'Wout')}
    del _L1_attn_all

    def _L1_xattn_setup():
        import jax, jax.numpy as jnp
        import numpy as np
        DIM_IN, DIM_LAT, DIM_HEAD = (96, 128, 64)
        INNER = max(DIM_LAT, DIM_IN)
        HEADS = INNER // DIM_HEAD
        SCALE = DIM_HEAD ** (-0.5)
        RMS_EPS = 1e-08
        LN_EPS = 1e-05

        def layernorm(x, g, b):
            mu = jnp.mean(x, axis=-1, keepdims=True)
            var = jnp.mean((x - mu) ** 2, axis=-1, keepdims=True)
            return (x - mu) * jax.lax.rsqrt(var + LN_EPS) * g + b

        def rmsnorm(x, gamma):
            norm = jnp.sqrt(jnp.sum(x * x, axis=-1, keepdims=True)) * x.shape[-1] ** (-0.5)
            return x / jnp.maximum(norm, RMS_EPS) * gamma
        key = jax.random.key(seed)
        ks = jax.random.split(key, 12)
        b, n, m = (4, 512, 64)
        x = jax.random.normal(ks[0], (b, n, DIM_IN), jnp.float32)
        latents = jax.random.normal(ks[1], (b, m, DIM_LAT), jnp.float32)
        mask = jax.random.randint(ks[2], (b, n), 0, 2).astype(bool)
        s = lambda k, sh, fan: jax.random.normal(k, sh, jnp.float32) * fan ** (-0.5)
        return {'x': x, 'latents': latents, 'mask': mask, 'ln_x_g': jnp.ones((DIM_IN,), jnp.float32), 'ln_x_b': jnp.zeros((DIM_IN,), jnp.float32), 'ln_l_g': jnp.ones((DIM_LAT,), jnp.float32), 'ln_l_b': jnp.zeros((DIM_LAT,), jnp.float32), 'qn_g': jnp.ones((DIM_HEAD,), jnp.float32), 'kn_g': jnp.ones((DIM_HEAD,), jnp.float32), 'Wq': s(ks[3], (INNER, DIM_LAT), DIM_LAT), 'Wkv': s(ks[4], (2 * INNER, DIM_IN), DIM_IN), 'Wlkv': s(ks[5], (2 * INNER, DIM_LAT), DIM_LAT), 'Wo': s(ks[6], (DIM_LAT, INNER), INNER), 'bo': jnp.zeros((DIM_LAT,), jnp.float32)}
    _L1_xattn_all = _L1_xattn_setup()
    _L1_xattn_in = {k: v for k, v in _L1_xattn_all.items() if k in ('ln_x_g', 'ln_x_b', 'ln_l_g', 'ln_l_b', 'qn_g', 'kn_g', 'Wq', 'Wkv', 'Wlkv', 'Wo', 'bo')}
    del _L1_xattn_all

    def _L1_ffn_setup():
        import jax, jax.numpy as jnp
        import numpy as np
        DIM = 128
        HIDDEN = 384
        SCALE = 1.0 / 127.0

        def _dequant(w_int, dtype):
            return w_int.astype(dtype) * jnp.asarray(SCALE, dtype)
        key = jax.random.key(seed)
        k_x, k_g, k_u, k_d = jax.random.split(key, 4)
        x = jax.random.normal(k_x, (4, 256, DIM), dtype=jnp.float32)
        w_gate = jax.random.randint(k_g, (HIDDEN, DIM), -127, 128, dtype=jnp.int32)
        w_up = jax.random.randint(k_u, (HIDDEN, DIM), -127, 128, dtype=jnp.int32)
        w_down = jax.random.randint(k_d, (DIM, HIDDEN), -127, 128, dtype=jnp.int32)
        return {'x': x, 'w_gate': w_gate, 'w_up': w_up, 'w_down': w_down}
    _L1_ffn_all = _L1_ffn_setup()
    _L1_ffn_in = {k: v for k, v in _L1_ffn_all.items() if k in ('w_gate', 'w_up', 'w_down')}
    del _L1_ffn_all

    def _L2_attn_setup():
        import jax, jax.numpy as jnp
        import numpy as np
        N_HEAD = 16
        HEAD_SIZE = 128
        EMBED = 128
        MULTI_HEAD_SIZE = HEAD_SIZE // N_HEAD
        B, S = (4, 256)
        key = jax.random.key(seed)
        k1, k2, k3, k4 = jax.random.split(key, 4)
        x = jax.random.normal(k1, (B, S, EMBED), dtype=jnp.float32)
        w_qkv = jax.random.normal(k2, (3 * HEAD_SIZE, EMBED), dtype=jnp.float32) * 0.02
        w_proj = jax.random.normal(k3, (EMBED, HEAD_SIZE), dtype=jnp.float32) * 0.02
        b_proj = jax.random.normal(k4, (EMBED,), dtype=jnp.float32) * 0.02
        return {'x': x, 'w_qkv': w_qkv, 'w_proj': w_proj, 'b_proj': b_proj}
    _L2_attn_all = _L2_attn_setup()
    _L2_attn_in = {k: v for k, v in _L2_attn_all.items() if k in ('w_qkv', 'w_proj', 'b_proj')}
    del _L2_attn_all

    def _L2_xattn_setup():
        import jax, jax.numpy as jnp
        import numpy as np
        NUM_HEADS = 16
        CLAMP = 10000.0
        key = jax.random.key(seed)
        ks = jax.random.split(key, 8)
        B, Nq, Nkv, Cq, Ckv = (4, 256, 256, 128, 96)
        s_q = 1.0 / np.sqrt(Cq)
        s_kv = 1.0 / np.sqrt(Ckv)
        return {'query': jax.random.normal(ks[0], (B, Nq, Cq), jnp.float32), 'key_value': jax.random.normal(ks[1], (B, Nkv, Ckv), jnp.float32), 'Wq': jax.random.normal(ks[2], (Cq, Cq), jnp.float32) * s_q, 'bq': jnp.zeros((Cq,), jnp.float32), 'Wk': jax.random.normal(ks[3], (Ckv, Cq), jnp.float32) * s_kv, 'bk': jnp.zeros((Cq,), jnp.float32), 'Wv': jax.random.normal(ks[4], (Ckv, Cq), jnp.float32) * s_kv, 'bv': jnp.zeros((Cq,), jnp.float32), 'Wo': jax.random.normal(ks[5], (Cq, Cq), jnp.float32) * s_q, 'bo': jnp.zeros((Cq,), jnp.float32)}
    _L2_xattn_all = _L2_xattn_setup()
    _L2_xattn_in = {k: v for k, v in _L2_xattn_all.items() if k in ('Wq', 'bq', 'Wk', 'bk', 'Wv', 'bv', 'Wo', 'bo')}
    del _L2_xattn_all

    def _L2_ffn_setup():
        import jax, jax.numpy as jnp
        import numpy as np
        import math
        B, L, D = (4, 512, 128)
        F = 512
        E = 16
        CAP_FACTOR = 1.0
        EPS = 1e-05
        key = jax.random.key(seed)
        ks = jax.random.split(key, 8)
        std = 0.02
        return {'x': jax.random.normal(ks[0], (B, L, D), dtype=jnp.float32), 'norm_weight': jnp.ones((D,), dtype=jnp.float32), 'router_weight': jax.random.normal(ks[1], (E, D), dtype=jnp.float32) * std, 'router_bias': jnp.zeros((E,), dtype=jnp.float32), 'fc1_weight': jax.random.normal(ks[2], (E, F, D), dtype=jnp.float32) * std, 'fc1_bias': jnp.zeros((E, F), dtype=jnp.float32), 'fc2_weight': jax.random.normal(ks[3], (E, D, F), dtype=jnp.float32) * std, 'fc2_bias': jnp.zeros((E, D), dtype=jnp.float32)}
    _L2_ffn_all = _L2_ffn_setup()
    _L2_ffn_in = {k: v for k, v in _L2_ffn_all.items() if k in ('norm_weight', 'router_weight', 'router_bias', 'fc1_weight', 'fc1_bias', 'fc2_weight', 'fc2_bias')}
    del _L2_ffn_all

    def _L3_attn_setup():
        import jax, jax.numpy as jnp
        import numpy as np
        from jax import lax
        H = 16
        D_CONV = 4
        NORMALIZER = 16.0
        EPS = 1e-05

        def _causal_conv_silu(x, w):
            B, L, D = x.shape
            xp = jnp.pad(x, ((0, 0), (D_CONV - 1, 0), (0, 0)))
            y = sum((xp[:, k:k + L, :] * w[:, k] for k in range(D_CONV)))
            return jax.nn.silu(y)

        def _gla_scan(q, k, v, gk):
            B, h, L, dk = q.shape
            dv = v.shape[-1]
            qT = jnp.moveaxis(q, 2, 0)
            kT = jnp.moveaxis(k, 2, 0)
            vT = jnp.moveaxis(v, 2, 0)
            gT = jnp.moveaxis(gk, 2, 0)

            def step(S, inp):
                qt, kt, vt, gt = inp
                S = S * jnp.exp(gt)[..., None] + kt[..., None] * vt[..., None, :]
                ot = jnp.einsum('bhk,bhkv->bhv', qt, S)
                return (S, ot)
            S0 = jnp.zeros((B, h, dk, dv), q.dtype)
            S, o = lax.scan(step, S0, (qT, kT, vT, gT))
            return (jnp.moveaxis(o, 0, 2), S)

        def _reference_tuple_inner(x, conv_w, Wq, Wkg, Wv, Wg, bg, Wout, aug_balance):
            xb = jnp.swapaxes(x, 0, 1)
            xb = _causal_conv_silu(xb, conv_w)
            q = xb @ Wq
            k_gate = xb @ Wkg
            v = xb @ Wv
            g = xb @ Wg + bg
            gk = jax.nn.log_sigmoid(k_gate) / NORMALIZER
            k = 1.0 - jnp.exp(gk)
            B, L, _ = q.shape
            split = lambda t: t.reshape(B, L, H, -1).transpose(0, 2, 1, 3)
            qh, kh, gkh, vh = (split(q), split(k), split(gk), split(v))
            dk = qh.shape[-1]
            o, new_state = _gla_scan(qh * dk ** (-0.5), kh, vh, gkh)
            aug = aug_balance.reshape(H, dk)
            aug_w = jnp.einsum('bhlk,hk,bhlk->bhl', qh, aug, kh)
            o = o + jax.nn.sigmoid(aug_w[..., None] * vh)
            mu = o.mean(-1, keepdims=True)
            var = o.var(-1, keepdims=True)
            o = (o - mu) * lax.rsqrt(var + EPS)
            o = o.transpose(0, 2, 1, 3).reshape(B, L, -1)
            out = jax.nn.silu(g) * o @ Wout
            return (jnp.swapaxes(out, 0, 1), new_state)
        key = jax.random.key(seed)
        ks = jax.random.split(key, 9)
        L, B, D = (1024, 8, 128)
        s = lambda fan: 1.0 / np.sqrt(fan)
        return {'x': jax.random.normal(ks[0], (L, B, D), jnp.float32), 'conv_w': jax.random.normal(ks[1], (D, D_CONV), jnp.float32) * s(D_CONV), 'Wq': jax.random.normal(ks[2], (D, D // 2), jnp.float32) * s(D), 'Wkg': jax.random.normal(ks[3], (D, D // 2), jnp.float32) * s(D), 'Wv': jax.random.normal(ks[4], (D, D), jnp.float32) * s(D), 'Wg': jax.random.normal(ks[5], (D, D), jnp.float32) * s(D), 'bg': jax.random.normal(ks[6], (D,), jnp.float32) * 0.02, 'Wout': jax.random.normal(ks[7], (D, D), jnp.float32) * s(D), 'aug_balance': jnp.zeros((D // 2,), jnp.float32)}
    _L3_attn_all = _L3_attn_setup()
    _L3_attn_in = {k: v for k, v in _L3_attn_all.items() if k in ('conv_w', 'Wq', 'Wkg', 'Wv', 'Wg', 'bg', 'Wout', 'aug_balance')}
    del _L3_attn_all

    def _L3_xattn_setup():
        import jax, jax.numpy as jnp
        import numpy as np
        N_HEADS = 16
        DIMS = 128
        D_CTX = 96
        HEAD = DIMS // N_HEADS
        key = jax.random.key(seed)
        ks = jax.random.split(key, 10)
        s_q = 1.0 / np.sqrt(DIMS)
        s_c = 1.0 / np.sqrt(D_CTX)
        return {'x': jax.random.normal(ks[0], (2, 256, DIMS), jnp.float32), 'context': jax.random.normal(ks[1], (2, 256, D_CTX), jnp.float32), 'w_q': jax.random.normal(ks[2], (DIMS, DIMS), jnp.float32) * s_q, 'b_q': jax.random.normal(ks[3], (DIMS,), jnp.float32) * 0.01, 'w_k': jax.random.normal(ks[4], (D_CTX, DIMS), jnp.float32) * s_c, 'b_k': jax.random.normal(ks[5], (DIMS,), jnp.float32) * 0.01, 'w_v': jax.random.normal(ks[6], (D_CTX, DIMS), jnp.float32) * s_c, 'b_v': jax.random.normal(ks[7], (DIMS,), jnp.float32) * 0.01, 'w_o': jax.random.normal(ks[8], (DIMS, DIMS), jnp.float32) * s_q, 'b_o': jax.random.normal(ks[9], (DIMS,), jnp.float32) * 0.01}
    _L3_xattn_all = _L3_xattn_setup()
    _L3_xattn_in = {k: v for k, v in _L3_xattn_all.items() if k in ('w_q', 'b_q', 'w_k', 'b_k', 'w_v', 'b_v', 'w_o', 'b_o')}
    del _L3_xattn_all

    def _L3_ffn_setup():
        import jax, jax.numpy as jnp
        import numpy as np
        D, H, P, E, K, F = (128, 16, 64, 8, 2, 512)
        B, S = (2, 256)
        NROT = 32
        BASE = 10000.0
        EPS = 1e-05

        def _ln(x, g, b):
            m = jnp.mean(x, -1, keepdims=True)
            v = jnp.mean(jnp.square(x - m), -1, keepdims=True)
            return (x - m) * jax.lax.rsqrt(v + EPS) * g + b

        def _rope(x):
            xr, xp = (x[..., :NROT], x[..., NROT:])
            half = NROT // 2
            inv = BASE ** (-jnp.arange(half, dtype=jnp.float32) / half)
            ang = jnp.arange(x.shape[2], dtype=jnp.float32)[:, None] * inv[None, :]
            cos, sin = (jnp.cos(ang), jnp.sin(ang))
            x1, x2 = (xr[..., :half], xr[..., half:])
            xr = jnp.concatenate([x1 * cos - x2 * sin, x1 * sin + x2 * cos], -1)
            return jnp.concatenate([xr, xp], -1)

        def _gate(x, Wsel):
            s = jax.nn.sigmoid(jnp.einsum('bsd,hed->bhse', x, Wsel))
            _, idx = jax.lax.top_k(s, K)
            mask = jax.nn.one_hot(idx, E, dtype=s.dtype).sum(-2)
            return s * mask

        def _moe_attn(x, Wq, Wk, Wv, Wo, Wsel_v, Wsel_o):
            q = _rope(jnp.einsum('bsd,hdp->bhsp', x, Wq))
            k = _rope(jnp.einsum('bsd,hdp->bhsp', x, Wk))
            gv = _gate(x, Wsel_v)
            v = jnp.einsum('bsd,bhse,hedp->bhsp', x, gv, Wv)
            att = jax.nn.softmax(jnp.einsum('bhsp,bhtp->bhst', q, k) / np.sqrt(P), axis=-1)
            o = jnp.einsum('bhst,bhtp->bhsp', att, v)
            go = _gate(x, Wsel_o)
            return jnp.einsum('bhsp,bhse,hepd->bsd', o, go, Wo)
        key = jax.random.key(seed)
        ks = jax.random.split(key, 10)
        f = lambda k, sh: jax.random.normal(k, sh, jnp.float32) * 0.02
        return dict(src=jax.random.normal(ks[0], (B, S, D), jnp.float32), Wq=f(ks[1], (H, D, P)), Wk=f(ks[2], (H, D, P)), Wv=f(ks[3], (H, E, D, P)), Wo=f(ks[4], (H, E, P, D)), Wsel_v=f(ks[5], (H, E, D)), Wsel_o=f(ks[6], (H, E, D)), ln1_g=jnp.ones(D, jnp.float32), ln1_b=jnp.zeros(D, jnp.float32), ln2_g=jnp.ones(D, jnp.float32), ln2_b=jnp.zeros(D, jnp.float32), W1=f(ks[7], (D, F)), b1=jnp.zeros(F, jnp.float32), W2=f(ks[8], (F, D)), b2=jnp.zeros(D, jnp.float32))
    _L3_ffn_all = _L3_ffn_setup()
    _L3_ffn_in = {k: v for k, v in _L3_ffn_all.items() if k in ('Wq', 'Wk', 'Wv', 'Wo', 'Wsel_v', 'Wsel_o', 'ln1_g', 'ln1_b', 'ln2_g', 'ln2_b', 'W1', 'b1', 'W2', 'b2')}
    del _L3_ffn_all
    return {'x': x, 'ctx_768': ctx_768, 'mask_BxS2_bf1': mask_BxS2_bf1, 'mask_BxS2_bk0': mask_BxS2_bk0, 'L0_attn_c_attn_kernel': _L0_attn_in['c_attn_kernel'], 'L0_attn_c_attn_bias': _L0_attn_in['c_attn_bias'], 'L0_attn_c_proj_kernel': _L0_attn_in['c_proj_kernel'], 'L0_attn_c_proj_bias': _L0_attn_in['c_proj_bias'], 'L0_xattn_g_norm': _L0_xattn_in['g_norm'], 'L0_xattn_null_kv': _L0_xattn_in['null_kv'], 'L0_xattn_Wq': _L0_xattn_in['Wq'], 'L0_xattn_Wkv': _L0_xattn_in['Wkv'], 'L0_xattn_Wout': _L0_xattn_in['Wout'], 'L0_xattn_g_out': _L0_xattn_in['g_out'], 'L0_ffn_Wr': _L0_ffn_in['Wr'], 'L0_ffn_br': _L0_ffn_in['br'], 'L0_ffn_W1': _L0_ffn_in['W1'], 'L0_ffn_b1': _L0_ffn_in['b1'], 'L0_ffn_W2': _L0_ffn_in['W2'], 'L0_ffn_b2': _L0_ffn_in['b2'], 'L1_attn_Wq': _L1_attn_in['Wq'], 'L1_attn_Wkv_down': _L1_attn_in['Wkv_down'], 'L1_attn_Wk_up': _L1_attn_in['Wk_up'], 'L1_attn_Wv_up': _L1_attn_in['Wv_up'], 'L1_attn_Wout': _L1_attn_in['Wout'], 'L1_xattn_ln_x_g': _L1_xattn_in['ln_x_g'], 'L1_xattn_ln_x_b': _L1_xattn_in['ln_x_b'], 'L1_xattn_ln_l_g': _L1_xattn_in['ln_l_g'], 'L1_xattn_ln_l_b': _L1_xattn_in['ln_l_b'], 'L1_xattn_qn_g': _L1_xattn_in['qn_g'], 'L1_xattn_kn_g': _L1_xattn_in['kn_g'], 'L1_xattn_Wq': _L1_xattn_in['Wq'], 'L1_xattn_Wkv': _L1_xattn_in['Wkv'], 'L1_xattn_Wlkv': _L1_xattn_in['Wlkv'], 'L1_xattn_Wo': _L1_xattn_in['Wo'], 'L1_xattn_bo': _L1_xattn_in['bo'], 'L1_ffn_w_gate': _L1_ffn_in['w_gate'], 'L1_ffn_w_up': _L1_ffn_in['w_up'], 'L1_ffn_w_down': _L1_ffn_in['w_down'], 'L2_attn_w_qkv': _L2_attn_in['w_qkv'], 'L2_attn_w_proj': _L2_attn_in['w_proj'], 'L2_attn_b_proj': _L2_attn_in['b_proj'], 'L2_xattn_Wq': _L2_xattn_in['Wq'], 'L2_xattn_bq': _L2_xattn_in['bq'], 'L2_xattn_Wk': _L2_xattn_in['Wk'], 'L2_xattn_bk': _L2_xattn_in['bk'], 'L2_xattn_Wv': _L2_xattn_in['Wv'], 'L2_xattn_bv': _L2_xattn_in['bv'], 'L2_xattn_Wo': _L2_xattn_in['Wo'], 'L2_xattn_bo': _L2_xattn_in['bo'], 'L2_ffn_norm_weight': _L2_ffn_in['norm_weight'], 'L2_ffn_router_weight': _L2_ffn_in['router_weight'], 'L2_ffn_router_bias': _L2_ffn_in['router_bias'], 'L2_ffn_fc1_weight': _L2_ffn_in['fc1_weight'], 'L2_ffn_fc1_bias': _L2_ffn_in['fc1_bias'], 'L2_ffn_fc2_weight': _L2_ffn_in['fc2_weight'], 'L2_ffn_fc2_bias': _L2_ffn_in['fc2_bias'], 'L3_attn_conv_w': _L3_attn_in['conv_w'], 'L3_attn_Wq': _L3_attn_in['Wq'], 'L3_attn_Wkg': _L3_attn_in['Wkg'], 'L3_attn_Wv': _L3_attn_in['Wv'], 'L3_attn_Wg': _L3_attn_in['Wg'], 'L3_attn_bg': _L3_attn_in['bg'], 'L3_attn_Wout': _L3_attn_in['Wout'], 'L3_attn_aug_balance': _L3_attn_in['aug_balance'], 'L3_xattn_w_q': _L3_xattn_in['w_q'], 'L3_xattn_b_q': _L3_xattn_in['b_q'], 'L3_xattn_w_k': _L3_xattn_in['w_k'], 'L3_xattn_b_k': _L3_xattn_in['b_k'], 'L3_xattn_w_v': _L3_xattn_in['w_v'], 'L3_xattn_b_v': _L3_xattn_in['b_v'], 'L3_xattn_w_o': _L3_xattn_in['w_o'], 'L3_xattn_b_o': _L3_xattn_in['b_o'], 'L3_ffn_Wq': _L3_ffn_in['Wq'], 'L3_ffn_Wk': _L3_ffn_in['Wk'], 'L3_ffn_Wv': _L3_ffn_in['Wv'], 'L3_ffn_Wo': _L3_ffn_in['Wo'], 'L3_ffn_Wsel_v': _L3_ffn_in['Wsel_v'], 'L3_ffn_Wsel_o': _L3_ffn_in['Wsel_o'], 'L3_ffn_ln1_g': _L3_ffn_in['ln1_g'], 'L3_ffn_ln1_b': _L3_ffn_in['ln1_b'], 'L3_ffn_ln2_g': _L3_ffn_in['ln2_g'], 'L3_ffn_ln2_b': _L3_ffn_in['ln2_b'], 'L3_ffn_W1': _L3_ffn_in['W1'], 'L3_ffn_b1': _L3_ffn_in['b1'], 'L3_ffn_W2': _L3_ffn_in['W2'], 'L3_ffn_b2': _L3_ffn_in['b2']}

def reference(x, ctx_768, mask_BxS2_bf1, mask_BxS2_bk0, L0_attn_c_attn_kernel, L0_attn_c_attn_bias, L0_attn_c_proj_kernel, L0_attn_c_proj_bias, L0_xattn_g_norm, L0_xattn_null_kv, L0_xattn_Wq, L0_xattn_Wkv, L0_xattn_Wout, L0_xattn_g_out, L0_ffn_Wr, L0_ffn_br, L0_ffn_W1, L0_ffn_b1, L0_ffn_W2, L0_ffn_b2, L1_attn_Wq, L1_attn_Wkv_down, L1_attn_Wk_up, L1_attn_Wv_up, L1_attn_Wout, L1_xattn_ln_x_g, L1_xattn_ln_x_b, L1_xattn_ln_l_g, L1_xattn_ln_l_b, L1_xattn_qn_g, L1_xattn_kn_g, L1_xattn_Wq, L1_xattn_Wkv, L1_xattn_Wlkv, L1_xattn_Wo, L1_xattn_bo, L1_ffn_w_gate, L1_ffn_w_up, L1_ffn_w_down, L2_attn_w_qkv, L2_attn_w_proj, L2_attn_b_proj, L2_xattn_Wq, L2_xattn_bq, L2_xattn_Wk, L2_xattn_bk, L2_xattn_Wv, L2_xattn_bv, L2_xattn_Wo, L2_xattn_bo, L2_ffn_norm_weight, L2_ffn_router_weight, L2_ffn_router_bias, L2_ffn_fc1_weight, L2_ffn_fc1_bias, L2_ffn_fc2_weight, L2_ffn_fc2_bias, L3_attn_conv_w, L3_attn_Wq, L3_attn_Wkg, L3_attn_Wv, L3_attn_Wg, L3_attn_bg, L3_attn_Wout, L3_attn_aug_balance, L3_xattn_w_q, L3_xattn_b_q, L3_xattn_w_k, L3_xattn_b_k, L3_xattn_w_v, L3_xattn_b_v, L3_xattn_w_o, L3_xattn_b_o, L3_ffn_Wq, L3_ffn_Wk, L3_ffn_Wv, L3_ffn_Wo, L3_ffn_Wsel_v, L3_ffn_Wsel_o, L3_ffn_ln1_g, L3_ffn_ln1_b, L3_ffn_ln2_g, L3_ffn_ln2_b, L3_ffn_W1, L3_ffn_b1, L3_ffn_W2, L3_ffn_b2):
    import jax
    import jax.numpy as jnp

    def _L0_attn_ref(hidden_states, c_attn_kernel, c_attn_bias, c_proj_kernel, c_proj_bias):
        import jax, jax.numpy as jnp
        import numpy as np
        B, S, D, H = (2, 256, 128, 16)
        HD = D // H
        b, s, d = hidden_states.shape
        qkv = hidden_states @ c_attn_kernel.T + c_attn_bias
        q, k, v = jnp.split(qkv, 3, axis=2)
        q = q.reshape(b, s, H, HD)
        k = k.reshape(b, s, H, HD)
        v = v.reshape(b, s, H, HD)
        causal = jnp.tril(jnp.ones((s, s), dtype=bool))
        neg = jnp.finfo(jnp.float32).min
        bias = jnp.where(causal, 0.0, neg).astype(jnp.float32)
        scale = 1.0 / jnp.sqrt(jnp.float32(HD))
        scores = jnp.einsum('bqhd,bkhd->bhqk', q * scale, k) + bias
        attn_weights = jax.nn.softmax(scores, axis=-1)
        attn_output = jnp.einsum('bhqk,bkhd->bqhd', attn_weights, v)
        attn_output = attn_output.reshape(b, s, d)
        out = attn_output @ c_proj_kernel.T + c_proj_bias
        return out

    def _L0_xattn_ref(x, context, mask, g_norm, null_kv, Wq, Wkv, Wout, g_out):
        import jax, jax.numpy as jnp
        import numpy as np
        import math
        B, N, M = (4, 128, 128)
        DIM, CTX_DIM = (128, 96)
        HEADS, DIM_HEAD = (16, 64)
        INNER = HEADS * DIM_HEAD

        def layer_norm(t, g, eps=1e-05):
            mean = jnp.mean(t, axis=-1, keepdims=True)
            var = jnp.mean((t - mean) ** 2, axis=-1, keepdims=True)
            return (t - mean) * jax.lax.rsqrt(var + eps) * g
        b = x.shape[0]
        scale = DIM_HEAD ** (-0.5)
        sqrt_scale = math.sqrt(scale)
        x = layer_norm(x, g_norm)
        q = x @ Wq
        kv = context @ Wkv
        k, v = jnp.split(kv, 2, axis=-1)

        def to_heads(t):
            return t.reshape(b, t.shape[1], HEADS, DIM_HEAD).transpose(0, 2, 1, 3)
        q, k, v = (to_heads(q), to_heads(k), to_heads(v))
        nk = jnp.broadcast_to(null_kv[0], (b, HEADS, 1, DIM_HEAD))
        nv = jnp.broadcast_to(null_kv[1], (b, HEADS, 1, DIM_HEAD))
        k = jnp.concatenate([nk, k], axis=2)
        v = jnp.concatenate([nv, v], axis=2)
        q = q * sqrt_scale
        k = k * sqrt_scale
        sim = jnp.einsum('bhid,bhjd->bhij', q, k)
        max_neg = -jnp.finfo(sim.dtype).max
        full_mask = jnp.pad(mask, ((0, 0), (1, 0)), constant_values=True)
        sim = jnp.where(full_mask[:, None, None, :], sim, max_neg)
        attn = jax.nn.softmax(sim.astype(jnp.float32), axis=-1).astype(sim.dtype)
        out = jnp.einsum('bhij,bhjd->bhid', attn, v)
        out = out.transpose(0, 2, 1, 3).reshape(b, -1, INNER)
        out = out @ Wout
        return layer_norm(out, g_out)

    def _L0_ffn_ref(x, Wr, br, W1, b1, W2, b2):
        import jax, jax.numpy as jnp
        import numpy as np
        TOP_P = 0.8
        B, T, H, F, E = (2, 256, 128, 512, 8)
        probs = jax.nn.softmax(x @ Wr + br, axis=-1)
        sorted_idx = jnp.argsort(-probs, axis=-1)
        sorted_probs = jnp.take_along_axis(probs, sorted_idx, axis=-1)
        cum = jnp.cumsum(sorted_probs, axis=-1)
        mask = cum < TOP_P
        mask = mask.at[..., 0].set(True)
        inv = jnp.argsort(sorted_idx, axis=-1)
        keep = jnp.take_along_axis(mask, inv, axis=-1)
        gate = probs * keep
        h = jax.nn.relu(jnp.einsum('bth,ehf->betf', x, W1) + b1[None, :, None, :])
        y = jnp.einsum('betf,efh->beth', h, W2) + b2[None, :, None, :]
        return jnp.einsum('bte,beth->bth', gate, y)

    def _L1_attn_ref(x_bld, Wq, Wkv_down, Wk_up, Wv_up, Wout):
        import jax, jax.numpy as jnp
        import numpy as np
        B, L, D = (2, 256, 128)
        H, HD = (16, 64)
        LD = 32
        q_blhd = jnp.einsum('bld,dhk->blhk', x_bld, Wq)
        latent_bll = jnp.einsum('bld,dc->blc', x_bld, Wkv_down)
        k_blhd = jnp.einsum('blc,chk->blhk', latent_bll, Wk_up)
        v_blhd = jnp.einsum('blc,chk->blhk', latent_bll, Wv_up)
        attn = jnp.einsum('bqhd,bkhd->bhqk', q_blhd, k_blhd) / jnp.sqrt(jnp.asarray(HD, dtype=x_bld.dtype))
        l = x_bld.shape[1]
        mask = (jnp.arange(l)[None, :] <= jnp.arange(l)[:, None])[None, None]
        neg_inf = jnp.finfo(attn.dtype).min
        attn = jax.nn.softmax(jnp.where(mask, attn, neg_inf), axis=-1)
        y_blhd = jnp.einsum('bhqk,bkhd->bqhd', attn, v_blhd)
        return jnp.einsum('bqhd,hdo->bqo', y_blhd, Wout)

    def _L1_xattn_ref(x, latents, mask, ln_x_g, ln_x_b, ln_l_g, ln_l_b, qn_g, kn_g, Wq, Wkv, Wlkv, Wo, bo):
        import jax, jax.numpy as jnp
        import numpy as np
        DIM_IN, DIM_LAT, DIM_HEAD = (96, 128, 64)
        INNER = max(DIM_LAT, DIM_IN)
        HEADS = INNER // DIM_HEAD
        SCALE = DIM_HEAD ** (-0.5)
        RMS_EPS = 1e-08
        LN_EPS = 1e-05

        def layernorm(x, g, b):
            mu = jnp.mean(x, axis=-1, keepdims=True)
            var = jnp.mean((x - mu) ** 2, axis=-1, keepdims=True)
            return (x - mu) * jax.lax.rsqrt(var + LN_EPS) * g + b

        def rmsnorm(x, gamma):
            norm = jnp.sqrt(jnp.sum(x * x, axis=-1, keepdims=True)) * x.shape[-1] ** (-0.5)
            return x / jnp.maximum(norm, RMS_EPS) * gamma
        b, n, _ = x.shape
        m = latents.shape[1]
        xn = layernorm(x, ln_x_g, ln_x_b)
        ln = layernorm(latents, ln_l_g, ln_l_b)
        q = ln @ Wq.T
        kv = jnp.concatenate([xn @ Wkv.T, ln @ Wlkv.T], axis=1)
        k, v = (kv[..., :INNER], kv[..., INNER:])
        split_heads = lambda t: t.reshape(t.shape[0], t.shape[1], HEADS, DIM_HEAD).transpose(0, 2, 1, 3)
        q, k, v = (split_heads(q), split_heads(k), split_heads(v))
        qn = rmsnorm(q, qn_g) * SCALE
        kn = rmsnorm(k, kn_g)
        attn = jnp.einsum('bhid,bhjd->bhij', qn, kn)
        full_mask = jnp.pad(mask, ((0, 0), (0, m)), constant_values=True)
        attn = jnp.where(full_mask[:, None, None, :], attn, -jnp.finfo(attn.dtype).max)
        attn = jax.nn.softmax(attn, axis=-1)
        out = jnp.einsum('bhij,bhjd->bhid', attn, v)
        out = out.transpose(0, 2, 1, 3).reshape(b, m, INNER)
        return out @ Wo.T + bo

    def _L1_ffn_ref(x, w_gate, w_up, w_down):
        import jax, jax.numpy as jnp
        import numpy as np
        DIM = 128
        HIDDEN = 384
        SCALE = 1.0 / 127.0

        def _dequant(w_int, dtype):
            return w_int.astype(dtype) * jnp.asarray(SCALE, dtype)
        wg = _dequant(w_gate, x.dtype)
        wu = _dequant(w_up, x.dtype)
        wd = _dequant(w_down, x.dtype)
        gate = jnp.einsum('bsd,hd->bsh', x, wg)
        up = jnp.einsum('bsd,hd->bsh', x, wu)
        h = jax.nn.silu(gate) * up
        return jnp.einsum('bsh,dh->bsd', h, wd)

    def _L2_attn_ref(x, w_qkv, w_proj, b_proj):
        import jax, jax.numpy as jnp
        import numpy as np
        N_HEAD = 16
        HEAD_SIZE = 128
        EMBED = 128
        MULTI_HEAD_SIZE = HEAD_SIZE // N_HEAD
        B, S = (4, 256)
        qkv = jnp.einsum('bse,he->bsh', x, w_qkv)
        q, k, v = jnp.split(qkv, 3, axis=-1)
        scale = 1.0 / np.sqrt(MULTI_HEAD_SIZE).astype(np.float32)
        scores = jnp.einsum('bqh,bkh->bqk', q, k) * scale
        probs = jax.nn.softmax(scores, axis=-1)
        out = jnp.einsum('bqk,bkh->bqh', probs, v)
        Bn, Sn, H = out.shape
        out = jnp.swapaxes(out, 1, 2).reshape(Bn, Sn, H)
        out = jnp.einsum('bsh,eh->bse', out, w_proj) + b_proj
        return out

    def _L2_xattn_ref(query, key_value, Wq, bq, Wk, bk, Wv, bv, Wo, bo):
        import jax, jax.numpy as jnp
        import numpy as np
        NUM_HEADS = 16
        CLAMP = 10000.0
        B, Nq, Cq = query.shape
        Nkv = key_value.shape[1]
        H = NUM_HEADS
        D = Cq // H
        scale = D ** (-0.5)
        q = (query @ Wq + bq).reshape(B, Nq, H, D).transpose(0, 2, 1, 3)
        k = (key_value @ Wk + bk).reshape(B, Nkv, H, D).transpose(0, 2, 1, 3)
        v = (key_value @ Wv + bv).reshape(B, Nkv, H, D).transpose(0, 2, 1, 3)
        attn = jnp.einsum('bhqd,bhkd->bhqk', q, k) * scale
        attn = jnp.clip(attn, -CLAMP, CLAMP)
        attn = jax.nn.softmax(attn, axis=-1)
        attn = jnp.where(jnp.any(jnp.isnan(attn)), jnp.asarray(1.0 / Nkv, attn.dtype), attn)
        x = jnp.einsum('bhqk,bhkd->bqhd', attn, v).reshape(B, Nq, Cq)
        return x @ Wo + bo

    def _L2_ffn_ref(x, norm_weight, router_weight, router_bias, fc1_weight, fc1_bias, fc2_weight, fc2_bias):
        import jax, jax.numpy as jnp
        import numpy as np
        import math
        B, L, D = (4, 512, 128)
        F = 512
        E = 16
        CAP_FACTOR = 1.0
        EPS = 1e-05
        b, l, d = x.shape
        n_tokens = b * l
        n_experts = router_weight.shape[0]
        capacity = max(1, math.ceil(CAP_FACTOR * n_tokens / n_experts))
        top_k = min(capacity, n_tokens)
        xf = x.reshape(n_tokens, d)
        rms = jnp.sqrt(jnp.mean(xf * xf, axis=-1, keepdims=True) + EPS)
        xn = xf / rms * norm_weight
        logits = xn @ router_weight.T + router_bias
        probs = jax.nn.softmax(logits, axis=-1)
        _, idx = jax.lax.top_k(logits.T, top_k)
        xe = xn[idx]
        h = jnp.einsum('ecd,efd->ecf', xe, fc1_weight) + fc1_bias[:, None, :]
        h = jax.nn.gelu(h, approximate=False)
        y = jnp.einsum('ecf,edf->ecd', h, fc2_weight) + fc2_bias[:, None, :]
        gates = jnp.take_along_axis(probs.T, idx, axis=1)
        flat_idx = idx.reshape(-1)
        contrib = (y * gates[:, :, None]).reshape(-1, d)
        output = jnp.zeros((n_tokens, d), dtype=x.dtype).at[flat_idx].add(contrib)
        gate_sums = jnp.zeros((n_tokens, 1), dtype=x.dtype).at[flat_idx].add(gates.reshape(-1, 1))
        assigned = gate_sums > 0
        output = jnp.where(assigned, output / jnp.where(assigned, gate_sums, 1.0), output)
        return output.reshape(b, l, d)

    def _L3_attn_ref(x, conv_w, Wq, Wkg, Wv, Wg, bg, Wout, aug_balance):
        import jax, jax.numpy as jnp
        import numpy as np
        from jax import lax
        H = 16
        D_CONV = 4
        NORMALIZER = 16.0
        EPS = 1e-05

        def _causal_conv_silu(x, w):
            B, L, D = x.shape
            xp = jnp.pad(x, ((0, 0), (D_CONV - 1, 0), (0, 0)))
            y = sum((xp[:, k:k + L, :] * w[:, k] for k in range(D_CONV)))
            return jax.nn.silu(y)

        def _gla_scan(q, k, v, gk):
            B, h, L, dk = q.shape
            dv = v.shape[-1]
            qT = jnp.moveaxis(q, 2, 0)
            kT = jnp.moveaxis(k, 2, 0)
            vT = jnp.moveaxis(v, 2, 0)
            gT = jnp.moveaxis(gk, 2, 0)

            def step(S, inp):
                qt, kt, vt, gt = inp
                S = S * jnp.exp(gt)[..., None] + kt[..., None] * vt[..., None, :]
                ot = jnp.einsum('bhk,bhkv->bhv', qt, S)
                return (S, ot)
            S0 = jnp.zeros((B, h, dk, dv), q.dtype)
            S, o = lax.scan(step, S0, (qT, kT, vT, gT))
            return (jnp.moveaxis(o, 0, 2), S)

        def _reference_tuple_inner(x, conv_w, Wq, Wkg, Wv, Wg, bg, Wout, aug_balance):
            xb = jnp.swapaxes(x, 0, 1)
            xb = _causal_conv_silu(xb, conv_w)
            q = xb @ Wq
            k_gate = xb @ Wkg
            v = xb @ Wv
            g = xb @ Wg + bg
            gk = jax.nn.log_sigmoid(k_gate) / NORMALIZER
            k = 1.0 - jnp.exp(gk)
            B, L, _ = q.shape
            split = lambda t: t.reshape(B, L, H, -1).transpose(0, 2, 1, 3)
            qh, kh, gkh, vh = (split(q), split(k), split(gk), split(v))
            dk = qh.shape[-1]
            o, new_state = _gla_scan(qh * dk ** (-0.5), kh, vh, gkh)
            aug = aug_balance.reshape(H, dk)
            aug_w = jnp.einsum('bhlk,hk,bhlk->bhl', qh, aug, kh)
            o = o + jax.nn.sigmoid(aug_w[..., None] * vh)
            mu = o.mean(-1, keepdims=True)
            var = o.var(-1, keepdims=True)
            o = (o - mu) * lax.rsqrt(var + EPS)
            o = o.transpose(0, 2, 1, 3).reshape(B, L, -1)
            out = jax.nn.silu(g) * o @ Wout
            return (jnp.swapaxes(out, 0, 1), new_state)
        return _reference_tuple_inner(x, conv_w, Wq, Wkg, Wv, Wg, bg, Wout, aug_balance)[0]

    def _L3_xattn_ref(x, context, w_q, b_q, w_k, b_k, w_v, b_v, w_o, b_o):
        import jax, jax.numpy as jnp
        import numpy as np
        N_HEADS = 16
        DIMS = 128
        D_CTX = 96
        HEAD = DIMS // N_HEADS
        B, Lq, D = x.shape
        q = x @ w_q + b_q
        k = context @ w_k + b_k
        v = context @ w_v + b_v
        q = q.reshape(B, Lq, N_HEADS, HEAD)
        k = k.reshape(B, -1, N_HEADS, HEAD)
        v = v.reshape(B, -1, N_HEADS, HEAD)
        scale = 1.0 / np.sqrt(HEAD).astype(np.float32)
        scores = jnp.einsum('bqhd,bkhd->bhqk', q, k) * scale
        weights = jax.nn.softmax(scores, axis=-1)
        out = jnp.einsum('bhqk,bkhd->bqhd', weights, v).reshape(B, Lq, D)
        return out @ w_o + b_o

    def _L3_ffn_ref(src, Wq, Wk, Wv, Wo, Wsel_v, Wsel_o, ln1_g, ln1_b, ln2_g, ln2_b, W1, b1, W2, b2):
        import jax, jax.numpy as jnp
        import numpy as np
        D, H, P, E, K, F = (128, 16, 64, 8, 2, 512)
        B, S = (2, 256)
        NROT = 32
        BASE = 10000.0
        EPS = 1e-05

        def _ln(x, g, b):
            m = jnp.mean(x, -1, keepdims=True)
            v = jnp.mean(jnp.square(x - m), -1, keepdims=True)
            return (x - m) * jax.lax.rsqrt(v + EPS) * g + b

        def _rope(x):
            xr, xp = (x[..., :NROT], x[..., NROT:])
            half = NROT // 2
            inv = BASE ** (-jnp.arange(half, dtype=jnp.float32) / half)
            ang = jnp.arange(x.shape[2], dtype=jnp.float32)[:, None] * inv[None, :]
            cos, sin = (jnp.cos(ang), jnp.sin(ang))
            x1, x2 = (xr[..., :half], xr[..., half:])
            xr = jnp.concatenate([x1 * cos - x2 * sin, x1 * sin + x2 * cos], -1)
            return jnp.concatenate([xr, xp], -1)

        def _gate(x, Wsel):
            s = jax.nn.sigmoid(jnp.einsum('bsd,hed->bhse', x, Wsel))
            _, idx = jax.lax.top_k(s, K)
            mask = jax.nn.one_hot(idx, E, dtype=s.dtype).sum(-2)
            return s * mask

        def _moe_attn(x, Wq, Wk, Wv, Wo, Wsel_v, Wsel_o):
            q = _rope(jnp.einsum('bsd,hdp->bhsp', x, Wq))
            k = _rope(jnp.einsum('bsd,hdp->bhsp', x, Wk))
            gv = _gate(x, Wsel_v)
            v = jnp.einsum('bsd,bhse,hedp->bhsp', x, gv, Wv)
            att = jax.nn.softmax(jnp.einsum('bhsp,bhtp->bhst', q, k) / np.sqrt(P), axis=-1)
            o = jnp.einsum('bhst,bhtp->bhsp', att, v)
            go = _gate(x, Wsel_o)
            return jnp.einsum('bhsp,bhse,hepd->bsd', o, go, Wo)
        src2 = _moe_attn(src, Wq, Wk, Wv, Wo, Wsel_v, Wsel_o)
        src = src + src2
        src = _ln(src, ln1_g, ln1_b)
        src2 = jax.nn.relu(src @ W1 + b1) @ W2 + b2
        src = src + src2
        return _ln(src, ln2_g, ln2_b)
    x = x + _L0_attn_ref(_layernorm(x, axis=-1), L0_attn_c_attn_kernel, L0_attn_c_attn_bias, L0_attn_c_proj_kernel, L0_attn_c_proj_bias)
    x = x + _L0_xattn_ref(_layernorm(x, axis=-1), ctx_768, mask_BxS2_bf1, L0_xattn_g_norm, L0_xattn_null_kv, L0_xattn_Wq, L0_xattn_Wkv, L0_xattn_Wout, L0_xattn_g_out)
    x = x + _L0_ffn_ref(_layernorm(x, axis=-1), L0_ffn_Wr, L0_ffn_br, L0_ffn_W1, L0_ffn_b1, L0_ffn_W2, L0_ffn_b2)
    x = x + _L1_attn_ref(_layernorm(x, axis=-1), L1_attn_Wq, L1_attn_Wkv_down, L1_attn_Wk_up, L1_attn_Wv_up, L1_attn_Wout)
    x = x + _L1_xattn_ref(ctx_768, _layernorm(x, axis=-1), mask_BxS2_bk0, L1_xattn_ln_x_g, L1_xattn_ln_x_b, L1_xattn_ln_l_g, L1_xattn_ln_l_b, L1_xattn_qn_g, L1_xattn_kn_g, L1_xattn_Wq, L1_xattn_Wkv, L1_xattn_Wlkv, L1_xattn_Wo, L1_xattn_bo)
    x = x + _L1_ffn_ref(_layernorm(x, axis=-1), L1_ffn_w_gate, L1_ffn_w_up, L1_ffn_w_down)
    x = x + _L2_attn_ref(_layernorm(x, axis=-1), L2_attn_w_qkv, L2_attn_w_proj, L2_attn_b_proj)
    x = x + _L2_xattn_ref(_layernorm(x, axis=-1), ctx_768, L2_xattn_Wq, L2_xattn_bq, L2_xattn_Wk, L2_xattn_bk, L2_xattn_Wv, L2_xattn_bv, L2_xattn_Wo, L2_xattn_bo)
    x = x + _L2_ffn_ref(_layernorm(x, axis=-1), L2_ffn_norm_weight, L2_ffn_router_weight, L2_ffn_router_bias, L2_ffn_fc1_weight, L2_ffn_fc1_bias, L2_ffn_fc2_weight, L2_ffn_fc2_bias)
    x = x + _L3_attn_ref(_layernorm(x, axis=-1), L3_attn_conv_w, L3_attn_Wq, L3_attn_Wkg, L3_attn_Wv, L3_attn_Wg, L3_attn_bg, L3_attn_Wout, L3_attn_aug_balance)
    x = x + _L3_xattn_ref(_layernorm(x, axis=-1), ctx_768, L3_xattn_w_q, L3_xattn_b_q, L3_xattn_w_k, L3_xattn_b_k, L3_xattn_w_v, L3_xattn_b_v, L3_xattn_w_o, L3_xattn_b_o)
    x = x + _L3_ffn_ref(_layernorm(x, axis=-1), L3_ffn_Wq, L3_ffn_Wk, L3_ffn_Wv, L3_ffn_Wo, L3_ffn_Wsel_v, L3_ffn_Wsel_o, L3_ffn_ln1_g, L3_ffn_ln1_b, L3_ffn_ln2_g, L3_ffn_ln2_b, L3_ffn_W1, L3_ffn_b1, L3_ffn_W2, L3_ffn_b2)
    return x

_drawn_inputs = setup_inputs


def setup_inputs(seed=0):
    import zlib

    import numpy as np

    out = dict(_drawn_inputs(seed))
    spreads = {'L0_attn_c_attn_bias': (0.0, 0.29),
     'L0_attn_c_proj_bias': (0.0, 0.1),
     'L0_xattn_g_norm': (1.0, 0.2),
     'L0_xattn_g_out': (1.0, 0.2),
     'L0_ffn_br': (0.0, 0.389),
     'L0_ffn_b1': (0.0, 0.753),
     'L0_ffn_b2': (0.0, 0.1),
     'L1_xattn_ln_x_g': (1.0, 0.6),
     'L1_xattn_ln_x_b': (0.0, 0.8),
     'L1_xattn_ln_l_g': (1.0, 0.2),
     'L1_xattn_ln_l_b': (0.0, 0.1),
     'L1_xattn_qn_g': (1.0, 0.6),
     'L1_xattn_kn_g': (1.0, 0.6),
     'L1_xattn_bo': (0.0, 0.1),
     'L2_xattn_bq': (0.0, 0.8),
     'L2_xattn_bk': (0.0, 2.0),
     'L2_xattn_bv': (0.0, 0.8),
     'L2_xattn_bo': (0.0, 2.0),
     'L2_ffn_norm_weight': (1.0, 0.6),
     'L2_ffn_router_bias': (0.0, 2.0),
     'L2_ffn_fc1_bias': (0.0, 2.0),
     'L2_ffn_fc2_bias': (0.0, 2.0),
     'L3_attn_aug_balance': (0.0, 2.0),
     'L3_ffn_ln1_g': (1.0, 0.6),
     'L3_ffn_ln1_b': (0.0, 2.0),
     'L3_ffn_ln2_g': (1.0, 0.6),
     'L3_ffn_ln2_b': (0.0, 2.0),
     'L3_ffn_b1': (0.0, 2.0),
     'L3_ffn_b2': (0.0, 2.0)}
    factors = {'L0_attn_c_attn_kernel': 8.0,
     'L0_ffn_W1': 3.228,
     'L2_attn_w_qkv': 8.0,
     'L2_attn_w_proj': 8.0,
     'L2_attn_b_proj': 62.883,
     'L2_xattn_Wq': 8.0,
     'L2_xattn_Wk': 8.0,
     'L2_xattn_Wv': 8.0,
     'L2_xattn_Wo': 8.0,
     'L2_ffn_router_weight': 8.0,
     'L2_ffn_fc1_weight': 8.0,
     'L2_ffn_fc2_weight': 8.0,
     'L3_attn_conv_w': 8.0,
     'L3_attn_Wq': 8.0,
     'L3_attn_Wkg': 8.0,
     'L3_attn_Wv': 8.0,
     'L3_attn_Wg': 8.0,
     'L3_attn_bg': 64.0,
     'L3_attn_Wout': 8.0,
     'L3_xattn_w_q': 8.0,
     'L3_xattn_b_q': 45.102,
     'L3_xattn_w_k': 8.0,
     'L3_xattn_b_k': 200.0,
     'L3_xattn_w_v': 8.0,
     'L3_xattn_b_v': 200.0,
     'L3_xattn_w_o': 8.0,
     'L3_xattn_b_o': 200.0,
     'L3_ffn_Wq': 200.0,
     'L3_ffn_Wk': 200.0,
     'L3_ffn_Wv': 200.0,
     'L3_ffn_Wo': 200.0,
     'L3_ffn_Wsel_v': 200.0,
     'L3_ffn_Wsel_o': 200.0,
     'L3_ffn_W1': 200.0,
     'L3_ffn_W2': 200.0}
    for name, (base, spread) in spreads.items():
        noise = np.random.default_rng([zlib.crc32(name.encode()), seed]).standard_normal(out[name].shape)
        drawn = base * np.exp(spread * noise) if base else spread * noise
        out[name] = jnp.asarray(drawn.astype(out[name].dtype))
    for name, factor in factors.items():
        out[name] = (out[name] * factor).astype(out[name].dtype)
    return out
```

```python
from contextlib import ExitStack

import numpy as np

import concourse.bass as bass
import concourse.mybir as mybir
from concourse.alu_op_type import AluOpType as ALU

ACT = mybir.ActivationFunctionType
AX = mybir.AxisListType
F32 = mybir.dt.float32
BF16 = mybir.dt.bfloat16
I32 = mybir.dt.int32
U8 = mybir.dt.uint8
U32 = mybir.dt.uint32

P = 128
B, S = 2, 512
T = B * S
NT = T // P
NQ = S // P
SC, DC = 77, 96
H = 16
BIG = 3.0e38
LAG = 3
STEPS = 16


class Core:

    def __init__(self):
        self.items = {}
        self.used = {b: 0 for b in range(8)}
        self.norms = self.norms_pool = self.turns_pe = self.turns_dve = 0


class Attention:

    def __init__(self, steps, group, keys, causal=False, q=None, k=None, values=None, group_done=None,
                 before_scores=None, after=None, scalar_after=None, vector_after=None):
        self.steps, self.group, self.causal = steps, group, causal
        self.keys = keys
        self.q, self.k, self.values = q, k, values
        self.group_done = group_done
        self.before_scores, self.after = before_scores or {}, after or {}
        self.scalar_after, self.vector_after = scalar_after or {}, vector_after or {}


class Cross:

    def __init__(self, nk, clip=None):
        self.nk, self.clip, self.vector_after = nk, clip, {}


def wait(eng, sem, value):
    if isinstance(value, int) and value <= 0:
        return
    eng.wait_ge(sem, value)


class Chain:

    def __init__(self, eng, sem):
        self.eng, self.sem, self.n = eng, sem, 0

    def done(self, instruction):
        instruction.then_inc(self.sem, 1)
        self.n = self.n + 1
        self.eng.wait_ge(self.sem, self.n)



def item(m, name, bank, times=1):
    m.items[name] = (bank, m.used[bank])
    m.used[bank] += times


def fill(m, pe, name, k=0):
    bank, base = m.items[name]
    wait(pe, m.emptied[bank], base + k)
    return m.ps[bank]


def filled(m, name):
    return m.filled[m.items[name][0]]


def read(m, eng, name, k=0):
    bank, base = m.items[name]
    eng.wait_ge(m.filled[bank], base + k + 1)
    return m.ps[bank]


def emptied(m, name):
    return m.emptied[m.items[name][0]]


def copied(m, eng, name, k=0):
    bank, base = m.items[name]
    eng.wait_ge(m.emptied[bank], base + k + 1)



def norm_vector(nc, dve, m, src, dst, eps=1e-5):
    for t in range(NT):
        last = nc.vector.bn_stats(m.stats[:, t, :], src[:, t, :])
    m.dve.done(last)
    for t in range(NT):
        last = nc.vector.bn_aggr(m.moments[:, t, :], m.stats[:, t, :])
    m.dve.done(last)
    nc.vector.tensor_scalar(m.var[:, :], m.moments[:, :, 1], float(eps), None, ALU.add).then_inc(m.var_ready, 1)
    m.norms += 1
    dve.wait_ge(m.rstd_ready, m.norms)
    for t in range(NT):
        last = nc.vector.tensor_scalar(dst[:, t, :], src[:, t, :], m.moments[:, t, 0:1], m.rstd[:, t:t + 1],
                                       ALU.subtract, ALU.mult)
    return last


def norm_to_turn(nc, dve, m, src):
    norm_vector(nc, dve, m, src, m.xn).then_inc(m.xn_ready, 1)
    m.turns_dve += 1


def norm_gpsimd(nc, pool, m):
    m.norms_pool += 1
    pool.wait_ge(m.var_ready, m.norms_pool)
    nc.gpsimd.tensor_tensor(m.rstd[:, :], m.var[:, :], m.minus_half[:, :], ALU.pow).then_inc(m.rstd_ready, 1)


def turn_tensor(nc, pe, m, name):
    m.turns_pe += 1
    pe.wait_ge(m.xn_ready, m.turns_pe)
    for j in range(2):
        bank = fill(m, pe, f"{name}{j}")
        for t in range(4):
            last = nc.tensor.transpose(bank[:, t * P:(t + 1) * P], m.xn[:, 4 * j + t, :], m.ident[:, :])
        last.then_inc(filled(m, f"{name}{j}"), 1)


def turn_scalar(nc, act, m, name, scale=1.0, bias=0.0):
    for j in range(2):
        bank = read(m, act, f"{name}{j}")
        nc.scalar.activation(m.xn_t[:, j * S:(j + 1) * S], bank[:, :], ACT.Identity, bias=bias,
                             scale=scale).then_inc(emptied(m, f"{name}{j}"), 1)


def turned(m, pe, name):
    for j in range(2):
        copied(m, pe, f"{name}{j}")



def attend_tensor(nc, pe, m, a, n0, half0):
    for k in range(a.steps + LAG + 1):
        if k < a.steps:
            u, qt = divmod(k, NQ)
            if k in a.before_scores:
                a.before_scores[k](pe)
            wait(pe, m.exp_done, n0 + k - 3)
            bank = m.ps[k % 4]
            keys = a.keys(qt)
            last = nc.tensor.matmul(bank[:, 0:keys], a.q(u, qt), a.k(u, keys), start=True, stop=not a.causal)
            if a.causal:
                last = nc.tensor.matmul(bank[:, keys - P:keys], m.ident_bf[:, :], m.future_bf[:, :],
                                        start=False, stop=True)
            last.then_inc(m.scores_ready, 1)
        j = k - LAG
        if 0 <= j < a.steps:
            u, qt = divmod(j, NQ)
            pe.wait_ge(m.probs_ready, n0 + j + 1)
            wait(pe, m.turned_taken[j % 2], half0 + j // 2)
            for kt in range(a.keys(qt) // P):
                last = nc.tensor.transpose(m.ps[4 + j % 2][:, kt * P:(kt + 1) * P],
                                           m.p[:, j % 4, kt * P:(kt + 1) * P], m.ident[:, :])
            last.then_inc(m.turned_ready, 1)
        j = k - LAG - 1
        if j >= 0 and (j + 1) % (NQ * a.group) == 0:
            g = j // (NQ * a.group)
            for par in range(2):
                pe.wait_ge(m.turned_taken[par], half0 + (j + 1) // 2)
            a.values(pe, g)
        if k in a.after:
            a.after[k](pe)


def attend_vector(nc, dve, m, a, n0):
    for k in range(a.steps + 2):
        if k < a.steps:
            u, qt = divmod(k, NQ)
            dve.wait_ge(m.scores_ready, n0 + k + 1)
            nc.vector.tensor_reduce(m.negmax[:, k % 4:k % 4 + 1], m.ps[k % 4][:, 0:a.keys(qt)], AX.X, ALU.max,
                                    negate=True).then_inc(m.negmax_ready, 1)
        j = k - 1
        if 0 <= j < a.steps:
            dve.wait_ge(m.exp_done, n0 + j + 1)
            nc.vector.reciprocal(m.rsum[:, j % 4:j % 4 + 1], m.sum[:, j % 4:j % 4 + 1]).then_inc(m.rsum_ready, 1)
            dve.wait_ge(m.rsum_ready, n0 + j + 1)
            pr = m.p[:, j % 4, 0:a.keys(j % NQ)]
            nc.vector.tensor_scalar(pr, pr, m.rsum[:, j % 4:j % 4 + 1], None, ALU.mult).then_inc(m.probs_ready, 1)
        if k in a.vector_after:
            a.vector_after[k](dve)
        j = k - 2
        if 0 <= j - 1 < a.steps and (j - 1) % 2 == 1:
            take_turned(nc.vector.tensor_copy, dve, m, a, j - 1, n0)
    take_turned(nc.vector.tensor_copy, dve, m, a, a.steps - 1, n0)


def attend_scalar(nc, act, m, a, n0):
    def take(out, in_):
        return nc.scalar.activation(out, in_, ACT.Copy)

    for k in range(a.steps + 3):
        if k < a.steps:
            u, qt = divmod(k, NQ)
            act.wait_ge(m.negmax_ready, n0 + k + 1)
            wait(act, m.turned_ready, n0 + k - 3)
            wait(act, m.rsum_ready, n0 + k - 3)
            nc.scalar.activation(m.p[:, k % 4, 0:a.keys(qt)], m.ps[k % 4][:, 0:a.keys(qt)], ACT.Exp,
                                 bias=m.negmax[:, k % 4:k % 4 + 1],
                                 accum_out=m.sum[:, k % 4:k % 4 + 1]).then_inc(m.exp_done, 1)
        if k in a.scalar_after:
            a.scalar_after[k](act)
        j = k - 2
        if 0 <= j < a.steps and j % 2 == 0:
            take_turned(take, act, m, a, j, n0)


def take_turned(copy, eng, m, a, j, n0):
    u, qt = divmod(j, NQ)
    nb = a.keys(qt) // P
    eng.wait_ge(m.turned_ready, n0 + j + 1)
    a.group_done(eng, (u - 4) // a.group)
    copy(m.pt[:, u % 4, 0:nb, qt * P:(qt + 1) * P],
         m.ps[4 + j % 2][:, 0:nb * P].rearrange("p (b q) -> p b q", q=P)).then_inc(m.turned_taken[j % 2], 1)



def l0_attn_tensor(nc, pe, m):
    w = m.w["l0a"]
    pe.wait_ge(m.consts_in, 16 * m.n_consts)
    turn_tensor(nc, pe, m, "l0n")
    pe.wait_ge(m.loaded["l0a"], 16)
    turned(m, pe, "l0n")
    pe.wait_ge(m.consts_cast, 3)
    for name, wt in (("l0q", w["wq"]), ("l0k", w["wk"])):
        for j in range(2):
            bank = fill(m, pe, f"{name}{j}")
            nc.tensor.matmul(bank[:, :], wt, m.xn_t[:, j * S:(j + 1) * S], start=True,
                             stop=True).then_inc(filled(m, f"{name}{j}"), 1)
    tokens_tensor(nc, pe, m, "l0v", m.xn_t, w["wv"])
    for name in ("l0q", "l0k", "l0v"):
        for j in range(2):
            copied(m, pe, f"{name}{j}")

    def one_pass(i, first, last):
        def before_first(pe):
            pe.wait_ge(m.head_q, 2 * i + 1)

        def before_second(pe):
            pe.wait_ge(m.head_q, 2 * i + 2)

        def values(pe, g):
            pe.wait_ge(m.head_v, 2 * i + g // 2 + 1)
            b = g % 2
            if first and g < 2:
                fill(m, pe, f"l0o{b}")
            for kt in range(NQ):
                out = nc.tensor.matmul(m.ps[6 + b][:, kt * P:S], m.head_vals[:, g // 2, b * NQ + kt, :],
                                       m.pt[:, g, kt, kt * P:S], start=(first and g < 2 and kt == 0),
                                       stop=False, skip_group_check=True)
            out.then_inc(m.pv_done, 1)

        a = Attention(
            steps=STEPS, group=1, causal=True, keys=lambda qt: (qt + 1) * P,
            q=lambda u, qt: m.head_qs[:, u // 2, (u % 2) * S + qt * P:(u % 2) * S + (qt + 1) * P],
            k=lambda u, keys: m.k_t[:, (u % 2) * S:(u % 2) * S + keys],
            before_scores={0: before_first, 8: before_second}, after={}, values=values)
        attend_tensor(nc, pe, m, a, STEPS * i, (STEPS // 2) * i)

    one_pass(0, True, False)
    with pe.Fori(1, H // 2) as i:
        one_pass(i, False, False)
    complete(nc, pe, m, "l0o")
    project_out_tensor(nc, pe, m, "l0o", "l0y", w["wo"])


def complete(nc, pe, m, name):
    for j in range(2):
        nc.tensor.matmul(m.ps[6 + j][:, 0:P], m.zeros[:, :], m.ident[:, :], start=False, stop=True,
                         skip_group_check=True).then_inc(filled(m, f"{name}{j}"), 1)


def tokens_tensor(nc, pe, m, name, x_t, w):
    for j in range(2):
        bank = fill(m, pe, f"{name}{j}")
        for t in range(4):
            last = nc.tensor.matmul(bank[:, t * P:(t + 1) * P], x_t[:, (4 * j + t) * P:(4 * j + t + 1) * P], w,
                                    start=True, stop=True)
        last.then_inc(filled(m, f"{name}{j}"), 1)


def project_out_tensor(nc, pe, m, source, name, w):
    for j in range(2):
        copied(m, pe, f"{source}{j}")
    tokens_tensor(nc, pe, m, name, m.o_t, w)


def add_to_x(nc, dve, m, name):
    add_to(nc, dve, m, name, m.x)


def add_to(nc, dve, m, name, x):
    for j in range(2):
        bank = read(m, dve, f"{name}{j}")
        last = nc.vector.tensor_tensor(x[:, 4 * j:4 * j + 4, :], x[:, 4 * j:4 * j + 4, :],
                                       bank[:, :].rearrange("p (t d) -> p t d", d=P), ALU.add)
        last.then_inc(emptied(m, f"{name}{j}"), 1)
    for j in range(2):
        copied(m, dve, f"{name}{j}")


def l0_attn_scalar(nc, act, m):
    w = m.w["l0a"]
    turn_scalar(nc, act, m, "l0n")
    act.wait_ge(m.loaded["l0a"], 16)
    for name, dst, bias in (("l0q", m.q_t, w["bq"]), ("l0k", m.k_t, w["bk"])):
        for j in range(2):
            bank = read(m, act, f"{name}{j}")
            nc.scalar.activation(dst[:, j * S:(j + 1) * S], bank[:, :], ACT.Identity,
                                 bias=bias).then_inc(emptied(m, f"{name}{j}"), 1)

    def one_pass(i):
        a = Attention(steps=STEPS, group=1, keys=lambda qt: (qt + 1) * P, scalar_after={},
                            group_done=lambda eng, g: wait(eng, m.pv_done, 4 * i + g + 1))
        attend_scalar(nc, act, m, a, STEPS * i)

    one_pass(0)
    with act.Fori(1, H // 2) as i:
        one_pass(i)
    for b in range(2):
        bank = read(m, act, f"l0o{b}")
        nc.scalar.activation(m.o_t[:, b * S:(b + 1) * S], bank[:, :], ACT.Copy).then_inc(emptied(m, f"l0o{b}"), 1)


def l0_attn_vector(nc, dve, m):
    w = m.w["l0a"]
    dve.wait_ge(m.x_in, 16)
    norm_to_turn(nc, dve, m, m.x)
    dve.wait_ge(m.loaded["l0a"], 16)
    for j in range(2):
        bank = read(m, dve, f"l0v{j}")
        nc.vector.tensor_tensor(m.v[:, 4 * j:4 * j + 4, :], bank[:, :].rearrange("p (t d) -> p t d", d=P),
                                w["bv"].rearrange("p (o d) -> p o d", o=1).broadcast_to([P, 4, P]),
                                ALU.add).then_inc(emptied(m, f"l0v{j}"), 1)
    for j in range(2):
        copied(m, dve, f"l0q{j}")

    def head_queries(p, head):
        nc.vector.tensor_scalar(m.head_qs[:, p, :], m.q_t[:, :], m.rows8[:, bass.ds(head, 1)] if not isinstance(head, int)
                                else m.rows8[:, head:head + 1], None, ALU.mult).then_inc(m.head_q, 1)

    head_queries(0, 0)

    def one_pass(i):
        hooks = {0: lambda dve: head_queries(1, 2 * i + 1),
                 8: lambda dve: head_queries(0, 2 * i + 2)}
        a = Attention(steps=STEPS, group=1, keys=lambda qt: (qt + 1) * P, vector_after=hooks,
                            group_done=lambda eng, g: wait(eng, m.pv_done, 4 * i + g + 1))
        attend_vector(nc, dve, m, a, STEPS * i)

    one_pass(0)
    with dve.Fori(1, H // 2) as i:
        one_pass(i)
    m.dve.done(nc.vector.tensor_tensor(m.x[:, :, :], m.x[:, :, :],
                                       w["bo"].rearrange("p (o d) -> p o d", o=1).broadcast_to([P, NT, P]), ALU.add))
    add_to_x(nc, dve, m, "l0y")


def l0_attn_gpsimd(nc, pool, m):
    norm_gpsimd(nc, pool, m)
    for j in range(2):
        copied(m, pool, f"l0v{j}")

    def head_values(p, head):
        mask = m.cols8[:, head, :] if isinstance(head, int) else m.cols8[:, bass.ds(head, 1), :]
        mask = mask.rearrange("p d -> p () d") if isinstance(head, int) else mask
        nc.gpsimd.tensor_tensor(m.head_vals[:, p, :, :], m.v[:, :, :], mask.broadcast_to([P, NT, P]),
                                ALU.mult).then_inc(m.head_v, 1)

    head_values(0, 0)

    def one_pass(i):
        wait(pool, m.pv_done, 4 * i)
        head_values(1, 2 * i + 1)
        pool.wait_ge(m.pv_done, 4 * i + 2)
        head_values(0, 2 * i + 2)

    one_pass(0)
    with pool.Fori(1, H // 2) as i:
        one_pass(i)



XSTEPS = 2 * B * NQ


def cross_units():
    return [(b, half, qt) for b in range(B) for half in range(2) for qt in range(NQ)]


def cross_tensor(nc, pe, m, a):
    nk, units = a.nk, cross_units()
    for k in range(XSTEPS + 3):
        if k < XSTEPS:
            b, half, qt = units[k]
            wait(pe, m.negmax_ready, a.s0 + k - 1)
            for j in range(2):
                last = a.scores(m.ps[2 * (k % 2) + j], b, half, j, qt)
            last.then_inc(m.scores_ready, 1)
        j = k - 2
        if 0 <= j < XSTEPS:
            b, half, qt = units[j]
            pe.wait_ge(m.probs_ready, a.s0 + j + 1)
            wait(pe, m.cross_taken, a.x0 + j)
            for h in range(8):
                last = nc.tensor.transpose(m.ps[4 + h // 4][0:nk, (h % 4) * P:(h % 4 + 1) * P],
                                           m.xp[:, j % 2, h * nk:(h + 1) * nk], m.ident[:, :])
            last.then_inc(m.turned_ready, 1)
        j = k - 3
        if j >= 0 and (j + 1) % NQ == 0:
            b, half, qt = units[j]
            pe.wait_ge(m.cross_taken, a.x0 + j + 1)
            a.values(pe, b, half)


def cross_vector(nc, dve, m, a):
    nk = a.nk
    view = lambda ap: ap.rearrange("p (g h k) -> p g h k", g=2, k=nk)
    spread = lambda ap: ap.rearrange("p (g h o) -> p g h o", g=2, o=1).broadcast_to([P, 2, 4, nk])
    for k in range(XSTEPS + 1):
        if k < XSTEPS:
            dve.wait_ge(m.scores_ready, a.s0 + k + 1)
            wait(dve, m.turned_ready, a.s0 + k - 1)
            scores = m.psum[:, 2 * (k % 2):2 * (k % 2) + 2, 0:4 * nk].rearrange("p g (h k) -> p g h k", k=nk)
            to = view(m.xp[:, k % 2, 0:8 * nk])
            if a.clip:
                m.dve.done(nc.vector.tensor_scalar(to, scores, a.clip, -a.clip, ALU.min, ALU.max))
                scores = to
            m.dve.done(nc.vector.tensor_reduce(m.xmax[:, k % 2, :].rearrange("p (g h) -> p g h", g=2), scores, AX.X, ALU.max))
            nc.vector.tensor_tensor(to, scores, spread(m.xmax[:, k % 2, :]), ALU.subtract).then_inc(m.negmax_ready, 1)
        j = k - 1
        if j >= 0:
            dve.wait_ge(m.exp_done, a.s0 + j + 1)
            sums = m.xsum[:, 8 * j:8 * j + 8]
            m.dve.done(nc.vector.tensor_reduce(sums, m.xp[:, j % 2, 0:8 * nk].rearrange("p (h k) -> p h k", k=nk),
                                               AX.X, ALU.add))
            wait(dve, m.probs_ready, a.s0 + j - 1)
            nc.vector.reciprocal(m.xrsum[:, j % 2, :], sums).then_inc(m.rsum_ready, 1)
        if k in a.vector_after:
            a.vector_after[k](dve)


def cross_scalar(nc, act, m, a):
    nk, units = a.nk, cross_units()
    for k in range(XSTEPS + 2):
        if k < XSTEPS:
            act.wait_ge(m.negmax_ready, a.s0 + k + 1)
            pr = m.xp[:, k % 2, 0:8 * nk]
            nc.scalar.activation(pr, pr, ACT.Exp).then_inc(m.exp_done, 1)
        j = k - 2
        if j >= 0:
            b, half, qt = units[j]
            act.wait_ge(m.turned_ready, a.s0 + j + 1)
            if b > 0 and qt == 0:
                a.unit_done(act, b - 1, half)
            nc.scalar.activation(m.xpt[0:nk, half, :, qt * P:(qt + 1) * P],
                                 m.psum[0:nk, 4:6, :].rearrange("p g (h q) -> p (g h) q", q=P),
                                 ACT.Copy).then_inc(m.cross_taken, 1)


def cross_gpsimd(nc, pool, m, a):
    nk = a.nk
    for k in range(XSTEPS):
        pool.wait_ge(m.rsum_ready, a.s0 + k + 1)
        pr = m.xp[:, k % 2, 0:8 * nk].rearrange("p (h k) -> p h k", k=nk)
        nc.gpsimd.tensor_tensor(pr, pr, m.xrsum[:, k % 2, :].rearrange("p (h o) -> p h o", o=1).broadcast_to([P, 8, nk]),
                                ALU.mult).then_inc(m.probs_ready, 1)


def project_turned_tensor(nc, pe, m, name, pairs, turn):
    for j in range(2):
        bank = fill(m, pe, f"{name}{j}")
        for n, (w, x_t) in enumerate(pairs):
            last = nc.tensor.matmul(bank[:, :], w, x_t(j), start=n == 0, stop=n == len(pairs) - 1)
        last.then_inc(filled(m, f"{name}{j}"), 1)
    turn_back_tensor(nc, pe, m, name, turn)


def turn_back_tensor(nc, pe, m, name, turn):
    for j in range(2):
        copied(m, pe, f"{name}{j}")
        bank = fill(m, pe, f"{turn}{j}")
        for t in range(4):
            last = nc.tensor.transpose(bank[:, t * P:(t + 1) * P], m.y_t[:, (4 * j + t) * P:(4 * j + t + 1) * P],
                                       m.ident[:, :])
        last.then_inc(filled(m, f"{turn}{j}"), 1)


def copy_out_scalar(nc, act, m, name, dst, scale=1.0, bias=0.0):
    for j in range(2):
        bank = read(m, act, f"{name}{j}")
        nc.scalar.activation(dst[:, j * S:(j + 1) * S], bank[:, :], ACT.Identity, scale=scale,
                             bias=bias).then_inc(emptied(m, f"{name}{j}"), 1)



L0X = Cross(SC + 1)
NPAIR = H // 2


def l0_cross_tensor(nc, pe, m):
    w, a = m.w["l0x"], L0X
    nk = a.nk
    a.s0, a.x0 = m.steps0["l0x"], m.cross0["l0x"]
    pe.wait_ge(m.loaded["l0x"], 16)
    pe.wait_ge(m.context_in, 16 * 5)
    for g in range(NPAIR):
        bank = fill(m, pe, f"l0xk{g}")
        nc.tensor.matmul(bank[:, 0:B * SC], w["wk"][0:DC, g * P:(g + 1) * P], m.context_t[0:DC, :], start=True,
                         stop=True).then_inc(filled(m, f"l0xk{g}"), 1)
    for n in range(2 * B):
        b, j = divmod(n, 2)
        bank = fill(m, pe, f"l0xv{n}")
        nc.tensor.matmul(bank[0:SC, :], m.context_t[0:DC, b * SC:(b + 1) * SC], w["wv"][0:DC, j * S:(j + 1) * S],
                         start=True, stop=True).then_inc(filled(m, f"l0xv{n}"), 1)
    turn_tensor(nc, pe, m, "l0xn")
    turned(m, pe, "l0xn")
    for n in range(2 * NPAIR):
        g, j = divmod(n, 2)
        bank = fill(m, pe, f"l0xq{n}")
        nc.tensor.matmul(bank[:, :], w["wq"][:, g * P:(g + 1) * P], m.xn_t[:, j * S:(j + 1) * S], start=True,
                         stop=True).then_inc(filled(m, f"l0xq{n}"), 1)
    for n in range(2 * NPAIR - 2, 2 * NPAIR):
        copied(m, pe, f"l0xq{n}")
    pe.wait_ge(m.cross_ready, 1)

    def scores(bank, b, half, j, qt):
        for i in range(2):
            g = 4 * half + 2 * j + i
            nc.tensor.matmul(bank[:, 2 * i * nk:2 * (i + 1) * nk], m.wide[:, g, b * S + qt * P:b * S + (qt + 1) * P],
                             m.keys_own[:, b, 2 * g * nk:2 * (g + 1) * nk], start=i == 0, stop=False,
                             skip_group_check=True)
        return nc.tensor.matmul(bank[:, 0:4 * nk], m.ones_bf[0:1, :], m.mask_row[0:1, b, :], start=False, stop=True,
                                skip_group_check=True)

    def values(pe, b, half):
        for i in range(4):
            g = 4 * half + i
            name = f"l0xo{(b * 2 + half) * 4 + i}"
            bank = fill(m, pe, name)
            for e in range(2):
                last = nc.tensor.matmul(bank[64 * e:64 * e + 64, :],
                                        m.context_v[0:nk, b, (2 * g + e) * 64:(2 * g + e + 1) * 64],
                                        m.xpt[0:nk, half, 2 * i + e, :], start=True, stop=True)
            last.then_inc(filled(m, name), 1)

    a.scores, a.values = scores, values
    cross_tensor(nc, pe, m, a)
    for n in range(4 * NPAIR // 2 - 2, 4 * NPAIR // 2):
        copied(m, pe, f"l0xo{n}")
    project_turned_tensor(nc, pe, m, "l0xy",
                          [(w["wo"][:, g * P:(g + 1) * P], lambda j, g=g: m.wide[:, g, j * S:(j + 1) * S])
                           for g in range(NPAIR)], "l0xz")


def l0_cross_scalar(nc, act, m):
    w, a = m.w["l0x"], L0X
    a.s0, a.x0 = m.steps0["l0x"], m.cross0["l0x"]
    nk = a.nk
    act.wait_ge(m.keys_zero, 1)
    for g in range(NPAIR):
        bank = read(m, act, f"l0xk{g}")
        for e in range(2):
            at = (2 * g + e) * nk
            last = nc.scalar.activation(m.keys_own[64 * e:64 * e + 64, :, at:at + SC],
                                        bank[64 * e:64 * e + 64, 0:B * SC].rearrange("p (b k) -> p b k", k=SC), ACT.Copy)
        last.then_inc(emptied(m, f"l0xk{g}"), 1)
    turn_scalar(nc, act, m, "l0xn", scale=w["g_norm"])
    for g in range(NPAIR):
        bank = read(m, act, f"l0xq{2 * g}")
        nc.scalar.activation(m.wide[:, g, 0:S], bank[:, :], ACT.Copy,
                             scale=64 ** -0.5).then_inc(emptied(m, f"l0xq{2 * g}"), 1)
    a.unit_done = lambda eng, b, half: read(m, eng, f"l0xo{(b * 2 + half) * 4 + 3}")
    cross_scalar(nc, act, m, a)
    copy_out_scalar(nc, act, m, "l0xy", m.y_t)


def l0_cross_vector(nc, dve, m):
    w, a = m.w["l0x"], L0X
    a.s0, a.x0 = m.steps0["l0x"], m.cross0["l0x"]
    nk = a.nk
    dve.wait_ge(m.context_in, 16 * 5)
    dve.wait_ge(m.loaded["l0x"], 16)
    dve.wait_ge(m.keys_zero, 1)
    for e in range(2):
        null = m.keys_own[64 * e:64 * e + 64, :, :].rearrange("p b (g k) -> p b g k", k=2 * nk)[:, :, :, e * nk + SC]
        nc.vector.tensor_copy(null, w["null_k"][64 * e:64 * e + 64, :].broadcast_to([64, B * NPAIR]).rearrange(
            "p (b g) -> p b g", b=B))
    m.dve.done(nc.vector.tensor_scalar(m.mask_low[0:1, :], m.mask_u8[0:1, 0:2 * B * SC], -1.0, BIG, ALU.add, ALU.mult))
    nc.vector.tensor_copy(m.mask_row[0:1, :, :].rearrange("p b (h k) -> p b h k", k=nk)[:, :, :, 0:SC],
                          m.mask_low[0:1, 0:B * SC].rearrange("p (b o k) -> p b o k", o=1, k=SC).broadcast_to(
                              [1, B, 4, SC])).then_inc(m.cross_ready, 1)
    for n in range(2 * B):
        b, j = divmod(n, 2)
        bank = read(m, dve, f"l0xv{n}")
        nc.vector.tensor_copy(m.context_v[0:SC, b, j * S:(j + 1) * S],
                              bank[0:SC, :]).then_inc(emptied(m, f"l0xv{n}"), 1)
    m.dve.done(norm_vector(nc, dve, m, m.x, m.xn))
    norm_to_turn(nc, dve, m, m.xn)
    for g in range(NPAIR):
        bank = read(m, dve, f"l0xq{2 * g + 1}")
        nc.vector.tensor_scalar(m.wide[:, g, S:T], bank[:, :], float(64 ** -0.5), None,
                                ALU.mult).then_inc(emptied(m, f"l0xq{2 * g + 1}"), 1)

    def take_values(b, half):
        for i in range(4):
            name = f"l0xo{(b * 2 + half) * 4 + i}"
            bank = read(m, dve, name)
            nc.vector.tensor_copy(m.wide[:, 4 * half + i, b * S:(b + 1) * S], bank[:, :]).then_inc(emptied(m, name), 1)

    a.vector_after = {6: lambda dve: take_values(0, 0), 10: lambda dve: take_values(0, 1),
                      14: lambda dve: take_values(1, 0)}
    cross_vector(nc, dve, m, a)
    take_values(1, 1)
    for j in range(2):
        bank = read(m, dve, f"l0xz{j}")
        last = nc.vector.tensor_copy(m.xn[:, 4 * j:4 * j + 4, :], bank[:, :].rearrange("p (t d) -> p t d", d=P))
        last.then_inc(emptied(m, f"l0xz{j}"), 1)
    for j in range(2):
        copied(m, dve, f"l0xz{j}")
    m.dve.done(norm_vector(nc, dve, m, m.xn, m.xn))
    m.dve.done(nc.vector.tensor_tensor(m.xn[:, :, :], m.xn[:, :, :], over_tiles(w["g_out"]), ALU.mult))
    m.dve.done(nc.vector.tensor_tensor(m.x[:, :, :], m.x[:, :, :], m.xn[:, :, :], ALU.add))


def over_tiles(row, tiles=NT):
    return row.rearrange("p (o d) -> p o d", o=1).broadcast_to([P, tiles, row.shape[1]])


def l0_cross_gpsimd(nc, pool, m):
    a = L0X
    a.s0 = m.steps0["l0x"]
    norm_gpsimd(nc, pool, m)
    norm_gpsimd(nc, pool, m)
    cross_gpsimd(nc, pool, m, a)
    norm_gpsimd(nc, pool, m)



def stream_sync(sp, m, dram, passes, free):
    def one_pass(i):
        for s in range(2):
            if not (isinstance(i, int) and i == 0):
                free(i, s)
            src = dram[2 * i + s] if isinstance(i, int) else dram[bass.ds(2 * i + s, 1)].rearrange("o p n -> (o p) n")
            sp.dma_start(m.slots[:, s, 0:dram.shape[2]], src).then_inc(m.slot_in[s], 16)

    one_pass(0)
    with sp.Fori(1, passes) as i:
        one_pass(i)



E0, F0 = 8, 512
TOP_P = 0.8


def l0_ffn_sync(nc, sp, m, dram):
    for j in range(2):
        copied(m, sp, f"l0fg{j}")
    sp.dma_start(dram["scratch_gates"], m.gate_t[0:E0, :]).then_inc(m.gates_out, 16)
    sp.wait_ge(m.gates_out, 16)
    for e in range(E0):
        sp.dma_start(m.wide[:, e, :], dram["scratch_gates"][e:e + 1, :].broadcast_to([P, T])).then_inc(m.gates_in, 16)
    stream_sync(sp, m, dram["s_l0f"], E0 // 2,
                lambda i, s: sp.wait_ge(m.hidden_used, m.h0["l0f"] + 16 * (i - 1) + 8 * (s + 1)))


def l0_ffn_tensor(nc, pe, m):
    w = m.w["l0f"]
    pe.wait_ge(m.loaded["l0f"], 16)
    turn_tensor(nc, pe, m, "l0fn")
    turned(m, pe, "l0fn")
    bank = fill(m, pe, "l0fr")
    for t in range(NT):
        last = nc.tensor.matmul(bank[:, t * E0:(t + 1) * E0], m.xn_t[:, t * P:(t + 1) * P], w["wr"], start=True, stop=True)
    last.then_inc(filled(m, "l0fr"), 1)
    pe.wait_ge(m.gates_ready, 1)
    for j in range(2):
        bank = fill(m, pe, f"l0fg{j}")
        for t in range(4):
            last = nc.tensor.transpose(bank[0:E0, t * P:(t + 1) * P], m.gates[:, 4 * j + t, :], m.ident[:, :])
        last.then_inc(filled(m, f"l0fg{j}"), 1)
    for j in range(2):
        copied(m, pe, f"l0fg{j}")
    for j in range(2):
        bank = fill(m, pe, f"l0fy{j}")
        nc.tensor.matmul(bank[:, :], w["b2"][0:E0, :], m.gate_t[0:E0, j * S:(j + 1) * S], start=True, stop=False,
                         skip_group_check=True)
    g0, h0 = m.slot0["l0f"], m.h0["l0f"]

    def one_pass(i):
        base = h0 + 16 * i
        for k in range(16 + 2):
            if k < 16:
                s, fc, j = k // 8, k // 2 % 4, k % 2
                if k % 8 == 0:
                    pe.wait_ge(m.slot_in[s], 16 * (g0 + i + 1))
                if k >= 4:
                    pe.wait_ge(m.hidden_read, base + k - 3)
                nc.tensor.matmul(m.ps[k % 4][:, :], m.slots[:, s, fc * P:(fc + 1) * P], m.xn_t[:, j * S:(j + 1) * S],
                                 start=True, stop=True).then_inc(m.hidden_ready, 1)
            q = k - 2
            if q >= 0:
                s, fc, j = q // 8, q // 2 % 4, q % 2
                pe.wait_ge(m.hidden_gated, base + q + 1)
                last = nc.tensor.matmul(m.ps[6 + j][:, :], m.slots[:, s, F0 + fc * P:F0 + (fc + 1) * P], m.hidden[:, q % 4, :],
                                        start=False, stop=False, skip_group_check=True)
                last.then_inc(m.hidden_used, 1)

    with pe.Fori(0, E0 // 2) as i:
        one_pass(i)
    complete(nc, pe, m, "l0fy")
    turn_back_tensor(nc, pe, m, "l0fy", "l0fz")


def l0_ffn_scalar(nc, act, m):
    w = m.w["l0f"]
    act.wait_ge(m.loaded["l0f"], 16)
    turn_scalar(nc, act, m, "l0fn")
    act.wait_ge(m.router_less_max, 1)
    nc.scalar.activation(m.gates[:, :, :], m.gates[:, :, :], ACT.Exp).then_inc(m.router_exp, 1)
    for j in range(2):
        bank = read(m, act, f"l0fg{j}")
        nc.scalar.activation(m.gate_t[0:E0, j * S:(j + 1) * S], bank[0:E0, :], ACT.Copy).then_inc(emptied(m, f"l0fg{j}"), 1)
    h0 = m.h0["l0f"]

    def one_pass(i):
        for k in range(16):
            s, fc = k // 8, k // 2 % 4
            act.wait_ge(m.hidden_ready, h0 + 16 * i + k + 1)
            wait(act, m.hidden_used, h0 + 16 * i + k - 3)
            nc.scalar.activation(m.hidden[:, k % 4, :], m.ps[k % 4][:, :], ACT.Relu,
                                 bias=m.slots[:, s, 2 * F0 + fc:2 * F0 + fc + 1]).then_inc(m.hidden_read, 1)

    one_pass(0)
    with act.Fori(1, E0 // 2) as i:
        one_pass(i)
    copy_out_scalar(nc, act, m, "l0fy", m.y_t)


def l0_ffn_vector(nc, dve, m):
    w = m.w["l0f"]
    d = m.dve
    dve.wait_ge(m.loaded["l0f"], 16)
    norm_to_turn(nc, dve, m, m.x)
    gates = m.gates[:, :, :]
    bank = read(m, dve, "l0fr")
    nc.vector.tensor_tensor(gates, bank[:, 0:NT * E0].rearrange("p (t e) -> p t e", e=E0),
                            over_tiles(w["br"]), ALU.add).then_inc(emptied(m, "l0fr"), 1)
    copied(m, dve, "l0fr")
    last8 = lambda ap: ap.rearrange("p (t o) -> p t o", o=1).broadcast_to([P, NT, E0])
    d.done(nc.vector.tensor_reduce(m.per_token[:, 0, :], gates, AX.X, ALU.max))
    nc.vector.tensor_tensor(gates, gates, last8(m.per_token[:, 0, :]), ALU.subtract).then_inc(m.router_less_max, 1)
    dve.wait_ge(m.router_exp, 1)
    d.done(nc.vector.tensor_reduce(m.per_token[:, 1, :], gates, AX.X, ALU.add))
    d.done(nc.vector.reciprocal(m.per_token[:, 2, :], m.per_token[:, 1, :]))
    d.done(nc.vector.tensor_tensor(gates, gates, last8(m.per_token[:, 2, :]), ALU.mult))
    shape = [P, NT, E0, E0]
    mine = gates.rearrange("p t (e o) -> p t e o", o=1).broadcast_to(shape)
    other = gates.rearrange("p t (o e) -> p t o e", o=1).broadcast_to(shape)
    ahead, tie = m.pairs[:, 0, :, :, :], m.pairs[:, 1, :, :, :]
    not_after = w["not_after"].rearrange("p (o e j) -> p o e j", o=1, j=E0).broadcast_to(shape)
    d.done(nc.vector.tensor_tensor(tie, mine, other, ALU.is_equal))
    d.done(nc.vector.tensor_tensor(tie, tie, not_after, ALU.mult))
    d.done(nc.vector.tensor_tensor(ahead, other, mine, ALU.is_gt))
    d.done(nc.vector.tensor_tensor(ahead, ahead, tie, ALU.add))
    d.done(nc.vector.tensor_reduce(m.keep[:, 0, :, :], ahead, AX.X, ALU.add))
    d.done(nc.vector.tensor_tensor(ahead, ahead, other, ALU.mult))
    d.done(nc.vector.tensor_reduce(m.keep[:, 1, :, :], ahead, AX.X, ALU.add))
    d.done(nc.vector.tensor_scalar(m.keep[:, 0, :, :], m.keep[:, 0, :, :], 1.5, None, ALU.is_lt))
    d.done(nc.vector.tensor_scalar(m.keep[:, 1, :, :], m.keep[:, 1, :, :], TOP_P, None, ALU.is_lt))
    d.done(nc.vector.tensor_tensor(m.keep[:, 0, :, :], m.keep[:, 0, :, :], m.keep[:, 1, :, :], ALU.max))
    nc.vector.tensor_tensor(gates, gates, m.keep[:, 0, :, :], ALU.mult).then_inc(m.gates_ready, 1)
    h0 = m.h0["l0f"]
    dve.wait_ge(m.gates_in, 16 * E0)

    with dve.Fori(0, E0 // 2) as i:
        for k in range(16):
            s, j = k // 8, k % 2
            dve.wait_ge(m.hidden_read, h0 + 16 * i + k + 1)
            gate = m.wide[:, bass.ds(2 * i + s, 1), j * S:(j + 1) * S].rearrange("p o n -> p (o n)")
            nc.vector.tensor_tensor(m.hidden[:, k % 4, :], m.hidden[:, k % 4, :], gate, ALU.mult).then_inc(m.hidden_gated, 1)
    add_to_x(nc, dve, m, "l0fz")


def l0_ffn_gpsimd(nc, pool, m):
    norm_gpsimd(nc, pool, m)



PAIR_STEPS = 2 * STEPS
PROJECT_AT = 12


class BankUses:
    def __init__(self, uses, first, output):
        self.uses, self.first, self.output = uses, first, output


def bank_uses(n):
    return BankUses(uses=2 * n + 2, first={(6, 0): 0, (7, 0): 0, (6, 1): n + 1, (7, 1): n},
                    output={(0, 0): (6, n), (0, 1): (7, 2 * n), (1, 0): (6, 2 * n + 1), (1, 1): (7, 2 * n + 1)})


PAIR1, PAIR3 = bank_uses(3), bank_uses(4)
USES = {"l1aj": PAIR1, "l3fj": PAIR3}


def pair_project_tensor(nc, pe, m, name, i, s, weights):
    w_q, w_k, k_src, v_src, w_v = weights(s)
    for n in range(6):
        what, j = divmod(n, 2)
        bank = fill(m, pe, f"{name}{j}", USES[name].uses * i + USES[name].first[6 + j, s] + what)
        if what == 0:
            last = nc.tensor.matmul(bank[:, :], w_q, m.xn_t[:, j * S:(j + 1) * S], start=True, stop=True)
        elif what == 1:
            last = nc.tensor.matmul(bank[:, :], w_k, k_src[:, j * S:(j + 1) * S], start=True, stop=True)
        else:
            for t in range(4):
                last = nc.tensor.matmul(bank[:, t * P:(t + 1) * P], v_src[:, (4 * j + t) * P:(4 * j + t + 1) * P], w_v,
                                        start=True, stop=True)
        last.then_inc(filled(m, f"{name}{j}"), 1)


def pair_project_scalar(nc, act, m, name, i, s, scale):
    for n in range(6):
        what, j = divmod(n, 2)
        bank = read(m, act, f"{name}{j}", USES[name].uses * i + USES[name].first[6 + j, s] + what)
        if what == 0:
            last = nc.scalar.activation(m.pair_q[s][:, j * S:(j + 1) * S], bank[:, :], ACT.Copy, scale=scale)
        elif what == 1:
            for e in range(2):
                last = nc.scalar.activation(m.pair_k[64 * e:64 * e + 64, s, e, j * S:(j + 1) * S],
                                            bank[64 * e:64 * e + 64, :], ACT.Copy)
        else:
            last = nc.scalar.activation(m.pair_v[s][:, 4 * j:4 * j + 4, :],
                                        bank[:, :].rearrange("p (t d) -> p t d", d=P), ACT.Copy)
        last.then_inc(emptied(m, f"{name}{j}"), 1)


def pair_attend_tensor(nc, pe, m, name, i, n0, half0, causal, project, projected=None):
    def copied_projections(pe, s):
        for j in range(2):
            copied(m, pe, f"{name}{j}", USES[name].uses * i + USES[name].first[6 + j, s] + 2)

    projected = projected or copied_projections

    def values(pe, g):
        s, b = divmod(g, 2)
        bank_no, use = USES[name].output[s, b]
        bank = fill(m, pe, f"{name}{bank_no - 6}", USES[name].uses * i + use)
        for kt in range(NQ):
            q0 = kt * P if causal else 0
            for e in range(2):
                last = nc.tensor.matmul(bank[64 * e:64 * e + 64, q0:S],
                                        m.pair_v[s][:, b * NQ + kt, 64 * e:64 * e + 64],
                                        m.pt[:, (2 * g + e) % 4, kt, q0:S], start=kt == 0, stop=kt == NQ - 1,
                                        skip_group_check=True)
        last.then_inc(filled(m, f"{name}{bank_no - 6}"), 1)

    project(pe, i, 0)
    projected(pe, 0)
    a = Attention(
        steps=PAIR_STEPS, group=2, causal=causal, keys=(lambda qt: (qt + 1) * P) if causal else (lambda qt: S),
        q=lambda u, qt: m.pair_q[u // 4][:, (u // 2 % 2) * S + qt * P:(u // 2 % 2) * S + (qt + 1) * P],
        k=lambda u, keys: m.pair_k[:, u // 4, u % 2, (u // 2 % 2) * S:(u // 2 % 2) * S + keys],
        before_scores={STEPS: lambda pe: projected(pe, 1)}, after={PROJECT_AT: lambda pe: project(pe, i, 1)},
        values=values)
    attend_tensor(nc, pe, m, a, n0 + PAIR_STEPS * i, half0 + STEPS * i)


def pair_attend_scalar(nc, act, m, name, i, n0, causal, project):
    project(act, 0)
    a = Attention(steps=PAIR_STEPS, group=2, keys=(lambda qt: (qt + 1) * P) if causal else (lambda qt: S),
                        group_done=lambda eng, g: pair_group_done(m, eng, name, i, g),
                        scalar_after={PROJECT_AT: lambda act: project(act, 1)})
    attend_scalar(nc, act, m, a, n0 + PAIR_STEPS * i)


def pair_group_done(m, eng, name, i, g):
    k = USES[name].uses * i
    if g < 0:
        if isinstance(i, int) and i == 0:
            return
        g, k = g + 4, k - USES[name].uses
    bank_no, use = USES[name].output[g // 2, g % 2]
    read(m, eng, f"{name}{bank_no - 6}", k + use)


def pair_attend_vector(nc, dve, m, name, i, n0, causal, project=lambda dve, s: None):
    def take_output(g):
        s, b = divmod(g, 2)
        bank_no, use = USES[name].output[s, b]
        bank = read(m, dve, f"{name}{bank_no - 6}", USES[name].uses * i + use)
        to = m.wide[:, bass.ds(2 * i + s, 1), b * S:(b + 1) * S].rearrange("p o n -> p (o n)")
        nc.vector.tensor_scalar(to, bank[:, :], 1.0, None, ALU.mult).then_inc(emptied(m, f"{name}{bank_no - 6}"), 1)

    def project_second(dve):
        take_output(0)
        project(dve, 1)

    project(dve, 0)
    a = Attention(steps=PAIR_STEPS, group=2, keys=(lambda qt: (qt + 1) * P) if causal else (lambda qt: S),
                        group_done=lambda eng, g: pair_group_done(m, eng, name, i, g),
                        vector_after={PROJECT_AT: project_second, 20: lambda dve: take_output(1),
                                      28: lambda dve: take_output(2)})
    attend_vector(nc, dve, m, a, n0 + PAIR_STEPS * i)
    take_output(3)



LATENT = 32
L1A_PARTS = ("wq", "wk", "wv")


def l1_attn_sync(nc, sp, m, dram):
    def free(i, s):
        copied(m, sp, "l1aj1", PAIR1.uses * (i - 1) + PAIR1.first[7, s] + 2)

    sp.wait_ge(m.hidden_used, 8 * E0)
    stream_sync(sp, m, dram["s_l1a"], NPAIR // 2, free)


def l1_attn_tensor(nc, pe, m):
    w = m.w["l1a"]
    n0, half0, g0 = m.steps0["l1a"], m.half0["l1a"], m.slot0["l1a"]
    pe.wait_ge(m.loaded["l1a"], 16)
    turn_tensor(nc, pe, m, "l1an")
    turned(m, pe, "l1an")
    for j in range(2):
        bank = fill(m, pe, f"l1al{j}")
        nc.tensor.matmul(bank[0:LATENT, :], w["down"], m.xn_t[:, j * S:(j + 1) * S], start=True,
                         stop=True).then_inc(filled(m, f"l1al{j}"), 1)
    for j in range(2):
        copied(m, pe, f"l1al{j}")

    def project(pe, i, s):
        pe.wait_ge(m.slot_in[s], 16 * (g0 + i + 1))
        part = lambda n: m.slots[:, s, n * P:(n + 1) * P]
        pair_project_tensor(nc, pe, m, "l1aj", i, s, lambda s: (part(0), part(1), m.latent_t, m.latent_t, part(2)))

    with pe.Fori(0, NPAIR // 2) as i:
        pair_attend_tensor(nc, pe, m, "l1aj", i, n0, half0, True, project)
    for j in range(2):
        copied(m, pe, f"l1aj{j}", PAIR1.uses * NPAIR // 2 - 1)
    project_turned_tensor(nc, pe, m, "l1ay",
                          [(w["wo"][:, g * P:(g + 1) * P], lambda j, g=g: m.wide[:, g, j * S:(j + 1) * S])
                           for g in range(NPAIR)], "l1az")


def l1_attn_scalar(nc, act, m):
    n0 = m.steps0["l1a"]
    turn_scalar(nc, act, m, "l1an")
    act.wait_ge(m.pair_zero, 1)
    for j in range(2):
        bank = read(m, act, f"l1al{j}")
        nc.scalar.activation(m.latent_t[0:LATENT, j * S:(j + 1) * S], bank[0:LATENT, :],
                             ACT.Copy).then_inc(emptied(m, f"l1al{j}"), 1)
    with act.Fori(0, NPAIR // 2) as i:
        pair_attend_scalar(nc, act, m, "l1aj", i, n0, True,
                           lambda act, s: pair_project_scalar(nc, act, m, "l1aj", i, s, 64 ** -0.5))
    copy_out_scalar(nc, act, m, "l1ay", m.y_t)


def l1_attn_vector(nc, dve, m):
    n0 = m.steps0["l1a"]
    norm_to_turn(nc, dve, m, m.x)
    with dve.Fori(0, NPAIR // 2) as i:
        pair_attend_vector(nc, dve, m, "l1aj", i, n0, True)
    add_to_x(nc, dve, m, "l1az")


def l1_attn_gpsimd(nc, pool, m):
    pool.wait_ge(m.stage_done, 3)
    nc.gpsimd.memset(m.latent_t[:, :], 0.0)
    nc.gpsimd.memset(m.pair_k[:, :, :, :], 0.0).then_inc(m.pair_zero, 1)
    norm_gpsimd(nc, pool, m)



RMS_EPS = 1e-8
ALLK = S + SC


def l1_cross_units():
    return [(b, h, qt) for b in range(B) for h in range(2) for qt in range(NQ)]


def l1_cross_tensor(nc, pe, m):
    w = m.w["l1x"]
    pe.wait_ge(m.loaded["l1x"], 16)
    pe.wait_ge(m.context_normed, 1)
    bank = fill(m, pe, "l1xc0")
    for b in range(B):
        last = nc.tensor.transpose(bank[0:DC, b * SC:(b + 1) * SC], m.context[:, b, :], m.ident[0:SC, 0:SC])
    last.then_inc(filled(m, "l1xc0"), 1)
    copied(m, pe, "l1xc0")
    for b in range(B):
        bank = fill(m, pe, f"l1xd{b}")
        nc.tensor.matmul(bank[0:SC, 0:2 * P], m.context_norm_t[0:DC, b * SC:(b + 1) * SC], w["wkv"][0:DC, :], start=True,
                         stop=True).then_inc(filled(m, f"l1xd{b}"), 1)
    turn_tensor(nc, pe, m, "l1xn")
    turned(m, pe, "l1xn")
    tokens_tensor(nc, pe, m, "l1xq", m.xn_t, w["wq"])
    tokens_tensor(nc, pe, m, "l1xk", m.xn_t, w["wlk"])
    tokens_tensor(nc, pe, m, "l1xv", m.xn_t, w["wlv"])
    pe.wait_ge(m.rms_done, 1)
    for name, src in (("l1xqt", m.q_tok), ("l1xkt", m.k_tok)):
        for j in range(2):
            bank = fill(m, pe, f"{name}{j}")
            for t in range(4):
                last = nc.tensor.transpose(bank[:, t * P:(t + 1) * P], src[:, 4 * j + t, :], m.ident[:, :])
            last.then_inc(filled(m, f"{name}{j}"), 1)
    bank = fill(m, pe, "l1xct0")
    for b in range(B):
        last = nc.tensor.transpose(bank[:, b * SC:(b + 1) * SC], m.context_kv[0:SC, b, 0:P], m.ident[0:SC, 0:SC])
    last.then_inc(filled(m, "l1xct0"), 1)
    for name in ("l1xqt0", "l1xqt1", "l1xkt0", "l1xkt1", "l1xct0"):
        copied(m, pe, name)
    pe.wait_ge(m.low_row_ready, 1)
    s0, x0, units = m.steps0["l1x"], m.cross0["l1x"], l1_cross_units()
    for k in range(XSTEPS + 3):
        if k < XSTEPS:
            b, h, qt = units[k]
            pe.wait_ge(m.exp_done, s0 + k - 1)
            q = m.q_t[:, b * S + qt * P:b * S + (qt + 1) * P]
            nc.tensor.matmul(m.ps[2 * (k % 2)], q, m.pair_k[:, 0, h, b * S:(b + 1) * S], start=True, stop=True)
            bank = m.ps[2 * (k % 2) + 1]
            nc.tensor.matmul(bank[:, 0:SC], q, m.pair_k[:, 1, h, b * SC:(b + 1) * SC], start=True, stop=False)
            nc.tensor.matmul(bank[:, 0:SC], m.ones_bf[0:1, :], m.low_row[0:1, b * SC:(b + 1) * SC], start=False,
                             stop=True).then_inc(m.scores_ready, 1)
        j = k - 2
        if 0 <= j < XSTEPS:
            pe.wait_ge(m.probs_ready, s0 + j + 1)
            pe.wait_ge(m.cross_taken, x0 + j)
            wait(pe, m.tail_taken, j)
            for n in range(NQ):
                nc.tensor.transpose(m.ps[4][:, n * P:(n + 1) * P], m.xp[:, j % 2, n * P:(n + 1) * P], m.ident[:, :])
            nc.tensor.transpose(m.ps[5][0:SC, 0:P], m.xp[:, j % 2, S:ALLK], m.ident[:, :]).then_inc(m.turned_ready, 1)
        j = k - 3
        if j >= 0 and (j + 1) % (2 * NQ) == 0:
            b = j // (2 * NQ)
            pe.wait_ge(m.cross_taken, x0 + j + 1)
            pe.wait_ge(m.tail_taken, j + 1)
            bank = fill(m, pe, f"l1xo{b}")
            for n in range(NQ + 1):
                for h in range(2):
                    hd = slice(64 * h, 64 * h + 64)
                    if n < NQ:
                        nc.tensor.matmul(bank[hd, :], m.v[:, b * NQ + n, hd], m.pt[:, 2 * b + h, n, :], start=n == 0,
                                         stop=False, skip_group_check=True)
                    else:
                        last = nc.tensor.matmul(bank[hd, :], m.context_kv[0:SC, b, P + 64 * h:P + 64 * h + 64],
                                                m.tail_pt[0:SC, 2 * b + h, :], start=False, stop=True,
                                                skip_group_check=True)
            last.then_inc(filled(m, f"l1xo{b}"), 1)
    project_out_tensor(nc, pe, m, "l1xo", "l1xy", w["wo"])


def l1_cross_scalar(nc, act, m):
    w = m.w["l1x"]
    act.wait_ge(m.loaded["l1x"], 16)
    bank = read(m, act, "l1xc0")
    nc.scalar.activation(m.context_norm_t[0:DC, :], bank[0:DC, 0:B * SC], ACT.Copy).then_inc(emptied(m, "l1xc0"), 1)
    for b in range(B):
        bank = read(m, act, f"l1xd{b}")
        nc.scalar.activation(m.context_kv[0:SC, b, :], bank[0:SC, 0:2 * P], ACT.Copy).then_inc(emptied(m, f"l1xd{b}"), 1)
    turn_scalar(nc, act, m, "l1xn", scale=w["ln_l_g"], bias=w["ln_l_b"])
    for name, dst in (("l1xq", m.q_tok), ("l1xk", m.k_tok), ("l1xv", m.v)):
        for j in range(2):
            bank = read(m, act, f"{name}{j}")
            nc.scalar.activation(dst[:, 4 * j:4 * j + 4, :], bank[:, :].rearrange("p (t d) -> p t d", d=P),
                                 ACT.Copy).then_inc(emptied(m, f"{name}{j}"), 1)
    for j in range(2):
        bank = read(m, act, f"l1xqt{j}")
        nc.scalar.activation(m.q_t[:, j * S:(j + 1) * S], bank[:, :], ACT.Copy,
                             scale=w["qn_g"]).then_inc(emptied(m, f"l1xqt{j}"), 1)
    for j in range(2):
        bank = read(m, act, f"l1xkt{j}")
        for h in range(2):
            own = slice(64 * h, 64 * h + 64)
            last = nc.scalar.activation(m.pair_k[own, 0, h, j * S:(j + 1) * S], bank[own, :], ACT.Copy,
                                        scale=w["kn_g"][own, :])
        last.then_inc(emptied(m, f"l1xkt{j}"), 1)
    bank = read(m, act, "l1xct0")
    for h in range(2):
        own = slice(64 * h, 64 * h + 64)
        last = nc.scalar.activation(m.pair_k[own, 1, h, 0:B * SC], bank[own, 0:B * SC], ACT.Copy, scale=w["kn_g"][own, :])
    last.then_inc(emptied(m, "l1xct0"), 1)
    s0, x0, units = m.steps0["l1x"], m.cross0["l1x"], l1_cross_units()
    for k in range(XSTEPS + 2):
        if k < XSTEPS:
            act.wait_ge(m.negmax_ready, s0 + k + 1)
            act.wait_ge(m.turned_ready, s0 + k - 1)
            nc.scalar.activation(m.xp[:, k % 2, 0:ALLK], scores_of(m, k), ACT.Exp, bias=m.negmax[:, k % 4:k % 4 + 1],
                                 accum_out=m.sum[:, k % 4:k % 4 + 1]).then_inc(m.exp_done, 1)
        j = k - 2
        if j >= 0:
            b, h, qt = units[j]
            act.wait_ge(m.turned_ready, s0 + j + 1)
            nc.scalar.activation(m.pt[:, 2 * b + h, :, qt * P:(qt + 1) * P],
                                 m.ps[4].rearrange("p (b q) -> p b q", q=P), ACT.Copy).then_inc(m.cross_taken, 1)
    copy_out_scalar(nc, act, m, "l1xo", m.o_t)


def scores_of(m, k):
    return m.psum[:, 2 * (k % 2):2 * (k % 2) + 2, :].rearrange("p g s -> p (g s)")[:, 0:ALLK]


def l1_cross_vector(nc, dve, m):
    w, d = m.w["l1x"], m.dve
    dve.wait_ge(m.loaded["l1x"], 16)
    for b in range(B):
        last = nc.vector.bn_stats(m.stats[0:SC, b, :], m.context[:, b, :])
    d.done(last)
    for b in range(B):
        last = nc.vector.bn_aggr(m.moments[0:SC, b, :], m.stats[0:SC, b, :])
    d.done(last)
    nc.vector.tensor_scalar(m.var[0:SC, 0:B], m.moments[0:SC, 0:B, 1], 1e-5, None, ALU.add).then_inc(m.var_ready, 1)
    m.norms += 1
    dve.wait_ge(m.rstd_ready, m.norms)
    for b in range(B):
        last = nc.vector.tensor_scalar(m.context[:, b, :], m.context[:, b, :], m.moments[0:SC, b, 0:1], m.rstd[0:SC, b:b + 1],
                                       ALU.subtract, ALU.mult)
    d.done(last)
    each = lambda row: row[0:SC, :].rearrange("p (o d) -> p o d", o=1).broadcast_to([SC, B, DC])
    d.done(nc.vector.tensor_tensor(m.context[:, :, :], m.context[:, :, :], each(w["ln_x_g"]), ALU.mult))
    nc.vector.tensor_tensor(m.context[:, :, :], m.context[:, :, :], each(w["ln_x_b"]), ALU.add).then_inc(m.context_normed, 1)
    nc.vector.tensor_copy(m.low_row[0:1, :], m.mask_low[0:1, B * SC:2 * B * SC]).then_inc(m.low_row_ready, 1)
    nc.vector.memset(m.rms[:, :], 1.0)
    d.done(norm_vector(nc, dve, m, m.x, m.xn))
    norm_to_turn(nc, dve, m, m.xn)
    heads = lambda ap: ap.rearrange("p t (h d) -> p (t h) d", d=64)
    for name, src, at in (("l1xq", m.q_tok, 0), ("l1xk", m.k_tok, 2 * NT)):
        for j in range(2):
            copied(m, dve, f"{name}{j}")
        d.done(nc.vector.tensor_tensor(m.squares, src, src, ALU.mult))
        d.done(nc.vector.tensor_reduce(m.rms[:, at:at + 2 * NT], heads(m.squares), AX.X, ALU.add))
    for b in range(B):
        copied(m, dve, f"l1xd{b}")
    ck = m.context_kv[0:SC, :, 0:P]
    d.done(nc.vector.tensor_tensor(m.squares[0:SC, 0:B, :], ck, ck, ALU.mult))
    d.done(nc.vector.tensor_reduce(m.rms[0:SC, 4 * NT:4 * NT + 2 * B], heads(m.squares[0:SC, 0:B, :]), AX.X, ALU.add))
    nc.vector.tensor_scalar(m.rms[:, :], m.rms[:, :], 1.0 / 64, RMS_EPS ** 2, ALU.mult, ALU.max).then_inc(m.rms_ready, 1)
    dve.wait_ge(m.rms_inverted, 1)
    q_r = m.rms[:, 0:2 * NT]
    d.done(nc.vector.tensor_scalar(q_r, q_r, float(64 ** -0.5), None, ALU.mult))
    spread = lambda ap, n: ap.rearrange("p (t o) -> p t o", o=1).broadcast_to([ap.shape[0], n, 64])
    nc.vector.tensor_tensor(heads(m.q_tok), heads(m.q_tok), spread(q_r, 2 * NT), ALU.mult)
    nc.vector.tensor_tensor(heads(m.k_tok), heads(m.k_tok), spread(m.rms[:, 2 * NT:4 * NT], 2 * NT), ALU.mult)
    ckh = ck.rearrange("p b (h d) -> p b h d", d=64)
    nc.vector.tensor_tensor(ckh, ckh, m.rms[0:SC, 4 * NT:4 * NT + 2 * B].rearrange("p (b h o) -> p b h o", h=2, o=1)
                            .broadcast_to([SC, B, 2, 64]), ALU.mult).then_inc(m.rms_done, 1)
    d.done(nc.vector.tensor_tensor(m.x[:, :, :], m.x[:, :, :], over_tiles(w["bo"]), ALU.add))
    s0, units = m.steps0["l1x"], l1_cross_units()
    for k in range(XSTEPS + 3):
        if k < XSTEPS:
            dve.wait_ge(m.scores_ready, s0 + k + 1)
            nc.vector.tensor_reduce(m.negmax[:, k % 4:k % 4 + 1], scores_of(m, k), AX.X, ALU.max,
                                    negate=True).then_inc(m.negmax_ready, 1)
        j = k - 1
        if 0 <= j < XSTEPS:
            dve.wait_ge(m.exp_done, s0 + j + 1)
            nc.vector.reciprocal(m.rsum[:, j % 4:j % 4 + 1], m.sum[:, j % 4:j % 4 + 1]).then_inc(m.rsum_ready, 1)
            dve.wait_ge(m.rsum_ready, s0 + j + 1)
            pr = m.xp[:, j % 2, 0:ALLK]
            nc.vector.tensor_scalar(pr, pr, m.rsum[:, j % 4:j % 4 + 1], None, ALU.mult).then_inc(m.probs_ready, 1)
        j = k - 3
        if j >= 0:
            b, h, qt = units[j]
            dve.wait_ge(m.turned_ready, s0 + j + 1)
            nc.vector.tensor_copy(m.tail_pt[0:SC, 2 * b + h, qt * P:(qt + 1) * P], m.ps[5][0:SC, 0:P]).then_inc(m.tail_taken, 1)
    add_to_x(nc, dve, m, "l1xy")


def l1_cross_gpsimd(nc, pool, m):
    for _ in range(3):
        norm_gpsimd(nc, pool, m)
    pool.wait_ge(m.rms_ready, 1)
    nc.gpsimd.tensor_tensor(m.rms[:, :], m.rms[:, :], m.minus_half[:, 0:1].broadcast_to([P, 4 * NT + 2 * B]),
                            ALU.pow).then_inc(m.rms_inverted, 1)





F1 = 384
INT_SCALE = 1.0 / 127.0


def l1_ffn_sync(nc, sp, m, dram):
    copied(m, sp, "l1aj1", PAIR1.uses * NPAIR // 2 - 1)
    sp.dma_start(m.ints[:, :], dram["ints"]).then_inc(m.ints_in, 16)


def l1_ffn_tensor(nc, pe, m):
    turn_tensor(nc, pe, m, "l1fn")
    turned(m, pe, "l1fn")
    pe.wait_ge(m.ints_cast, 1)
    n = F1 // P
    part = lambda what, c: m.cast_w[:, what * F1 + c * P:what * F1 + (c + 1) * P]
    for k in range(2 * n + 1):
        if k < 2 * n:
            c, j = divmod(k, 2)
            wait(pe, m.swiglu_done, k - 1)
            for what in range(2):
                last = nc.tensor.matmul(m.ps[2 * (k % 2) + what], part(what, c), m.xn_t[:, j * S:(j + 1) * S], start=True,
                                        stop=True)
            last.then_inc(m.swiglu_ready, 1)
        q = k - 1
        if q >= 0:
            c, j = divmod(q, 2)
            pe.wait_ge(m.swiglu_done, q + 1)
            bank = fill(m, pe, f"l1fy{j}") if c == 0 else m.ps[6 + j]
            last = nc.tensor.matmul(bank, part(2, c), m.hidden[:, q % 4, :], start=c == 0, stop=c == n - 1,
                                    skip_group_check=True)
            last.then_inc(filled(m, f"l1fy{j}") if c == n - 1 else m.swiglu_added, 1)
    turn_back_tensor(nc, pe, m, "l1fy", "l1fz")


def l1_ffn_scalar(nc, act, m):
    turn_scalar(nc, act, m, "l1fn")
    for k in range(2 * F1 // P):
        act.wait_ge(m.swiglu_ready, k + 1)
        wait(act, m.swiglu_added, k - 3)
        nc.scalar.activation(m.hidden[:, k % 4, :], m.ps[2 * (k % 2)], ACT.Exp, scale=-1.0).then_inc(m.swiglu_exp, 1)
    copy_out_scalar(nc, act, m, "l1fy", m.y_t)


def l1_ffn_vector(nc, dve, m):
    d = m.dve
    norm_to_turn(nc, dve, m, m.x)
    dve.wait_ge(m.ints_in, 16)
    nc.vector.tensor_scalar(m.cast_w, m.ints[:, :], float(INT_SCALE), None, ALU.mult).then_inc(m.ints_cast, 1)
    for k in range(2 * F1 // P):
        h = m.hidden[:, k % 4, :]
        gate, up = m.ps[2 * (k % 2)], m.ps[2 * (k % 2) + 1]
        dve.wait_ge(m.swiglu_exp, k + 1)
        d.done(nc.vector.tensor_scalar(h, h, 1.0, None, ALU.add))
        d.done(nc.vector.reciprocal(h, h))
        d.done(nc.vector.tensor_tensor(h, h, gate, ALU.mult))
        nc.vector.tensor_tensor(h, h, up, ALU.mult).then_inc(m.swiglu_done, 1)
    add_to_x(nc, dve, m, "l1fz")


def one_norm_gpsimd(nc, pool, m):
    norm_gpsimd(nc, pool, m)



def l2_attn_tensor(nc, pe, m):
    w = m.w["l2a"]
    pe.wait_ge(m.loaded["l2a"], 16)
    turn_tensor(nc, pe, m, "l2an")
    turned(m, pe, "l2an")
    for name, wt in (("l2aq", w["wq"]), ("l2ak", w["wk"])):
        for j in range(2):
            bank = fill(m, pe, f"{name}{j}")
            nc.tensor.matmul(bank[:, :], wt, m.xn_t[:, j * S:(j + 1) * S], start=True,
                             stop=True).then_inc(filled(m, f"{name}{j}"), 1)
    tokens_tensor(nc, pe, m, "l2av", m.xn_t, w["wv"])
    for name in ("l2aq", "l2ak", "l2av"):
        for j in range(2):
            copied(m, pe, f"{name}{j}")

    def values(pe, b):
        bank = fill(m, pe, f"l2ao{b}")
        for qt in range(NQ):
            for kt in range(NQ):
                last = nc.tensor.matmul(bank[:, qt * P:(qt + 1) * P], m.pt[:, b, kt, qt * P:(qt + 1) * P],
                                        m.v[:, b * NQ + kt, :], start=kt == 0, stop=kt == NQ - 1)
        last.then_inc(filled(m, f"l2ao{b}"), 1)

    a = Attention(steps=B * NQ, group=1, causal=False, keys=lambda qt: S,
                        q=lambda u, qt: m.q_t[:, u * S + qt * P:u * S + (qt + 1) * P],
                        k=lambda u, keys: m.k_t[:, u * S:(u + 1) * S], before_scores={}, after={}, values=values)
    attend_tensor(nc, pe, m, a, m.steps0["l2a"], m.half0["l2a"])
    project_out_tensor(nc, pe, m, "l2ao", "l2ay", w["wo"])


def l2_attn_scalar(nc, act, m):
    turn_scalar(nc, act, m, "l2an")
    for name, dst, scale in (("l2aq", m.q_t, float(np.float32(1.0) / np.sqrt(np.float32(P // H)))), ("l2ak", m.k_t, 1.0)):
        for j in range(2):
            bank = read(m, act, f"{name}{j}")
            nc.scalar.activation(dst[:, j * S:(j + 1) * S], bank[:, :], ACT.Copy,
                                 scale=scale).then_inc(emptied(m, f"{name}{j}"), 1)
    for j in range(2):
        bank = read(m, act, f"l2av{j}")
        nc.scalar.activation(m.v[:, 4 * j:4 * j + 4, :], bank[:, :].rearrange("p (t d) -> p t d", d=P),
                             ACT.Copy).then_inc(emptied(m, f"l2av{j}"), 1)
    a = Attention(steps=B * NQ, group=1, keys=lambda qt: S, scalar_after={}, group_done=lambda eng, g: None)
    attend_scalar(nc, act, m, a, m.steps0["l2a"])
    for b in range(B):
        bank = read(m, act, f"l2ao{b}")
        nc.scalar.activation(m.o_t[:, b * S:(b + 1) * S].rearrange("p (h q) -> p q h", q=NQ),
                             bank[:, :].rearrange("p (q h) -> p q h", q=NQ), ACT.Copy).then_inc(emptied(m, f"l2ao{b}"), 1)


def l2_attn_vector(nc, dve, m):
    w = m.w["l2a"]
    norm_to_turn(nc, dve, m, m.x)
    dve.wait_ge(m.loaded["l2a"], 16)
    dve.wait_ge(m.xn_ready, m.turns_dve)
    m.dve.done(nc.vector.tensor_tensor(m.x[:, :, :], m.x[:, :, :], over_tiles(w["bo"]), ALU.add))
    a = Attention(steps=B * NQ, group=1, keys=lambda qt: S, vector_after={}, group_done=lambda eng, g: None)
    attend_vector(nc, dve, m, a, m.steps0["l2a"])
    add_to_x(nc, dve, m, "l2ay")



def narrow_cross(stage, clip=None):
    a = Cross(SC, clip)

    def start(m):
        a.s0, a.x0, a.v0 = m.steps0[stage], m.cross0[stage], m.values0[stage]
        return m.w[stage]

    def tensor(nc, pe, m):
        w = start(m)
        pe.wait_ge(m.loaded[stage], 16)
        bank = fill(m, pe, f"{stage}k0")
        nc.tensor.matmul(bank[:, 0:B * SC], w["wk"][0:DC, :], m.context_t[0:DC, :], start=True,
                         stop=True).then_inc(filled(m, f"{stage}k0"), 1)
        bank = fill(m, pe, f"{stage}v0")
        for b in range(B):
            last = nc.tensor.matmul(bank[0:SC, b * P:(b + 1) * P], m.context_t[0:DC, b * SC:(b + 1) * SC], w["wv"][0:DC, :],
                                    start=True, stop=True)
        last.then_inc(filled(m, f"{stage}v0"), 1)
        turn_tensor(nc, pe, m, f"{stage}n")
        turned(m, pe, f"{stage}n")
        for j in range(2):
            bank = fill(m, pe, f"{stage}q{j}")
            nc.tensor.matmul(bank, w["wq"], m.xn_t[:, j * S:(j + 1) * S], start=True,
                             stop=True).then_inc(filled(m, f"{stage}q{j}"), 1)
        for j in range(2):
            copied(m, pe, f"{stage}q{j}")
        pe.wait_ge(m.narrow_keys, a.v0 // 2 + 1)
        pe.wait_ge(m.narrow_values, a.v0 // 2 + 1)

        def scores(bank, b, half, j, qt):
            at = (8 * half + 4 * j) * SC
            return nc.tensor.matmul(bank[:, 0:4 * SC], m.q_t[:, b * S + qt * P:b * S + (qt + 1) * P],
                                    m.keys_own[:, b, at:at + 4 * SC], start=True, stop=True)

        def values(pe, b, half):
            bank = fill(m, pe, f"{stage}o{b}") if half == 0 else m.ps[6 + b]
            for h in range(8):
                last = nc.tensor.matmul(bank, m.values_own[0:SC, b, 8 * half + h, :], m.xpt[0:SC, half, h, :],
                                        start=half == 0 and h == 0, stop=half == 1 and h == 7, skip_group_check=True)
            last.then_inc(filled(m, f"{stage}o{b}") if half else m.pv_done, 1)

        a.scores, a.values = scores, values
        cross_tensor(nc, pe, m, a)
        if clip:
            bank = fill(m, pe, f"{stage}g0")
            for b in range(B):
                nc.tensor.matmul(bank[:, b:b + 1], m.context_kv[0:SC, b, 0:P], m.share[0:SC, :], start=True, stop=True)
            pe.wait_ge(m.sums_are_numbers, 1)
            nc.tensor.transpose(bank[0:1, P:2 * P], m.number[:, 0:1], m.ident[:, :]).then_inc(filled(m, f"{stage}g0"), 1)
            pe.wait_ge(m.sums_are_numbers, 2)
            bank = fill(m, pe, f"{stage}h0")
            nc.tensor.matmul(bank[:, 0:1], m.ones_row[0:1, :], m.number[0:1, 1:2], start=True,
                             stop=True).then_inc(filled(m, f"{stage}h0"), 1)
            pe.wait_ge(m.sums_are_numbers, 3)
        project_out_tensor(nc, pe, m, f"{stage}o", f"{stage}y", w["wo"])

    def scalar(nc, act, m):
        w = start(m)
        act.wait_ge(m.loaded[stage], 16)
        bank = read(m, act, f"{stage}k0")
        nc.scalar.activation(m.context_k[:, :], bank[:, 0:B * SC], ACT.Identity,
                             bias=w["bk"]).then_inc(emptied(m, f"{stage}k0"), 1)
        turn_scalar(nc, act, m, f"{stage}n")
        for j in range(2):
            bank = read(m, act, f"{stage}q{j}")
            nc.scalar.activation(m.q_t[:, j * S:(j + 1) * S], bank, ACT.Identity,
                                 bias=w["bq"]).then_inc(emptied(m, f"{stage}q{j}"), 1)

        def unit_done(act, b, half):
            if half:
                read(m, act, f"{stage}o{b}")
            else:
                act.wait_ge(m.pv_done, m.pv0 + a.v0 + b + 1)

        a.unit_done = unit_done
        cross_scalar(nc, act, m, a)
        copy_out_scalar(nc, act, m, f"{stage}o", m.o_t)

    def vector(nc, dve, m):
        w, d = start(m), m.dve
        dve.wait_ge(m.loaded[stage], 16)
        copied(m, dve, f"{stage}k0")
        for b in range(B):
            shape = [P, H, SC]
            last = nc.vector.tensor_tensor(
                m.keys_own[:, b, 0:H * SC].rearrange("p (h k) -> p h k", k=SC),
                m.context_k[:, b * SC:(b + 1) * SC].rearrange("p (o k) -> p o k", o=1).broadcast_to(shape),
                m.rows8[:, 0:H].rearrange("p (h o) -> p h o", o=1).broadcast_to(shape), ALU.mult)
        last.then_inc(m.narrow_keys, 1)
        bank = read(m, dve, f"{stage}v0")
        nc.vector.tensor_tensor(m.context_kv[0:SC, :, 0:P], bank[0:SC, 0:B * P].rearrange("p (b d) -> p b d", b=B),
                                over_tiles(w["bv"], B)[0:SC], ALU.add).then_inc(emptied(m, f"{stage}v0"), 1)
        norm_to_turn(nc, dve, m, m.x)
        dve.wait_ge(m.xn_ready, m.turns_dve)
        d.done(nc.vector.tensor_tensor(m.x[:, :, :], m.x[:, :, :], over_tiles(w["bo"]), ALU.add))
        cross_vector(nc, dve, m, a)
        if clip:
            d.done(nc.vector.tensor_tensor(m.numbers[:, :], m.xsum[:, :], m.xsum[:, :], ALU.is_equal))
            nc.vector.tensor_reduce(m.number[:, 0:1], m.numbers[:, :], AX.X, ALU.min).then_inc(m.sums_are_numbers, 1)
            bank = read(m, dve, f"{stage}g0")
            nc.vector.tensor_copy(m.average[:, :], bank[:, 0:B])
            d.done(nc.vector.tensor_reduce(m.number[0:1, 1:2], bank[0:1, P:2 * P], AX.X, ALU.min))
            nc.vector.engine_nop().then_inc(emptied(m, f"{stage}g0"), 1)
            nc.vector.engine_nop().then_inc(m.sums_are_numbers, 1)
            bank = read(m, dve, f"{stage}h0")
            nc.vector.tensor_scalar(m.number[:, 2:3], bank[:, 0:1], 0.5, None, ALU.is_lt).then_inc(emptied(m, f"{stage}h0"), 1)
            copied(m, dve, f"{stage}h0")
            for b in range(B):
                copied(m, dve, f"{stage}o{b}")
            for b in range(B):
                last = nc.vector.copy_predicated(m.o_t[:, b * S:(b + 1) * S],
                                                 m.number[:, 2:3].bitcast(U32).broadcast_to([P, S]),
                                                 m.average[:, b:b + 1].broadcast_to([P, S]))
            last.then_inc(m.sums_are_numbers, 1)
        add_to_x(nc, dve, m, f"{stage}y")

    def gpsimd(nc, pool, m):
        start(m)
        copied(m, pool, f"{stage}v0")
        for b in range(B):
            last = nc.gpsimd.tensor_tensor(m.values_own[0:SC, b, :, :],
                                           m.context_kv[0:SC, b, 0:P].rearrange("p (o d) -> p o d", o=1).broadcast_to([SC, H, P]),
                                           m.cols8[0:SC, 0:H, :], ALU.mult)
        last.then_inc(m.narrow_values, 1)
        norm_gpsimd(nc, pool, m)
        cross_gpsimd(nc, pool, m, a)

    return stage, tensor, scalar, vector, gpsimd, None



E2, F2 = 16, 512
CAP = T // E2
SLOT_W = 2 * F2 + F2 // P + P


def l2_ffn_sync(nc, sp, m, dram):
    sp.wait_ge(m.ints_cast, 1)
    stream_sync(sp, m, dram["s_l2f"], E2 // 2, lambda i, s: sp.wait_ge(m.expert_taken, 2 * (i - 1) + s + 1))


def l2_ffn_tensor(nc, pe, m):
    w = m.w["l2f"]
    pe.wait_ge(m.loaded["l2f"], 16)
    turn_tensor(nc, pe, m, "l2fn")
    turned(m, pe, "l2fn")
    for j in range(2):
        bank = fill(m, pe, f"l2fr{j}")
        nc.tensor.matmul(bank[0:E2, :], w["router"], m.xn_t[:, j * S:(j + 1) * S], start=True,
                         stop=True).then_inc(filled(m, f"l2fr{j}"), 1)
    for name, src in (("l2fl0", m.logits), ("l2fp0", m.places)):
        if name == "l2fl0":
            for j in range(2):
                copied(m, pe, f"l2fr{j}")
        else:
            pe.wait_ge(m.places_ready, 1)
        bank = fill(m, pe, name)
        for t in range(NT):
            last = nc.tensor.transpose(bank[:, t * E2:(t + 1) * E2], src[0:E2, t * P:(t + 1) * P], m.ident[0:E2, 0:E2])
        last.then_inc(filled(m, name), 1)
    for j in range(2):
        fill(m, pe, f"l2fx{j}")
    for t in range(NT):
        pe.wait_ge(m.chosen_ready, t + 1)
        for j in range(2):
            last = nc.tensor.matmul(m.ps[m.items[f"l2fx{j}"][0]], m.xn[:, t, :], m.wide[:, t, j * S:(j + 1) * S],
                                    start=t == 0, stop=t == NT - 1, skip_group_check=True)
            if t == NT - 1:
                last.then_inc(filled(m, f"l2fx{j}"), 1)
    for j in range(2):
        copied(m, pe, f"l2fx{j}")
    g0 = m.slot0["l2f"]

    with pe.Fori(0, E2 // 2) as i:
        for s in range(2):
            pe.wait_ge(m.slot_in[s], 16 * (g0 + i + 1))
            for c in range(F2 // P):
                last = nc.tensor.matmul(m.ps[s][:, c * CAP:(c + 1) * CAP], m.slots[:, s, c * P:(c + 1) * P],
                                        m.chosen_t[:, bass.ds((2 * i + s) * CAP, CAP)], start=True, stop=True)
            last.then_inc(m.expert_hidden, 1)
        for s in range(2):
            pe.wait_ge(m.expert_gelu, 2 * i + s + 1)
            for c in range(F2 // P):
                last = nc.tensor.matmul(m.ps[2 + s][64 * s:64 * s + CAP, 0:P], m.expert_h[:, s, c * CAP:(c + 1) * CAP],
                                        m.slots[:, s, F2 + c * P:F2 + (c + 1) * P], start=c == 0, stop=c == F2 // P - 1)
            last.then_inc(m.expert_y_ready, 1)
    for n in range(2 * NT):
        t, j = divmod(n, 2)
        pe.wait_ge(m.weighted_ready, NT)
        bank = fill(m, pe, f"l2fw{n}")
        for g in range(4):
            last = nc.tensor.transpose(bank[:, g * P:(g + 1) * P], m.weighted[:, t, (4 * j + g) * P:(4 * j + g + 1) * P],
                                       m.ident[:, :])
        last.then_inc(filled(m, f"l2fw{n}"), 1)
    for n in (2 * NT - 2, 2 * NT - 1):
        copied(m, pe, f"l2fw{n}")
    pe.wait_ge(m.expert_taken, E2)
    for j in range(2):
        bank = fill(m, pe, f"l2fy{j}")
        for g in range(E2 // 2):
            last = nc.tensor.matmul(bank, m.v[:, g, :], m.wide[:, g, j * S:(j + 1) * S], start=g == 0,
                                    stop=g == E2 // 2 - 1)
        last.then_inc(filled(m, f"l2fy{j}"), 1)
    turn_back_tensor(nc, pe, m, "l2fy", "l2fz")


def l2_ffn_scalar(nc, act, m):
    w = m.w["l2f"]
    act.wait_ge(m.loaded["l2f"], 16)
    turn_scalar(nc, act, m, "l2fn")
    for j in range(2):
        bank = read(m, act, f"l2fr{j}")
        nc.scalar.activation(m.logits[0:E2, j * S:(j + 1) * S], bank[0:E2, :], ACT.Identity,
                             bias=w["router_b"][0:E2, :]).then_inc(emptied(m, f"l2fr{j}"), 1)
    act.wait_ge(m.router_less_max, 2)
    nc.scalar.activation(m.probs16[:, :, :], m.probs16[:, :, :], ACT.Exp).then_inc(m.router_exp, 1)
    for j in range(2):
        bank = read(m, act, f"l2fx{j}")
        nc.scalar.activation(m.chosen_t[:, j * S:(j + 1) * S], bank, ACT.Copy).then_inc(emptied(m, f"l2fx{j}"), 1)

    with act.Fori(0, E2 // 2) as i:
        for s in range(2):
            act.wait_ge(m.expert_biased, 2 * i + s + 1)
            h = m.expert_h[:, s, :]
            nc.scalar.activation(h, h, ACT.Gelu).then_inc(m.expert_gelu, 1)
    for n in range(0, 2 * NT, 2):
        take_weighted(lambda out, in_: nc.scalar.activation(out, in_, ACT.Copy), act, m, n)
    copy_out_scalar(nc, act, m, "l2fy", m.y_t)


def take_weighted(copy, eng, m, n):
    t, j = divmod(n, 2)
    bank = read(m, eng, f"l2fw{n}")
    copy(m.wide[:, 4 * j:4 * j + 4, t * P:(t + 1) * P],
         bank.rearrange("p (g q) -> p g q", q=P)).then_inc(emptied(m, f"l2fw{n}"), 1)


def l2_ffn_vector(nc, dve, m):
    w, d = m.w["l2f"], m.dve
    dve.wait_ge(m.loaded["l2f"], 16)
    d.done(norm_vector(nc, dve, m, m.x, m.xn))
    d.done(nc.vector.tensor_tensor(m.squares, m.xn[:, :, :], m.xn[:, :, :], ALU.mult))
    d.done(nc.vector.tensor_reduce(m.per_token[:, 0, :], m.squares, AX.X, ALU.add))
    nc.vector.tensor_scalar(m.var[:, :], m.per_token[:, 0, :], 1.0 / P, 1e-5, ALU.mult, ALU.add).then_inc(m.var_ready, 1)
    m.norms += 1
    dve.wait_ge(m.rstd_ready, m.norms)
    d.done(nc.vector.tensor_tensor(m.xn[:, :, :], m.xn[:, :, :],
                                   m.rstd[:, :].rearrange("p (t o) -> p t o", o=1).broadcast_to([P, NT, P]), ALU.mult))
    nc.vector.tensor_tensor(m.xn[:, :, :], m.xn[:, :, :], over_tiles(w["norm_w"]), ALU.mult).then_inc(m.xn_ready, 1)
    m.turns_dve += 1
    for j in range(2):
        copied(m, dve, f"l2fr{j}")
    src = m.logits[0:E2, :]
    for r in range(CAP // 8):
        d.done(nc.vector.max(m.top8[0:E2, r % 2, :], src))
        if r < CAP // 8 - 1:
            d.done(nc.vector.match_replace(m.left[0:E2, :], m.top8[0:E2, r % 2, :], src, -BIG))
            src = m.left[0:E2, :]
    limit = m.top8[0:E2, (CAP // 8 - 1) % 2, 7:8]
    above, level, count = m.left[0:E2, :], m.places[0:E2, :], m.running[0:E2, :]
    one = m.ones_col[0:E2, 0:1].broadcast_to([E2, T])
    d.done(nc.vector.tensor_scalar(above, m.logits[0:E2, :], limit, None, ALU.is_gt))
    d.done(nc.vector.tensor_reduce(m.needed[0:E2, 0:1], above, AX.X, ALU.add))
    d.done(nc.vector.tensor_scalar(m.needed[0:E2, 1:2], m.needed[0:E2, 0:1], -1.0, float(CAP), ALU.mult, ALU.add))
    d.done(nc.vector.tensor_scalar(level, m.logits[0:E2, :], limit, None, ALU.is_equal))
    d.done(nc.vector.tensor_tensor_scan(count, one, level, 0.0, ALU.mult, ALU.add))
    d.done(nc.vector.tensor_scalar(count, count, m.needed[0:E2, 1:2], None, ALU.is_le))
    d.done(nc.vector.tensor_tensor(level, level, count, ALU.mult))
    d.done(nc.vector.tensor_tensor(above, above, level, ALU.add))
    d.done(nc.vector.tensor_tensor_scan(count, one, above, 0.0, ALU.mult, ALU.add))
    nc.vector.tensor_tensor(level, count, above, ALU.mult).then_inc(m.places_ready, 1)
    probs = m.probs16[:, :, :]
    last16 = lambda ap: ap.rearrange("p (t o) -> p t o", o=1).broadcast_to([P, NT, E2])
    bank = read(m, dve, "l2fl0")
    logits = bank[:, 0:NT * E2].rearrange("p (t e) -> p t e", e=E2)
    d.done(nc.vector.tensor_reduce(m.per_token[:, 1, :], logits, AX.X, ALU.max))
    nc.vector.tensor_tensor(probs, logits, last16(m.per_token[:, 1, :]), ALU.subtract).then_inc(emptied(m, "l2fl0"), 1)
    copied(m, dve, "l2fl0")
    nc.vector.engine_nop().then_inc(m.router_less_max, 1)
    bank = read(m, dve, "l2fp0")
    nc.vector.tensor_copy(m.place[:, :, :], bank[:, 0:NT * E2].rearrange("p (t e) -> p t e", e=E2)).then_inc(
        emptied(m, "l2fp0"), 1)
    copied(m, dve, "l2fp0")
    for t in range(NT):
        shape = [P, E2, CAP]
        nc.vector.tensor_tensor(m.wide[:, t, :].rearrange("p (e s) -> p e s", s=CAP),
                                w["one_to_cap"].rearrange("p (o s) -> p o s", o=1).broadcast_to(shape),
                                m.place[:, t, :].rearrange("p (e o) -> p e o", o=1).broadcast_to(shape),
                                ALU.is_equal).then_inc(m.chosen_ready, 1)
    dve.wait_ge(m.router_exp, 2)
    d.done(nc.vector.tensor_reduce(m.per_token[:, 2, :], probs, AX.X, ALU.add))
    d.done(nc.vector.reciprocal(m.per_token[:, 3, :], m.per_token[:, 2, :]))
    d.done(nc.vector.tensor_tensor(probs, probs, last16(m.per_token[:, 3, :]), ALU.mult))
    d.done(nc.vector.tensor_scalar(m.place[:, :, :], m.place[:, :, :], 0.5, None, ALU.is_gt))
    nc.vector.tensor_tensor(m.place[:, :, :], m.place[:, :, :], probs, ALU.mult).then_inc(m.gates_ready, 1)
    dve.wait_ge(m.gates_ready, 2)
    d.done(nc.vector.tensor_reduce(m.per_token[:, 0, :], m.place[:, :, :], AX.X, ALU.add))
    d.done(nc.vector.tensor_scalar(m.per_token[:, 1, :], m.per_token[:, 0, :], 0.0, None, ALU.is_le))
    d.done(nc.vector.tensor_tensor(m.per_token[:, 0, :], m.per_token[:, 0, :], m.per_token[:, 1, :], ALU.add))
    d.done(nc.vector.reciprocal(m.per_token[:, 1, :], m.per_token[:, 0, :]))

    with dve.Fori(0, E2 // 2) as i:
        for s in range(2):
            dve.wait_ge(m.expert_hidden, 2 * i + s + 1)
            bias = m.slots[:, s, 2 * F2:2 * F2 + F2 // P].rearrange("p (c o) -> p c o", o=1)
            nc.vector.tensor_tensor(m.expert_h[:, s, :].rearrange("p (c n) -> p c n", n=CAP),
                                    m.ps[s][:, 0:F2 // P * CAP].rearrange("p (c n) -> p c n", n=CAP),
                                    bias.broadcast_to([P, F2 // P, CAP]), ALU.add).then_inc(m.expert_biased, 1)
        for s in range(2):
            dve.wait_ge(m.expert_y_ready, 2 * i + s + 1)
            own = slice(64 * s, 64 * s + CAP)
            nc.vector.tensor_tensor(m.v[own, bass.ds(i, 1), :].rearrange("p o d -> p (o d)"), m.ps[2 + s][own, 0:P],
                                    m.slots[own, s, SLOT_W - P:SLOT_W], ALU.add).then_inc(m.expert_taken, 1)
    for n in range(1, 2 * NT, 2):
        take_weighted(nc.vector.tensor_copy, dve, m, n)
    for j in range(2):
        bank = read(m, dve, f"l2fz{j}")
        tiles = slice(4 * j, 4 * j + 4)
        nc.vector.tensor_tensor(m.xn[:, tiles, :], bank.rearrange("p (t d) -> p t d", d=P),
                                m.per_token[:, 1, tiles].rearrange("p (t o) -> p t o", o=1).broadcast_to([P, 4, P]),
                                ALU.mult).then_inc(emptied(m, f"l2fz{j}"), 1)
    for j in range(2):
        copied(m, dve, f"l2fz{j}")
    d.done(nc.vector.tensor_tensor(m.x[:, :, :], m.x[:, :, :], m.xn[:, :, :], ALU.add))


def l2_ffn_gpsimd(nc, pool, m):
    norm_gpsimd(nc, pool, m)
    norm_gpsimd(nc, pool, m)
    pool.wait_ge(m.gates_ready, 2)
    for t in range(NT):
        shape = [P, E2, CAP]
        pool.wait_ge(m.chosen_ready, t + 1)
        split = lambda ap: ap.rearrange("p (e s) -> p e s", s=CAP)
        nc.gpsimd.tensor_tensor(split(m.weighted[:, t, :]), split(m.wide[:, t, :]),
                                m.place[:, t, :].rearrange("p (e o) -> p e o", o=1).broadcast_to(shape),
                                ALU.mult).then_inc(m.weighted_ready, 1)



DK, DV = 4, 8
QKVG = 2 * H * DK + 2 * P
TAPS = 4
FAR = -87.0


def per_head(ap, width):
    return ap.rearrange("p t (h d) -> p t h d", d=width)


def over_head(ap, width):
    t = ap.shape[1]
    return ap.rearrange("p t (h o) -> p t h o", o=1).broadcast_to([P, t, H, width])


def l3_attn_tensor(nc, pe, m):
    w = m.w["l3a"]
    pe.wait_ge(m.loaded["l3a"], 16)
    turn_tensor(nc, pe, m, "l3an")
    pe.wait_ge(m.conv_done, 1)
    for t in range(NT):
        bank = fill(m, pe, f"l3ap{t}")
        nc.tensor.matmul(bank[:, 0:QKVG], m.k_t[:, t * P:(t + 1) * P], w["wqkvg"], start=True,
                         stop=True).then_inc(filled(m, f"l3ap{t}"), 1)
    turn_tensor(nc, pe, m, "l3am")
    turned(m, pe, "l3am")
    tokens_tensor(nc, pe, m, "l3ay", m.xn_t, w["wo"])


def l3_attn_scalar(nc, act, m):
    turn_scalar(nc, act, m, "l3an")
    act.wait_ge(m.gla_ready, 1)
    nc.scalar.activation(m.q_t[:, :], m.q_t[:, :], ACT.Exp, scale=-1.0).then_inc(m.gla_exp, 1)
    for t in range(NT):
        bank = read(m, act, f"l3ap{t}")
        nc.scalar.activation(m.wide[:, t, 0:QKVG], bank[:, 0:QKVG], ACT.Copy).then_inc(emptied(m, f"l3ap{t}"), 1)
    decay = m.gla["decay"]
    act.wait_ge(m.gla_ready, 2)
    nc.scalar.activation(decay, decay, ACT.Exp, scale=-1.0).then_inc(m.gla_exp, 1)
    act.wait_ge(m.gla_exp, 2)
    nc.scalar.activation(decay, decay, ACT.Ln, bias=m.ones_col[:, :]).then_inc(m.gla_exp, 1)
    act.wait_ge(m.gla_ready, 3)
    nc.scalar.activation(decay, decay, ACT.Exp, scale=1.0 / 16.0).then_inc(m.gla_exp, 1)
    act.wait_ge(m.gla_ready, 4)
    nc.scalar.activation(m.gla["sig_g"], m.gla["sig_g"], ACT.Exp, scale=-1.0).then_inc(m.gla_exp, 1)
    act.wait_ge(m.gla_ready, 5)
    nc.scalar.activation(m.gla["aug"], m.gla["aug"], ACT.Exp, scale=-1.0).then_inc(m.gla_exp, 1)
    turn_scalar(nc, act, m, "l3am")


def l3_attn_vector(nc, dve, m):
    w, d, g = m.w["l3a"], m.dve, m.gla
    tt, ts = nc.vector.tensor_tensor, nc.vector.tensor_scalar
    dve.wait_ge(m.loaded["l3a"], 16)
    norm_to_turn(nc, dve, m, m.x)
    for j in range(2):
        copied(m, dve, f"l3an{j}")
    y, e = m.k_t, m.q_t
    d.done(ts(y[:, :], m.xn_t[:, :], w["conv"][:, TAPS - 1:TAPS], None, ALU.mult))
    d.done(ts(e[:, 0:S], m.xn_t[:, 0:S], w["conv"][:, TAPS - 2:TAPS - 1], None, ALU.mult))
    d.done(tt(y[:, S:T], y[:, S:T], e[:, 0:S], ALU.add))
    ts(e[:, :], y[:, :], FAR, None, ALU.max).then_inc(m.gla_ready, 1)
    dve.wait_ge(m.gla_exp, 1)
    d.done(ts(e[:, :], e[:, :], 1.0, None, ALU.add))
    d.done(nc.vector.reciprocal(e[:, :], e[:, :]))
    tt(y[:, :], y[:, :], e[:, :], ALU.mult).then_inc(m.conv_done, 1)
    for t in range(NT):
        copied(m, dve, f"l3ap{t}")
    q, gate, v, decay, k = g["q"], g["gate"], g["v"], g["decay"], g["k"]
    d.done(ts(k, gate, -1.0, None, ALU.mult))
    tt(decay, gate, k, ALU.max).then_inc(m.gla_ready, 1)
    dve.wait_ge(m.gla_ready, 2)
    d.done(ts(k, gate, 0.0, None, ALU.min))
    dve.wait_ge(m.gla_exp, 3)
    tt(decay, k, decay, ALU.subtract).then_inc(m.gla_ready, 1)
    d.done(tt(g["g"], g["g"], over_tiles(w["bg"]), ALU.add))
    ts(g["sig_g"], g["g"], FAR, None, ALU.max).then_inc(m.gla_ready, 1)
    dve.wait_ge(m.gla_exp, 4)
    d.done(ts(k, decay, -1.0, 1.0, ALU.mult, ALU.add))
    qk, own, past = g["qk"], m.place[:, :, :], m.probs16[:, NQ:NT, :]
    d.done(tt(qk, q, k, ALU.mult))
    d.done(nc.vector.tensor_reduce(own, per_head(qk, DK), AX.X, ALU.add))
    d.done(tt(qk, qk, over_tiles(w["aug_balance"]), ALU.mult))
    d.done(nc.vector.tensor_reduce(m.probs16[:, :, :], per_head(qk, DK), AX.X, ALU.add))
    d.done(tt(per_head(g["aug"], DV), over_head(m.probs16[:, :, :], DV), per_head(v, DV), ALU.mult))
    ts(g["aug"], g["aug"], FAR, None, ALU.max).then_inc(m.gla_ready, 1)
    dve.wait_ge(m.gla_ready, 5)
    d.done(ts(own, own, DK ** -0.5, None, ALU.mult))
    d.done(tt(per_head(g["o"], DV), over_head(own, DV), per_head(v, DV), ALU.mult))
    second = slice(NQ, NT)
    d.done(tt(qk[:, second], q[:, second], decay[:, second], ALU.mult))
    d.done(tt(qk[:, second], qk[:, second], k[:, 0:NQ], ALU.mult))
    d.done(nc.vector.tensor_reduce(past, per_head(qk[:, second], DK), AX.X, ALU.add))
    d.done(ts(past, past, DK ** -0.5, None, ALU.mult))
    d.done(tt(per_head(g["tmp"][:, second], DV), over_head(past, DV), per_head(v[:, 0:NQ], DV), ALU.mult))
    d.done(tt(g["o"][:, second], g["o"][:, second], g["tmp"][:, second], ALU.add))
    dve.wait_ge(m.gla_exp, 6)
    for part in ("aug", "sig_g"):
        d.done(ts(g[part], g[part], 1.0, None, ALU.add))
        d.done(nc.vector.reciprocal(g[part], g[part]))
    o = g["o"]
    d.done(tt(o, o, g["aug"], ALU.add))
    mean, var = m.place[:, :, :], m.probs16[:, :, :]
    d.done(nc.vector.tensor_reduce(mean, per_head(o, DV), AX.X, ALU.add))
    d.done(ts(mean, mean, 1.0 / DV, None, ALU.mult))
    d.done(tt(per_head(o, DV), per_head(o, DV), over_head(mean, DV), ALU.subtract))
    d.done(tt(g["tmp"], o, o, ALU.mult))
    d.done(nc.vector.tensor_reduce(var, per_head(g["tmp"], DV), AX.X, ALU.add))
    ts(var, var, 1.0 / DV, 1e-5, ALU.mult, ALU.add).then_inc(m.head_var_ready, 1)
    d.done(tt(g["sig_g"], g["sig_g"], g["g"], ALU.mult))
    d.done(tt(o, o, g["sig_g"], ALU.mult))
    dve.wait_ge(m.head_rstd_ready, 1)
    tt(per_head(m.xn[:, :, :], DV), per_head(o, DV), over_head(var, DV), ALU.mult).then_inc(m.xn_ready, 1)
    m.turns_dve += 1
    add_to_x(nc, dve, m, "l3ay")


def l3_attn_gpsimd(nc, pool, m):
    norm_gpsimd(nc, pool, m)
    pool.wait_ge(m.head_var_ready, 1)
    var = m.probs16[:, :, :].rearrange("p t h -> p (t h)")
    nc.gpsimd.tensor_tensor(var, var, m.minus_half[:, 0:1].broadcast_to([P, NT * H]), ALU.pow).then_inc(m.head_rstd_ready, 1)



E3, ROT, F3 = 8, 32, 512
GROUPS3 = 4
MIXES = 2 * NT
SPREADS = B * E3


def l3_ffn_sync(nc, sp, m, dram):
    sp.wait_ge(m.expert_taken, E2)
    stream_sync(sp, m, dram["s_l3v"], NPAIR // 2,
                lambda i, s: sp.wait_ge(m.mixed_taken, MIXES * (2 * (i - 1) + s + 1)))
    weights = dram["s_l3q"]

    def one_pass(i):
        for s in range(2):
            if isinstance(i, int):
                sp.wait_ge(m.mixed_gated, MIXES * NPAIR)
                src, values = weights[2 * i + s], m.wide[:, 2 * i + s, :]
            else:
                read(m, sp, "l3fj1", PAIR3.uses * (i - 1) + PAIR3.output[s, 1][1])
                src = weights[bass.ds(2 * i + s, 1)].rearrange("o p n -> (o p) n")
                values = m.wide[:, bass.ds(2 * i + s, 1), :].rearrange("p o n -> p (o n)")
            sp.dma_start(m.slots[:, s, 0:S], src).then_inc(m.slot_in[s], 16)
            sp.dma_start(m.pair_v[s].rearrange("p t d -> p (t d)"), values).then_inc(m.values_in[s], 16)

    one_pass(0)
    with sp.Fori(1, NPAIR // 2) as i:
        one_pass(i)
    sp.wait_ge(m.rope_added, 6 * NPAIR)
    stream_sync(sp, m, dram["s_l3o"], NPAIR // 2,
                lambda i, s: sp.wait_ge(m.spread_used, SPREADS * (2 * (i - 1) + s + 1)))


def l3_ffn_tensor(nc, pe, m):
    w = m.w["l3f"]
    pe.wait_ge(m.loaded["l3f"], 16)
    turn_tensor(nc, pe, m, "l3fn")
    turned(m, pe, "l3fn")
    for n in range(4):
        bank = fill(m, pe, f"l3fs{n}")
        for k in range(2):
            last = nc.tensor.matmul(bank[:, k * 2 * P:(k + 1) * 2 * P], m.xn_t[:, (2 * n + k) * P:(2 * n + k + 1) * P],
                                    w["wsel"], start=True, stop=True)
        last.then_inc(filled(m, f"l3fs{n}"), 1)
    g0 = m.slot0["l3v"]

    with pe.Fori(0, NPAIR // 2) as i:
        for s in range(2):
            pe.wait_ge(m.slot_in[s], 16 * (g0 + i + 1))
            for n in range(MIXES):
                t, h = divmod(n, 2)
                if s > 0 or n >= 4:
                    pe.wait_ge(m.mixed_taken, 2 * MIXES * i + MIXES * s + n - 3)
                nc.tensor.matmul(m.ps[n % 4], m.xn_t[:, t * P:(t + 1) * P], m.slots[:, s, h * S:(h + 1) * S], start=True,
                                 stop=True).then_inc(m.mixed_ready, 1)
        pe.wait_ge(m.mixed_taken, 2 * MIXES * (i + 1))
    pe.wait_ge(m.parts_ready, 1)
    for q in range(GROUPS3):
        for j in range(2):
            bank = fill(m, pe, f"l3fg{2 * q + j}")
            for t in range(4):
                last = nc.tensor.matmul(bank[:, t * P:(t + 1) * P],
                                        m.gate_parts[:, 4 * j + t, q, :, :].rearrange("p c g -> p (c g)"),
                                        m.ident_bf[:, :], start=True, stop=True)
            last.then_inc(filled(m, f"l3fg{2 * q + j}"), 1)
    n0, half0, q0 = m.steps0["l3f"], m.half0["l3f"], m.slot0["l3q"]

    def project(pe, i, s):
        pe.wait_ge(m.slot_in[s], 16 * (q0 + i + 1))
        for n in range(8):
            what, j = divmod(n, 2)
            bank = fill(m, pe, f"l3fj{j}", PAIR3.uses * i + PAIR3.first[6 + j, s] + what)
            nc.tensor.matmul(bank, m.slots[:, s, what * P:(what + 1) * P], m.xn_t[:, j * S:(j + 1) * S], start=True,
                             stop=True).then_inc(filled(m, f"l3fj{j}"), 1)

    def projected(pe, i, s):
        pe.wait_ge(m.rope_added, 12 * i + 6 * (s + 1))
        pe.wait_ge(m.values_in[s], 16 * (i + 1))

    with pe.Fori(0, NPAIR // 2) as i:
        pair_attend_tensor(nc, pe, m, "l3fj", i, n0, half0, False, project, lambda pe, s: projected(pe, i, s))
    for j in range(2):
        copied(m, pe, f"l3fj{j}", PAIR3.uses * NPAIR // 2 - 1)
    for j in range(2):
        bank = fill(m, pe, f"l3fy{j}")
        nc.tensor.matmul(bank, m.zeros[:, :], m.xn_t[:, j * S:(j + 1) * S], start=True, stop=False, skip_group_check=True)
    o0 = m.slot0["l3o"]

    with pe.Fori(0, NPAIR // 2) as i:
        base = 2 * SPREADS * i
        for k in range(2 * SPREADS + 2):
            if k < 2 * SPREADS:
                s, e, b = k // SPREADS, k % SPREADS // 2, k % 2
                if k % SPREADS == 0:
                    pe.wait_ge(m.slot_in[s], 16 * (o0 + i + 1))
                if k >= 4:
                    pe.wait_ge(m.spread_gated, base + k - 3)
                nc.tensor.matmul(m.ps[k % 4], m.select[:, s * E3 + e, :],
                                 m.gate_rows[:, bass.ds(i, 1), b * S:(b + 1) * S].rearrange("p o n -> p (o n)"), start=True,
                                 stop=True).then_inc(m.spread_ready, 1)
            q = k - 2
            if q >= 0:
                s, e, b = q // SPREADS, q % SPREADS // 2, q % 2
                pe.wait_ge(m.spread_gated, base + q + 1)
                nc.tensor.matmul(m.ps[6 + b], m.slots[:, s, e * P:(e + 1) * P], m.gated[:, q % 4, :], start=False,
                                 stop=False, skip_group_check=True).then_inc(m.spread_used, 1)
    complete(nc, pe, m, "l3fy")
    turn_back_tensor(nc, pe, m, "l3fy", "l3fz")
    turn_tensor(nc, pe, m, "l3fm")
    turned(m, pe, "l3fm")
    h0, chunks = m.h0["l3f"], F3 // P
    for k in range(2 * chunks + 2):
        if k < 2 * chunks:
            c, j = divmod(k, 2)
            if k >= 4:
                pe.wait_ge(m.hidden_read, h0 + k - 3)
            nc.tensor.matmul(m.ps[k % 4], w["w1"][:, c * P:(c + 1) * P], m.xn_t[:, j * S:(j + 1) * S], start=True,
                             stop=True).then_inc(m.hidden_ready, 1)
        q = k - 2
        if q >= 0:
            c, j = divmod(q, 2)
            pe.wait_ge(m.hidden_read, h0 + q + 1)
            bank = fill(m, pe, f"l3fu{j}") if c == 0 else m.ps[6 + j]
            last = nc.tensor.matmul(bank, w["w2"][:, c * P:(c + 1) * P], m.hidden[:, q % 4, :], start=c == 0,
                                    stop=c == chunks - 1, skip_group_check=True)
            last.then_inc(filled(m, f"l3fu{j}") if c == chunks - 1 else m.hidden_used, 1)
    turn_back_tensor(nc, pe, m, "l3fu", "l3fw")


def l3_ffn_scalar(nc, act, m):
    w = m.w["l3f"]
    act.wait_ge(m.loaded["l3f"], 16)
    turn_scalar(nc, act, m, "l3fn")
    for n in range(4):
        act.wait_ge(m.pick_ready, n + 1)
        part = m.pick[:, n * S:(n + 1) * S]
        nc.scalar.activation(part, part, ACT.Exp, scale=-1.0).then_inc(m.pick_exp, 1)
    for n in range(2 * GROUPS3):
        q, j = divmod(n, 2)
        bank = read(m, act, f"l3fg{n}")
        nc.scalar.activation(m.gate_rows[:, q, j * S:(j + 1) * S], bank, ACT.Copy).then_inc(emptied(m, f"l3fg{n}"), 1)
    with act.Fori(0, NPAIR // 2) as i:
        pair_attend_scalar(nc, act, m, "l3fj", i, m.steps0["l3f"], False, lambda act, s: None)
    copy_out_scalar(nc, act, m, "l3fy", m.y_t)
    turn_scalar(nc, act, m, "l3fm")
    h0 = m.h0["l3f"]
    for k in range(2 * F3 // P):
        c = k // 2
        act.wait_ge(m.hidden_ready, h0 + k + 1)
        if k >= 4:
            act.wait_ge(m.hidden_used, h0 + k - 3)
        nc.scalar.activation(m.hidden[:, k % 4, :], m.ps[k % 4], ACT.Relu, bias=w["b1"][:, c:c + 1]).then_inc(
            m.hidden_read, 1)
    copy_out_scalar(nc, act, m, "l3fu", m.y_t)


def l3_ffn_vector(nc, dve, m):
    w, d = m.w["l3f"], m.dve
    tt, ts, reduce = nc.vector.tensor_tensor, nc.vector.tensor_scalar, nc.vector.tensor_reduce
    dve.wait_ge(m.loaded["l3f"], 16)
    norm_to_turn(nc, dve, m, m.x)
    for n in range(4):
        bank = read(m, dve, f"l3fs{n}")
        ts(m.pick[:, n * S:(n + 1) * S], bank, FAR, None, ALU.max).then_inc(emptied(m, f"l3fs{n}"), 1)
        copied(m, dve, f"l3fs{n}")
        nc.vector.engine_nop().then_inc(m.pick_ready, 1)
    dve.wait_ge(m.pick_exp, 4)
    s, tmp, first = m.pick, m.pick_tmp, m.pick_first
    experts = lambda ap: ap.rearrange("p (h e) -> p h e", e=E3)
    spread = lambda ap: ap.rearrange("p (h o) -> p h o", o=1).broadcast_to([P, NT * 2 * H, E3])
    best = m.pick_best
    d.done(ts(s, s, 1.0, None, ALU.add))
    d.done(nc.vector.reciprocal(s, s))

    def choose(values):
        falling = w["falling"].rearrange("p (o e) -> p o e", o=1).broadcast_to([P, NT * 2 * H, E3])
        d.done(reduce(best, experts(values), AX.X, ALU.max))
        d.done(tt(experts(tmp), experts(values), spread(best), ALU.is_equal))
        d.done(tt(experts(tmp), experts(tmp), falling, ALU.mult))
        d.done(reduce(best, experts(tmp), AX.X, ALU.max))
        d.done(tt(experts(tmp), experts(tmp), spread(best), ALU.is_equal))

    choose(s)
    d.done(tt(first, s, tmp, ALU.mult))
    d.done(tt(s, s, first, ALU.subtract))
    choose(s)
    d.done(tt(s, s, tmp, ALU.mult))
    d.done(tt(s, s, first, ALU.add))
    gates = s.rearrange("p (t w g) -> p t w g", w=2, g=P)
    out_gates = gates[:, :, 1, :].rearrange("p t (q g) -> p t q g", q=GROUPS3)
    part = lambda c: m.gate_parts[:, :, :, c, :]
    rest = tmp[:, 0:T].rearrange("p (t q g) -> p t q g", t=NT, q=GROUPS3)
    dve.wait_ge(m.parts_zero, 1)
    d.done(nc.vector.tensor_copy(part(0), out_gates))
    d.done(tt(rest, out_gates, part(0), ALU.subtract))
    d.done(nc.vector.tensor_copy(part(1), rest))
    tt(part(2), rest, part(1), ALU.subtract).then_inc(m.parts_ready, 1)
    dve.wait_ge(m.parts_ready, 1)

    mixed = tmp.rearrange("p (n s) -> p n s", s=S)
    with dve.Fori(0, NPAIR // 2) as i:
        def gather(n):
            s, k = divmod(n, MIXES)
            t, h = divmod(k, 2)
            dve.wait_ge(m.mixed_taken, 2 * MIXES * i + n + 1)
            to = m.wide[:, bass.ds(2 * i + s, 1), t * P + 64 * h:t * P + 64 * h + 64].rearrange("p o d -> p (o d)")
            reduce(to, mixed[:, n % 2, :].rearrange("p (e d) -> p d e", e=E3), AX.X, ALU.add).then_inc(m.mixed_gated, 1)

        for n in range(2 * MIXES):
            s, k = divmod(n, MIXES)
            t, h = divmod(k, 2)
            dve.wait_ge(m.mixed_ready, 2 * MIXES * i + n + 1)
            if n >= 2:
                dve.wait_ge(m.mixed_gated, 2 * MIXES * i + n - 1)
            gate = gates[:, t, 0, bass.ds((2 * (2 * i + s) + h) * E3, E3)]
            tt(mixed[:, n % 2, :].rearrange("p (e d) -> p e d", e=E3), m.ps[n % 4].rearrange("p (e d) -> p e d", e=E3),
               gate.rearrange("p (e o) -> p e o", o=1).broadcast_to([P, E3, 64]), ALU.mult).then_inc(m.mixed_taken, 1)
            if n > 0:
                gather(n - 1)
        gather(2 * MIXES - 1)
        dve.wait_ge(m.mixed_gated, 2 * MIXES * (i + 1))
    dve.wait_ge(m.pair_zero, 2)

    def rope(dve, i, s):
        for what in range(2):
            tables = (w["cos_q"], w["sin_q"]) if what == 0 else (w["cos"], w["sin"])
            added = 12 * i + 6 * s
            for r in range(2):
                for j in range(2):
                    bank = read(m, dve, f"l3fj{j}", PAIR3.uses * i + PAIR3.first[6 + j, s] + 2 * what + r)
                    tt(m.rope_tmp[:, j, r, :], bank, tables[r], ALU.mult).then_inc(emptied(m, f"l3fj{j}"), 1)
            for j in range(2):
                copied(m, dve, f"l3fj{j}", PAIR3.uses * i + PAIR3.first[6 + j, s] + 2 * what + 1)
                at = slice(j * S, (j + 1) * S)
                if what == 0:
                    tt(m.pair_q[s][:, at], m.rope_tmp[:, j, 0, :], m.rope_tmp[:, j, 1, :], ALU.add).then_inc(m.rope_added, 1)
                else:
                    for e in range(2):
                        own = slice(64 * e, 64 * e + 64)
                        tt(m.pair_k[own, s, e, at], m.rope_tmp[own, j, 0, :], m.rope_tmp[own, j, 1, :],
                           ALU.add).then_inc(m.rope_added, 1)
            dve.wait_ge(m.rope_added, added + (2 if what == 0 else 6))

    with dve.Fori(0, NPAIR // 2) as i:
        pair_attend_vector(nc, dve, m, "l3fj", i, m.steps0["l3f"], False, lambda dve, s: rope(dve, i, s))
    with dve.Fori(0, NPAIR // 2) as i:
        for k in range(2 * SPREADS):
            s, b = k // SPREADS, k % 2
            dve.wait_ge(m.spread_ready, 2 * SPREADS * i + k + 1)
            out = m.wide[:, bass.ds(2 * i + s, 1), b * S:(b + 1) * S].rearrange("p o n -> p (o n)")
            tt(m.gated[:, k % 4, :], m.ps[k % 4], out, ALU.mult).then_inc(m.spread_gated, 1)
    add_to(nc, dve, m, "l3fz", m.xn)
    affine_norm(nc, dve, m, w["ln1_g"], w["ln1_b"]).then_inc(m.xn_ready, 1)
    m.turns_dve += 1
    dve.wait_ge(m.xn_ready, m.turns_dve)
    d.done(tt(m.q_tok, m.xn[:, :, :], over_tiles(w["b2"]), ALU.add))
    for j in range(2):
        read(m, dve, f"l3fm{j}")
    d.done(nc.vector.tensor_copy(m.xn[:, :, :], m.q_tok))
    add_to(nc, dve, m, "l3fw", m.xn)
    d.done(affine_norm(nc, dve, m, w["ln2_g"], w["ln2_b"]))
    d.done(tt(m.x[:, :, :], m.x[:, :, :], m.xn[:, :, :], ALU.add))


def affine_norm(nc, dve, m, gain, offset):
    m.dve.done(norm_vector(nc, dve, m, m.xn, m.xn))
    m.dve.done(nc.vector.tensor_tensor(m.xn[:, :, :], m.xn[:, :, :], over_tiles(gain), ALU.mult))
    return nc.vector.tensor_tensor(m.xn[:, :, :], m.xn[:, :, :], over_tiles(offset), ALU.add)


def l3_ffn_gpsimd(nc, pool, m):
    pool.wait_ge(m.stage_done, 11)
    nc.gpsimd.memset(m.gate_parts[:, :, :, :, :], 0.0).then_inc(m.parts_zero, 1)
    nc.gpsimd.memset(m.pair_k[:, :, :, :], 0.0).then_inc(m.pair_zero, 1)
    for _ in range(3):
        norm_gpsimd(nc, pool, m)



def plan(m):
    m.pv0 = 4 * NPAIR
    m.values0 = {}

    def pair(name):
        item(m, f"{name}0", 6)
        item(m, f"{name}1", 7)

    def narrow(stage, values):
        m.values0[stage] = values
        for name, times in (("k", 1), ("v", 1), ("n", 2), ("q", 2), ("o", 2)):
            run(stage + name, times)
        if stage == "l2x":
            run("l2xg", 1)
            run("l2xh", 1)
        run(stage + "y", 2)

    def run(name, times):
        for n in range(times):
            item(m, f"{name}{n}", 6 + n % 2)

    for name in ("l0n", "l0q", "l0k", "l0v", "l0o", "l0y"):
        pair(name)
    for name, times in (("l0xk", NPAIR), ("l0xv", 2 * B), ("l0xn", 2), ("l0xq", 2 * NPAIR), ("l0xo", 2 * NPAIR),
                        ("l0xy", 2), ("l0xz", 2)):
        run(name, times)
    run("l0fn", 2)
    item(m, "l0fr", 6)
    item(m, "l0fg0", 7)
    item(m, "l0fg1", 6)
    run("l0fy", 2)
    run("l0fz", 2)
    run("l1an", 2)
    run("l1al", 2)
    item(m, "l1aj0", 6, PAIR1.uses * NPAIR // 2)
    item(m, "l1aj1", 7, PAIR1.uses * NPAIR // 2)
    run("l1ay", 2)
    run("l1az", 2)
    for name, times in (("l1xc", 1), ("l1xd", 2), ("l1xn", 2), ("l1xq", 2), ("l1xk", 2), ("l1xv", 2), ("l1xqt", 2),
                        ("l1xkt", 2), ("l1xct", 1), ("l1xo", 2), ("l1xy", 2)):
        run(name, times)
    run("l1fn", 2)
    run("l1fy", 2)
    run("l1fz", 2)
    for name in ("n", "q", "k", "v", "o", "y"):
        run(f"l2a{name}", 2)
    narrow("l2x", 0)
    for name, times in (("l2fn", 2), ("l2fr", 2), ("l2fl", 1), ("l2fp", 1), ("l2fx", 2), ("l2fw", 2 * NT), ("l2fy", 2),
                        ("l2fz", 2)):
        run(name, times)
    run("l3an", 2)
    run("l3ap", NT)
    run("l3am", 2)
    run("l3ay", 2)
    narrow("l3x", 2)
    run("l3fn", 2)
    run("l3fs", 4)
    run("l3fg", 2 * GROUPS3)
    item(m, "l3fj0", 6, PAIR3.uses * NPAIR // 2)
    item(m, "l3fj1", 7, PAIR3.uses * NPAIR // 2)
    for name in ("y", "z", "m", "u", "w"):
        run(f"l3f{name}", 2)
    m.slot0 = {"l0f": 0, "l1a": E0 // 2, "l2f": E0 // 2 + NPAIR // 2}
    at = m.slot0["l2f"] + E2 // 2
    for name in ("l3v", "l3q", "l3o"):
        m.slot0[name] = at
        at += NPAIR // 2
    m.h0 = {"l0f": 0, "l3f": 8 * E0}
    m.steps0, m.half0, m.cross0 = {}, {}, {}
    own = cross = 0
    for stage, kind, steps in (("l0a", "self", 8 * STEPS), ("l0x", "cross", XSTEPS), ("l1a", "self", 8 * STEPS),
                               ("l1x", "cross", XSTEPS), ("l2a", "self", B * NQ), ("l2x", "cross", XSTEPS),
                               ("l3x", "cross", XSTEPS), ("l3f", "self", 8 * STEPS)):
        m.steps0[stage], m.half0[stage], m.cross0[stage] = own + cross, own // 2, cross
        if kind == "self":
            own += steps
        else:
            cross += steps
def build(nc, shapes, dram, out):
    m = Core()
    with ExitStack() as ctx:
        def sb(name, shape, dt=F32):
            return ctx.enter_context(nc.sbuf_tensor(name, shape, dt))

        def sem(name):
            return ctx.enter_context(nc.semaphore(name))

        m.psum = ctx.enter_context(nc.psum_tensor("psum", [P, 8, S], F32))
        m.ps = [m.psum[:, b, :] for b in range(8)]
        m.x = sb("x", [P, NT, P])
        m.xn = sb("xn", [P, NT, P])
        m.xn_t = sb("xn_t", [P, T])
        m.q_t = sb("q_t", [P, T])
        m.k_t = sb("k_t", [P, T])
        m.v = sb("v", [P, NT, P])
        m.o_t = sb("o_t", [P, T])
        m.y_t = m.o_t
        heads = sb("heads", [P, 4, T])
        m.head_qs = heads[:, 0:2, :]
        m.head_vals = heads[:, 2:4, :].rearrange("p n (t d) -> p n t d", d=P)
        m.wide = sb("wide", [P, NPAIR, T])
        m.p = sb("p", [P, 4, S])
        m.xp = m.p[:, :, :].rearrange("p (n a) s -> p n (a s)", a=2)
        m.pt = sb("pt", [P, 4, NQ, S])
        m.xpt = m.pt[:, :, :, :].rearrange("p (n a) h s -> p n (a h) s", a=2)
        m.keys_own = sb("keys_own", [P, B, H * (SC + 1)])
        m.context_t = sb("context_t", [P, B * SC])
        m.context_v = sb("context_v", [P, B, H * 64])
        m.mask_words = sb("mask_words", [1, 2 * B * SC // 4], I32)
        m.mask_u8 = m.mask_words[:, :].bitcast(U8)
        m.mask_low = sb("mask_low", [1, 2 * B * SC])
        m.mask_row = sb("mask_row", [1, B, 4 * (SC + 1)], BF16)
        m.ones_bf = sb("ones_bf", [1, P], BF16)
        m.pair_q = [m.q_t, m.k_t]
        m.pair_k = heads[:, :, :].rearrange("p (s e) n -> p s e n", e=2)
        m.pair_v = [m.v, m.o_t[:, :].rearrange("p (t d) -> p t d", d=P)]
        m.latent_t = m.keys_own[:, 0, 0:T]
        m.slots_all = sb("slots", [P, 2 * SLOT_W])
        m.slots = m.slots_all[:, :].rearrange("p (s n) -> p s n", s=2)
        m.context = sb("context", [SC, B, DC])
        m.context_norm_t = sb("context_norm_t", [P, B * SC])
        m.context_kv = m.context_v[:, :, 0:2 * P]
        tiles = lambda ap: ap.rearrange("p (t d) -> p t d", d=P)
        m.q_tok, m.k_tok, m.squares = (tiles(m.wide[:, n, :]) for n in range(3))
        m.tail_pt = m.wide[:, 4:8, 0:S]
        m.ints = m.slots_all[:, 0:3 * F1].bitcast(I32)
        m.cast_w = m.keys_own[:, 0, 0:3 * F1]
        m.context_k = m.context_norm_t
        m.values_own = heads[:, :, :].rearrange("p (b n) (h d) -> p b (n h) d", b=B, d=P)
        m.numbers = sb("numbers", [P, 8 * XSTEPS])
        m.number = sb("number", [P, 3])
        m.average = sb("average", [P, B])
        m.share = sb("share", [P, 1])
        m.ones_row = sb("ones_row", [1, P])
        m.logits, m.left, m.places, m.running = m.q_t, m.k_t, m.o_t, heads[:, 0, :]
        m.probs16 = sb("probs16", [P, NT, E2])
        m.place = sb("place", [P, NT, E2])
        m.top8 = sb("top8", [P, 2, 8])
        m.needed = sb("needed", [P, 2])
        m.ones_col = sb("ones_col", [P, 1])
        m.chosen_t = m.xn_t
        m.weighted = m.pt[:, :, :, :].rearrange("p n (a b) s -> p (n a) (b s)", b=2)
        m.expert_h = sb("expert_h", [P, 2, F2 // P * CAP])
        m.rms = sb("rms", [P, 4 * NT + 2 * B])
        m.low_row = sb("low_row", [1, B * SC], BF16)
        m.hidden = m.p
        columns = {"q": 64, "gate": 64, "v": P, "g": P, "decay": 64, "k": 64, "qk": 64, "aug": P, "sig_g": P, "o": P}
        m.gla, at = {"tmp": m.v[:, :, :]}, 0
        for name, n in columns.items():
            m.gla[name] = m.wide[:, :, at:at + n]
            at += n
        m.select = sb("select", [P, 16, P], BF16)
        m.pick = m.p[:, :, :].rearrange("p a s -> p (a s)")
        flat = m.pt[:, :, :, :].rearrange("p a b s -> p (a b s)")
        m.pick_tmp, m.pick_first = flat[:, 2048:4096], flat[:, 4096:6144]
        m.pick_best = flat[:, 6144:6400]
        m.gate_parts = flat[:, 0:2048].bitcast(BF16).rearrange("p (t q c g) -> p t q c g", q=GROUPS3, c=4, g=32)
        m.gated = flat[:, 0:2048].rearrange("p (n s) -> p n s", s=S)
        m.gate_rows = m.keys_own[:, :, :].rearrange("p a b -> p (a b)")[:, 0:2048].bitcast(BF16).rearrange(
            "p (q n) -> p q n", q=GROUPS3)
        m.rope_tmp = m.context_v[:, :, :].rearrange("p s (r n) -> p s r n", n=S)
        m.gates = sb("gates", [P, NT, E0])
        m.gate_t = m.q_t
        m.pairs = m.pt[:, 0:2, 0, :].rearrange("p n (t e j) -> p n t e j", e=E0, j=E0)
        m.keep = sb("keep", [P, 2, NT, E0])
        m.per_token = sb("per_token", [P, 4, NT])
        m.xmax = sb("xmax", [P, 2, 8])
        m.xsum = sb("xsum", [P, 8 * XSTEPS])
        m.xrsum = sb("xrsum", [P, 2, 8])
        m.negmax = sb("negmax", [P, 4])
        m.sum = sb("sum", [P, 4])
        m.rsum = sb("rsum", [P, 4])
        m.stats = sb("stats", [P, NT, nc.vector.BN_STATS_DIM])
        m.moments = sb("moments", [P, NT, 2])
        m.var = sb("var", [P, NT])
        m.rstd = sb("rstd", [P, NT])
        m.minus_half = sb("minus_half", [P, NT])
        m.zeros = sb("zeros", [P, P])
        m.ident = sb("ident", [P, P])
        m.ident_bf = sb("ident_bf", [P, P], BF16)
        m.future_bf = sb("future", [P, P], BF16)
        m.rows8 = sb("rows8", [P, H + 1])
        m.cols8 = sb("cols8", [P, H + 1, P])
        m.weights, m.w, m.loaded = {}, {}, {}
        widths = [sum(n for _, n in parts) for parts in shapes.values()]
        arenas = [sb(f"weights{n}", [P, max(widths[n::2], default=1)]) for n in range(2)]
        for stage, parts in shapes.items():
            width = sum(n for _, n in parts)
            m.weights[stage] = arenas[len(m.weights) % 2][:, 0:width]
            m.loaded[stage] = sem(f"loaded_{stage}")
            at, m.w[stage] = 0, {}
            for name, n in parts:
                m.w[stage][name] = m.weights[stage][:, at:at + n]
                at += n
        m.consts = [("ident", m.ident[:, :]), ("future", m.wide[:, 2, 0:P]),
                    ("rows8", m.rows8[:, :]), ("cols8", m.cols8[:, :, :]), ("zeros", m.zeros[:, :]),
                    ("share", m.share[:, :]), ("ones_col", m.ones_col[:, :]), ("select", m.wide[:, 0:2, :].rearrange("p a (e o) -> p (a e) o", o=P)), ("ones_row", m.ones_row[:, :]), ("minus_half", m.minus_half[:, :])]
        m.n_consts = len(m.consts)
        m.filled = {b: sem(f"filled{b}") for b in (6, 7)}
        m.emptied = {b: sem(f"emptied{b}") for b in (6, 7)}
        m.conv_done = sem("conv_done")
        m.gla_ready = sem("gla_ready")
        m.gla_exp = sem("gla_exp")
        m.head_var_ready = sem("head_var_ready")
        m.head_rstd_ready = sem("head_rstd_ready")
        m.pick_exp = sem("pick_exp")
        m.pick_ready = sem("pick_ready")
        m.parts_zero = sem("parts_zero")
        m.parts_ready = sem("parts_ready")
        m.mixed_ready = sem("mixed_ready")
        m.mixed_taken = sem("mixed_taken")
        m.mixed_gated = sem("mixed_gated")
        m.rope_added = sem("rope_added")
        m.spread_ready = sem("spread_ready")
        m.spread_gated = sem("spread_gated")
        m.spread_used = sem("spread_used")
        m.x_in = sem("x_in")
        m.consts_in = sem("consts_in")
        m.out_done = sem("out_done")
        m.var_ready = sem("var_ready")
        m.rstd_ready = sem("rstd_ready")
        m.consts_cast = sem("consts_cast")
        m.xn_ready = sem("xn_ready")
        m.scores_ready = sem("scores_ready")
        m.negmax_ready = sem("negmax_ready")
        m.exp_done = sem("exp_done")
        m.rsum_ready = sem("rsum_ready")
        m.probs_ready = sem("probs_ready")
        m.turned_ready = sem("turned_ready")
        m.pv_done = sem("pv_done")
        m.head_q = sem("head_q")
        m.head_v = sem("head_v")
        m.cross_taken = sem("cross_taken")
        m.keys_zero = sem("keys_zero")
        m.cross_ready = sem("cross_ready")
        m.context_in = sem("context_in")
        m.stage_done = sem("stage_done")
        m.gates_out = sem("gates_out")
        m.places_ready = sem("places_ready")
        m.chosen_ready = sem("chosen_ready")
        m.weighted_ready = sem("weighted_ready")
        m.expert_hidden = sem("expert_hidden")
        m.expert_biased = sem("expert_biased")
        m.expert_gelu = sem("expert_gelu")
        m.expert_y_ready = sem("expert_y_ready")
        m.expert_taken = sem("expert_taken")
        m.ints_in = sem("ints_in")
        m.ints_cast = sem("ints_cast")
        m.swiglu_ready = sem("swiglu_ready")
        m.swiglu_exp = sem("swiglu_exp")
        m.swiglu_done = sem("swiglu_done")
        m.swiglu_added = sem("swiglu_added")
        m.narrow_keys = sem("narrow_keys")
        m.narrow_values = sem("narrow_values")
        m.sums_are_numbers = sem("sums_are_numbers")
        m.context_normed = sem("context_normed")
        m.low_row_ready = sem("low_row_ready")
        m.rms_ready = sem("rms_ready")
        m.rms_inverted = sem("rms_inverted")
        m.rms_done = sem("rms_done")
        m.tail_taken = sem("tail_taken")
        m.pair_zero = sem("pair_zero")
        m.gates_in = sem("gates_in")
        m.gates_ready = sem("gates_ready")
        m.router_less_max = sem("router_less_max")
        m.router_exp = sem("router_exp")
        m.hidden_ready = sem("hidden_ready")
        m.hidden_read = sem("hidden_read")
        m.hidden_gated = sem("hidden_gated")
        m.hidden_used = sem("hidden_used")
        m.turned_taken = [sem("turned_taken0"), sem("turned_taken1")]
        m.values_in = [sem("values_in0"), sem("values_in1")]
        m.slot_in = [sem("slot_in0"), sem("slot_in1")]
        plan(m)
        block = ctx.enter_context(nc.Block())

        @block.sync
        def _(sp):
            sp.dma_start(m.x[:, :, :], dram["x"]).then_inc(m.x_in, 16)
            for name, dst in m.consts:
                sp.dma_start(dst, dram[name]).then_inc(m.consts_in, 16)
            sp.dma_start(m.context_t[0:DC, :], dram["context_t"]).then_inc(m.context_in, 16)
            sp.dma_start(m.context[:, :, :], dram["context"]).then_inc(m.context_in, 16)
            sp.dma_start(m.mask_words[:, :], dram["masks"]).then_inc(m.context_in, 16)
            for b in range(B):
                sp.dma_start(m.context_v[SC:SC + 1, b, :], dram["null_v"]).then_inc(m.context_in, 16)
            stages = [stage[0] for stage in STAGES]
            for n in range(2):
                sp.dma_start(m.weights[stages[n]], dram[f"w_{stages[n]}"]).then_inc(m.loaded[stages[n]], 16)
            for n, stage in enumerate(STAGES):
                if 0 < n < len(stages) - 1:
                    sp.wait_ge(m.stage_done, n)
                    sp.dma_start(m.weights[stages[n + 1]], dram[f"w_{stages[n + 1]}"]).then_inc(
                        m.loaded[stages[n + 1]], 16)
                if stage[5]:
                    stage[5](nc, sp, m, dram)
            sp.wait_ge(m.stage_done, len(STAGES))
            sp.dma_start(out, m.x[:, :, :]).then_inc(m.out_done, 16)
            sp.wait_ge(m.out_done, 16)

        @block.gpsimd
        def _(pool):
            pool.wait_ge(m.consts_in, 16 * m.n_consts)
            nc.gpsimd.memset(m.mask_row[:, :, :], 0.0)
            nc.gpsimd.memset(m.ones_bf[:, :], 1.0)
            nc.gpsimd.memset(m.keys_own[:, :, :], 0.0).then_inc(m.keys_zero, 1)
            for stage in STAGES:
                stage[4](nc, pool, m)

        @block.scalar
        def _(act):
            act.wait_ge(m.consts_in, 16 * m.n_consts)
            nc.scalar.activation(m.ident_bf[:, :], m.ident[:, :], ACT.Copy).then_inc(m.consts_cast, 1)
            nc.scalar.activation(m.future_bf[:, :], m.wide[:, 2, 0:P], ACT.Copy).then_inc(m.consts_cast, 1)
            nc.scalar.activation(m.select[:, :, :], m.wide[:, 0:2, :].rearrange("p a (e o) -> p (a e) o", o=P),
                                 ACT.Copy).then_inc(m.consts_cast, 1)
            for stage in STAGES:
                stage[2](nc, act, m)

        @block.vector
        def _(dve):
            m.dve = Chain(dve, ctx.enter_context(nc.semaphore("vector_chain")))
            dve.wait_ge(m.consts_in, 16 * m.n_consts)
            for stage in STAGES:
                stage[3](nc, dve, m)
                dve.sem_inc(m.stage_done, 1)

        @block.tensor
        def _(pe):
            for stage in STAGES:
                stage[1](nc, pe, m)


STAGES = [
    ("l0a", l0_attn_tensor, l0_attn_scalar, l0_attn_vector, l0_attn_gpsimd, None),
    ("l0x", l0_cross_tensor, l0_cross_scalar, l0_cross_vector, l0_cross_gpsimd, None),
    ("l0f", l0_ffn_tensor, l0_ffn_scalar, l0_ffn_vector, l0_ffn_gpsimd, l0_ffn_sync),
    ("l1a", l1_attn_tensor, l1_attn_scalar, l1_attn_vector, l1_attn_gpsimd, l1_attn_sync),
    ("l1x", l1_cross_tensor, l1_cross_scalar, l1_cross_vector, l1_cross_gpsimd, None),
    ("l1f", l1_ffn_tensor, l1_ffn_scalar, l1_ffn_vector, one_norm_gpsimd, l1_ffn_sync),
    ("l2a", l2_attn_tensor, l2_attn_scalar, l2_attn_vector, one_norm_gpsimd, None),
    narrow_cross("l2x", clip=10000.0),
    ("l2f", l2_ffn_tensor, l2_ffn_scalar, l2_ffn_vector, l2_ffn_gpsimd, l2_ffn_sync),
    ("l3a", l3_attn_tensor, l3_attn_scalar, l3_attn_vector, l3_attn_gpsimd, None),
    narrow_cross("l3x"),
    ("l3f", l3_ffn_tensor, l3_ffn_scalar, l3_ffn_vector, l3_ffn_gpsimd, l3_ffn_sync),
]



def rows(a):
    out = np.zeros((P, a.shape[1]), a.dtype)
    out[:a.shape[0]] = a
    return out


def column(a):
    return a.reshape(-1, 1)


def every(a):
    return np.tile(a.reshape(1, -1), (P, 1))


def layout(v):
    w = v["L0_attn_c_attn_kernel"]
    bias = v["L0_attn_c_attn_bias"]
    packs = {
        "l0a": [("wq", w[0:P].T), ("wk", w[P:2 * P].T), ("wv", w[2 * P:].T),
                ("wo", v["L0_attn_c_proj_kernel"].T), ("bq", column(bias[0:P])), ("bk", column(bias[P:2 * P])),
                ("bv", every(bias[2 * P:])), ("bo", every(v["L0_attn_c_proj_bias"]))],
        "l0x": [("wq", v["L0_xattn_Wq"]), ("wk", v["L0_xattn_Wkv"][:, 0:H * 64]), ("wv", v["L0_xattn_Wkv"][:, H * 64:]),
                ("wo", v["L0_xattn_Wout"].reshape(NPAIR, P, P).transpose(1, 0, 2).reshape(P, NPAIR * P)),
                ("g_norm", column(v["L0_xattn_g_norm"])), ("g_out", every(v["L0_xattn_g_out"])),
                ("null_k", column(np.tile(v["L0_xattn_null_kv"][0], 2)))],
        "l0f": [("wr", v["L0_ffn_Wr"]), ("br", every(v["L0_ffn_br"])), ("b2", v["L0_ffn_b2"]),
                ("not_after", every(np.tril(np.ones((E0, E0), np.float32))))],
        "l1a": [("down", v["L1_attn_Wkv_down"]),
                ("wo", v["L1_attn_Wout"].reshape(NPAIR, P, P).transpose(1, 0, 2).reshape(P, NPAIR * P))],
    }
    packs["l1x"] = [
        ("wq", v["L1_xattn_Wq"].T), ("wkv", v["L1_xattn_Wkv"].T), ("wlk", v["L1_xattn_Wlkv"][0:P].T),
        ("wlv", v["L1_xattn_Wlkv"][P:].T), ("wo", v["L1_xattn_Wo"].T), ("ln_l_g", column(v["L1_xattn_ln_l_g"])),
        ("ln_l_b", column(v["L1_xattn_ln_l_b"])), ("ln_x_g", every(v["L1_xattn_ln_x_g"])),
        ("ln_x_b", every(v["L1_xattn_ln_x_b"])), ("qn_g", column(np.tile(v["L1_xattn_qn_g"], 2))),
        ("kn_g", column(np.tile(v["L1_xattn_kn_g"], 2))), ("bo", every(v["L1_xattn_bo"]))]
    w = v["L2_attn_w_qkv"]
    packs["l1f"] = [("none", np.zeros((P, 1), np.float32))]
    packs["l2a"] = [("wq", w[0:P].T), ("wk", w[P:2 * P].T), ("wv", w[2 * P:].T), ("wo", v["L2_attn_w_proj"].T),
                    ("bo", every(v["L2_attn_b_proj"]))]
    packs["l2x"] = [("wq", v["L2_xattn_Wq"]), ("wk", v["L2_xattn_Wk"]), ("wv", v["L2_xattn_Wv"]), ("wo", v["L2_xattn_Wo"]),
                    ("bq", column(v["L2_xattn_bq"])), ("bk", column(v["L2_xattn_bk"])), ("bv", every(v["L2_xattn_bv"])),
                    ("bo", every(v["L2_xattn_bo"]))]
    packs["l2f"] = [("router", v["L2_ffn_router_weight"].T), ("router_b", column(v["L2_ffn_router_bias"])),
                    ("norm_w", every(v["L2_ffn_norm_weight"])),
                    ("one_to_cap", every(np.arange(1, CAP + 1, dtype=np.float32)))]
    split = lambda g: np.concatenate(g, axis=1)
    packs["l3a"] = [("wqkvg", split([v["L3_attn_Wq"], v["L3_attn_Wkg"], v["L3_attn_Wv"], v["L3_attn_Wg"]])),
                    ("wo", v["L3_attn_Wout"]), ("bg", every(v["L3_attn_bg"])),
                    ("aug_balance", every(v["L3_attn_aug_balance"])), ("conv", v["L3_attn_conv_w"])]
    packs["l3x"] = [("wq", v["L3_xattn_w_q"]), ("wk", v["L3_xattn_w_k"]), ("wv", v["L3_xattn_w_v"]),
                    ("wo", v["L3_xattn_w_o"]), ("bq", column(v["L3_xattn_b_q"])), ("bk", column(v["L3_xattn_b_k"])),
                    ("bv", every(v["L3_xattn_b_v"])), ("bo", every(v["L3_xattn_b_o"]))]
    cos, sin = rope_tables()
    packs["l3f"] = [("wsel", split([v["L3_ffn_Wsel_v"].reshape(P, P).T, v["L3_ffn_Wsel_o"].reshape(P, P).T])),
                    ("w1", v["L3_ffn_W1"]), ("w2", v["L3_ffn_W2"].reshape(F3 // P, P, P).transpose(1, 0, 2).reshape(P, F3)),
                    ("b1", v["L3_ffn_b1"].reshape(F3 // P, P).T), ("falling", every(np.arange(E3, 0, -1, dtype=np.float32))),
                    ("cos", cos), ("sin", sin), ("cos_q", cos * np.float32(64 ** -0.5)), ("sin_q", sin * np.float32(64 ** -0.5))]
    packs["l3f"] += [(name, every(v["L3_ffn_" + name])) for name in ("ln1_g", "ln1_b", "ln2_g", "ln2_b", "b2")]
    return packs


def rope_tables():
    inverse = (10000.0 ** (-np.arange(ROT // 2) / (ROT // 2))).astype(np.float32)
    angle = np.arange(S, dtype=np.float32)[None, :] * inverse[:, None]
    head_cos, head_sin = np.ones((64, S), np.float32), np.zeros((64, S), np.float32)
    head_cos[0:ROT // 2], head_cos[ROT // 2:ROT] = np.cos(angle), np.cos(angle)
    head_sin[0:ROT // 2], head_sin[ROT // 2:ROT] = -np.sin(angle), np.sin(angle)
    return np.tile(head_cos, (2, 1)), np.tile(head_sin, (2, 1))


def turned_features(w):
    partner = np.arange(64)
    partner[0:ROT] = np.roll(partner[0:ROT], ROT // 2)
    return w.reshape(P, H, 64)[:, :, partner].reshape(P, H * 64)


def streams(v):
    return {
        "l0f": np.concatenate([v["L0_ffn_W1"], v["L0_ffn_W2"].reshape(E0, 4, P, P).transpose(0, 2, 1, 3).reshape(E0, P, F0),
                               v["L0_ffn_b1"].reshape(E0, 4, P).transpose(0, 2, 1)], axis=2),
        "l2f": np.concatenate([v["L2_ffn_fc1_weight"].transpose(0, 2, 1),
                               v["L2_ffn_fc2_weight"].reshape(E2, P, F2 // P, P).transpose(0, 3, 2, 1).reshape(E2, P, F2),
                               v["L2_ffn_fc1_bias"].reshape(E2, F2 // P, P).transpose(0, 2, 1),
                               np.broadcast_to(v["L2_ffn_fc2_bias"][:, None, :], (E2, P, P))], axis=2),
        "l1a": np.concatenate([by_pair(v["L1_attn_Wq"].reshape(P, H * 64)),
                               by_pair(rows(v["L1_attn_Wk_up"].reshape(LATENT, H * 64))),
                               by_pair(rows(v["L1_attn_Wv_up"].reshape(LATENT, H * 64)))], axis=2),
        "l3v": v["L3_ffn_Wv"].reshape(NPAIR, 2, E3, P, 64).transpose(0, 3, 1, 2, 4).reshape(NPAIR, P, 2 * E3 * 64),
        "l3q": np.concatenate([by_pair(turn(v[name].transpose(1, 0, 2).reshape(P, H * 64)))
                               for name in ("L3_ffn_Wq", "L3_ffn_Wk") for turn in (lambda w: w, turned_features)], axis=2),
        "l3o": v["L3_ffn_Wo"].reshape(NPAIR, 2, E3, 64, P).transpose(0, 1, 3, 2, 4).reshape(NPAIR, P, E3 * P),
    }


def by_pair(w):
    return w.reshape(P, NPAIR, P).transpose(1, 0, 2)


def constants():
    head = np.arange(P) // (P // H)
    own = (head[:, None] == np.arange(H + 1)[None, :]).astype(np.float32)
    select = np.zeros((4, 32, 2, E3, 2, 64), np.float32)
    for pair in range(2):
        for h in range(2):
            for e in range(E3):
                select[0:3, (2 * pair + h) * E3 + e, pair, e, h, :] = 1
    return {
        "select": select.reshape(P, 16, P),
        "ident": np.eye(P, dtype=np.float32),
        "future": np.where(np.arange(P)[None, :] > np.arange(P)[:, None], np.float32(-BIG), np.float32(0)),
        "rows8": own * np.float32((P // H) ** -0.5),
        "cols8": np.ascontiguousarray(np.broadcast_to(own.T[None], (P, H + 1, P))),
        "zeros": np.zeros((P, P), np.float32),
        "ones_col": np.ones((P, 1), np.float32),
        "share": np.full((P, 1), 1.0 / SC, np.float32),
        "ones_row": np.ones((1, P), np.float32),
        "minus_half": np.full((P, NT), -0.5, np.float32),
    }


def kernel(**inputs):
    import concourse.bacc as bacc
    from concourse.bass_utils import run_bass_kernel_spmd

    v = {name: np.asarray(a) for name, a in inputs.items()}
    packs = layout(v)
    arrays = {"x": np.ascontiguousarray(v["x"].reshape(NT, P, P).transpose(1, 0, 2))}
    arrays |= constants()
    arrays["context_t"] = np.ascontiguousarray(v["ctx_768"].transpose(2, 0, 1).reshape(DC, B * SC))
    arrays["context"] = np.ascontiguousarray(v["ctx_768"].transpose(1, 0, 2))
    arrays["ints"] = np.concatenate([v["L1_ffn_w_gate"].T, v["L1_ffn_w_up"].T, v["L1_ffn_w_down"].reshape(P, F1 // P, P)
                                     .transpose(2, 1, 0).reshape(P, F1)], axis=1)
    arrays["masks"] = np.stack([v["mask_BxS2_bf1"], v["mask_BxS2_bk0"]]).reshape(1, -1).view(np.int32)
    arrays["null_v"] = np.tile(v["L0_xattn_null_kv"][1], H).reshape(1, -1)
    for stage, parts in packs.items():
        arrays[f"w_{stage}"] = np.concatenate([rows(a) for _, a in parts], axis=1)
    arrays |= {f"s_{stage}": np.ascontiguousarray(a) for stage, a in streams(v).items()}
    shapes = {stage: [(name, a.shape[1]) for name, a in parts] for stage, parts in packs.items()}

    nc = bacc.Bacc("TRN2", target_bir_lowering=False, num_devices=1)
    dram = {name: nc.dram_tensor(f"in_{name}", a.shape, mybir.dt.from_np(a.dtype), kind="ExternalInput").ap()
            for name, a in arrays.items()}
    dram["scratch_gates"] = nc.dram_tensor("scratch_gates", (E0, T), F32, kind="Internal").ap()
    out = nc.dram_tensor("out", (P, NT, P), F32, kind="ExternalOutput").ap()
    build(nc, shapes, dram, out)
    got = run_bass_kernel_spmd(nc, [{f"in_{name}": a for name, a in arrays.items()}], core_ids=[0])
    return got.results[0]["out"].transpose(1, 0, 2).reshape(B, S, P)
```

```python
from contextlib import ExitStack

import numpy as np

import concourse.bass as bass
import concourse.mybir as mybir
from concourse.alu_op_type import AluOpType as ALU

ACT = mybir.ActivationFunctionType
AX = mybir.AxisListType
F32 = mybir.dt.float32
BF16 = mybir.dt.bfloat16
I32 = mybir.dt.int32
U8 = mybir.dt.uint8
U32 = mybir.dt.uint32

P = 128
B, S = 2, 512
T = B * S
NT = T // P
NQ = S // P
SC, DC = 77, 96
H = 16
BIG = 3.0e38
LAG = 3
VECTOR_TAKES, SCALAR_TAKES = 3, 3
STEPS = 16


class Core:

    def __init__(self):
        self.items = {}
        self.used = {b: 0 for b in range(8)}
        self.norms = self.norms_pool = self.turns_pe = self.turns_dve = 0


class Attention:

    def __init__(self, n0, half0, group, keys, steps=STEPS, causal=False, q=None, k=None, values=None, group_done=None,
                 before_scores=None, after=None, scalar_before=None, vector_before=None):
        self.n0, self.half0 = n0, half0
        self.steps, self.group, self.causal = steps, group, causal
        self.keys = keys
        self.q, self.k, self.values = q, k, values
        self.group_done = group_done
        self.before_scores, self.after = before_scores or {}, after or {}
        self.scalar_before, self.vector_before = scalar_before or {}, vector_before or {}


class Cross:

    def __init__(self, nk, clip=None):
        self.nk, self.clip, self.vector_after = nk, clip, {}


def wait(eng, sem, value):
    if isinstance(value, int) and value <= 0:
        return
    eng.wait_ge(sem, value)


class Chain:

    def __init__(self, eng, sem):
        self.eng, self.sem, self.n = eng, sem, 0

    def done(self, instruction):
        instruction.then_inc(self.sem, 1)
        self.n = self.n + 1
        self.eng.wait_ge(self.sem, self.n)



def item(m, name, bank, times=1):
    m.items[name] = (bank, m.used[bank])
    m.used[bank] += times


def fill(m, pe, name, k=0):
    bank, base = m.items[name]
    wait(pe, m.emptied[bank], base + k)
    return m.ps[bank]


def filled(m, name):
    return m.filled[m.items[name][0]]


def read(m, eng, name, k=0):
    bank, base = m.items[name]
    eng.wait_ge(m.filled[bank], base + k + 1)
    return m.ps[bank]


def emptied(m, name):
    return m.emptied[m.items[name][0]]


def copied(m, eng, name, k=0):
    bank, base = m.items[name]
    eng.wait_ge(m.emptied[bank], base + k + 1)



def norm_vector(nc, dve, m, src, dst, eps=1e-5, half_ready=None):
    for t in range(NT):
        last = nc.vector.bn_stats(m.stats[:, t, :], src[:, t, :])
    m.dve.done(last)
    for t in range(NT):
        last = nc.vector.bn_aggr(m.moments[:, t, :], m.stats[:, t, :])
    m.dve.done(last)
    nc.vector.tensor_scalar(m.var[:, :], m.moments[:, :, 1], float(eps), None, ALU.add).then_inc(m.var_ready, 1)
    m.norms += 1
    dve.wait_ge(m.rstd_ready, m.norms)
    for t in range(NT):
        last = nc.vector.tensor_scalar(dst[:, t, :], src[:, t, :], m.moments[:, t, 0:1], m.rstd[:, t:t + 1],
                                       ALU.subtract, ALU.mult)
        if half_ready and t == NT // 2 - 1:
            last.then_inc(half_ready, 1)
    return last


def norm_to_turn(nc, dve, m, src):
    norm_vector(nc, dve, m, src, m.xn, half_ready=m.xn_ready).then_inc(m.xn_ready, 1)
    m.turns_dve += 2


def norm_gpsimd(nc, pool, m):
    m.norms_pool += 1
    pool.wait_ge(m.var_ready, m.norms_pool)
    nc.gpsimd.tensor_tensor(m.rstd[:, :], m.var[:, :], m.minus_half[:, :], ALU.pow).then_inc(m.rstd_ready, 1)


def turn_tensor(nc, pe, m, name):
    for j in range(2):
        m.turns_pe += 1
        pe.wait_ge(m.xn_ready, m.turns_pe)
        bank = fill(m, pe, f"{name}{j}")
        for t in range(4):
            last = nc.tensor.transpose(bank[:, t * P:(t + 1) * P], m.xn[:, 4 * j + t, :], m.ident[:, :])
        last.then_inc(filled(m, f"{name}{j}"), 1)


def turn_scalar(nc, act, m, name, scale=1.0, bias=0.0):
    for j in range(2):
        bank = read(m, act, f"{name}{j}")
        nc.scalar.activation(m.xn_t[:, j * S:(j + 1) * S], bank[:, :], ACT.Identity, bias=bias,
                             scale=scale).then_inc(emptied(m, f"{name}{j}"), 1)


def turned(m, pe, name):
    for j in range(2):
        copied(m, pe, f"{name}{j}")



def later(before, k):
    return before, k + before.steps if before else k


def attend_tensor(nc, pe, m, a, before=None):
    for k in range(a.steps if a else LAG + NQ):
        if a:
            u, qt = divmod(k, NQ)
            if k in a.before_scores:
                a.before_scores[k](pe)
            wait(pe, m.exp_done, a.n0 + k - 3)
            bank = m.ps[k % 4]
            keys = a.keys(qt)
            last = nc.tensor.matmul(bank[:, 0:keys], a.q(u, qt), a.k(u, keys), start=True, stop=not a.causal)
            if a.causal:
                last = nc.tensor.matmul(bank[:, keys - P:keys], m.ident_bf[:, :], m.future_bf[:, :],
                                        start=False, stop=True)
            last.then_inc(m.scores_ready, 1)
        c, j = (a, k - LAG) if k >= LAG else later(before, k - LAG)
        if c:
            u, qt = divmod(j, NQ)
            pe.wait_ge(m.probs_ready, c.n0 + j + 1)
            wait(pe, m.turned_taken[j % 2], c.half0 + j // 2)
            for kt in range(c.keys(qt) // P):
                last = nc.tensor.transpose(m.ps[4 + j % 2][:, kt * P:(kt + 1) * P],
                                           m.p[:, j % 4, kt * P:(kt + 1) * P], m.ident[:, :])
            last.then_inc(m.turned_ready, 1)
        group_steps = NQ * (a or before).group
        g, part = divmod(k - LAG, group_steps)
        c, g = (a, g - 1) if g >= 1 else (before, g - 1 + before.steps // group_steps if before else g)
        if c and part < NQ:
            if part == 0:
                for par in range(2):
                    pe.wait_ge(m.turned_taken[par], c.half0 + (g + 1) * group_steps // 2)
            c.values(pe, g, part)
        if a and k in a.after:
            a.after[k](pe)


def attend_vector(nc, dve, m, a, before=None):
    for k in range(a.steps if a else VECTOR_TAKES):
        if a:
            if k in a.vector_before:
                a.vector_before[k](dve)
            dve.wait_ge(m.scores_ready, a.n0 + k + 1)
            nc.vector.tensor_reduce(m.negmax[:, k % 4:k % 4 + 1], m.ps[k % 4][:, 0:a.keys(k % NQ)], AX.X, ALU.max,
                                    negate=True).then_inc(m.negmax_ready, 1)
        c, j = (a, k - 1) if k >= 1 else later(before, k - 1)
        if c:
            dve.wait_ge(m.exp_done, c.n0 + j + 1)
            nc.vector.reciprocal(m.rsum[:, j % 4:j % 4 + 1], m.sum[:, j % 4:j % 4 + 1]).then_inc(m.rsum_ready, 1)
            dve.wait_ge(m.rsum_ready, c.n0 + j + 1)
            pr = m.p[:, j % 4, 0:c.keys(j % NQ)]
            nc.vector.tensor_scalar(pr, pr, m.rsum[:, j % 4:j % 4 + 1], None, ALU.mult).then_inc(m.probs_ready, 1)
        c, j = (a, k - VECTOR_TAKES) if k >= VECTOR_TAKES else later(before, k - VECTOR_TAKES)
        if c and j % 2 == 1:
            take_turned(nc.vector.tensor_copy, dve, m, c, j)


def attend_scalar(nc, act, m, a, before=None):
    def take(out, in_):
        return nc.scalar.activation(out, in_, ACT.Copy)

    for k in range(a.steps if a else SCALAR_TAKES):
        if a:
            if k in a.scalar_before:
                a.scalar_before[k](act)
            act.wait_ge(m.negmax_ready, a.n0 + k + 1)
            wait(act, m.turned_ready, a.n0 + k - 3)
            wait(act, m.rsum_ready, a.n0 + k - 3)
            keys = a.keys(k % NQ)
            nc.scalar.activation(m.p[:, k % 4, 0:keys], m.ps[k % 4][:, 0:keys], ACT.Exp, bias=m.negmax[:, k % 4:k % 4 + 1],
                                 accum_out=m.sum[:, k % 4:k % 4 + 1]).then_inc(m.exp_done, 1)
        c, j = (a, k - SCALAR_TAKES) if k >= SCALAR_TAKES else later(before, k - SCALAR_TAKES)
        if c and j % 2 == 0:
            take_turned(take, act, m, c, j)


def take_turned(copy, eng, m, a, j):
    u, qt = divmod(j, NQ)
    nb = a.keys(qt) // P
    eng.wait_ge(m.turned_ready, a.n0 + j + 1)
    a.group_done(eng, (u - 4) // a.group)
    copy(m.pt[:, u % 4, 0:nb, qt * P:(qt + 1) * P],
         m.ps[4 + j % 2][:, 0:nb * P].rearrange("p (b q) -> p b q", q=P)).then_inc(m.turned_taken[j % 2], 1)



def l0_attn_tensor(nc, pe, m):
    w = m.w["l0a"]
    pe.wait_ge(m.consts_in, 16 * m.n_consts)
    turn_tensor(nc, pe, m, "l0n")
    pe.wait_ge(m.loaded["l0a"], 16)
    turned(m, pe, "l0n")
    pe.wait_ge(m.consts_cast, 3)
    for name, wt in (("l0q", w["wq"]), ("l0k", w["wk"])):
        for j in range(2):
            bank = fill(m, pe, f"{name}{j}")
            nc.tensor.matmul(bank[:, :], wt, m.xn_t[:, j * S:(j + 1) * S], start=True,
                             stop=True).then_inc(filled(m, f"{name}{j}"), 1)
    tokens_tensor(nc, pe, m, "l0v", m.xn_t, w["wv"])
    for name in ("l0q", "l0k", "l0v"):
        for j in range(2):
            copied(m, pe, f"{name}{j}")

    def make(i, first=False):
        def before_first(pe):
            pe.wait_ge(m.head_q, 2 * i + 1)

        def before_second(pe):
            pe.wait_ge(m.head_q, 2 * i + 2)

        def values(pe, g, kt):
            b = g % 2
            if kt == 0:
                pe.wait_ge(m.head_v, 2 * i + g // 2 + 1)
                if first and g < 2:
                    fill(m, pe, f"l0o{b}")
            out = nc.tensor.matmul(m.ps[6 + b][:, kt * P:S], m.head_vals[:, g // 2, b * NQ + kt, :],
                                   m.pt[:, g, kt, kt * P:S], start=(first and g < 2 and kt == 0),
                                   stop=False, skip_group_check=True)
            if kt == NQ - 1:
                out.then_inc(m.pv_done, 1)

        return Attention(
            STEPS * i, STEPS // 2 * i, group=1, causal=True, keys=lambda qt: (qt + 1) * P,
            q=lambda u, qt: m.head_qs[:, u // 2, (u % 2) * S + qt * P:(u % 2) * S + (qt + 1) * P],
            k=lambda u, keys: m.k_t[:, (u % 2) * S:(u % 2) * S + keys],
            before_scores={0: before_first, 8: before_second}, after={}, values=values)

    attend_tensor(nc, pe, m, make(0, True))
    with pe.Fori(1, H // 2) as i:
        attend_tensor(nc, pe, m, make(i), make(i - 1))
    attend_tensor(nc, pe, m, None, make(H // 2 - 1))
    complete(nc, pe, m, "l0o")
    project_out_tensor(nc, pe, m, "l0o", "l0y", w["wo"])


def complete(nc, pe, m, name):
    for j in range(2):
        nc.tensor.matmul(m.ps[6 + j][:, 0:P], m.zeros[:, :], m.ident[:, :], start=False, stop=True,
                         skip_group_check=True).then_inc(filled(m, f"{name}{j}"), 1)


def tokens_tensor(nc, pe, m, name, x_t, w):
    for j in range(2):
        bank = fill(m, pe, f"{name}{j}")
        for t in range(4):
            last = nc.tensor.matmul(bank[:, t * P:(t + 1) * P], x_t[:, (4 * j + t) * P:(4 * j + t + 1) * P], w,
                                    start=True, stop=True)
        last.then_inc(filled(m, f"{name}{j}"), 1)


def project_out_tensor(nc, pe, m, source, name, w):
    for j in range(2):
        copied(m, pe, f"{source}{j}")
    tokens_tensor(nc, pe, m, name, m.o_t, w)


def add_to_x(nc, dve, m, name):
    add_to(nc, dve, m, name, m.x)


def add_to(nc, dve, m, name, x):
    for j in range(2):
        bank = read(m, dve, f"{name}{j}")
        last = nc.vector.tensor_tensor(x[:, 4 * j:4 * j + 4, :], x[:, 4 * j:4 * j + 4, :],
                                       bank[:, :].rearrange("p (t d) -> p t d", d=P), ALU.add)
        last.then_inc(emptied(m, f"{name}{j}"), 1)
    for j in range(2):
        copied(m, dve, f"{name}{j}")


def l0_attn_scalar(nc, act, m):
    w = m.w["l0a"]
    turn_scalar(nc, act, m, "l0n")
    act.wait_ge(m.loaded["l0a"], 16)
    for name, dst, bias in (("l0q", m.q_t, w["bq"]), ("l0k", m.k_t, w["bk"])):
        for j in range(2):
            bank = read(m, act, f"{name}{j}")
            nc.scalar.activation(dst[:, j * S:(j + 1) * S], bank[:, :], ACT.Identity,
                                 bias=bias).then_inc(emptied(m, f"{name}{j}"), 1)

    def make(i):
        return Attention(STEPS * i, STEPS // 2 * i, group=1, keys=lambda qt: (qt + 1) * P,
                         group_done=lambda eng, g: wait(eng, m.pv_done, 4 * i + g + 1))

    attend_scalar(nc, act, m, make(0))
    with act.Fori(1, H // 2) as i:
        attend_scalar(nc, act, m, make(i), make(i - 1))
    attend_scalar(nc, act, m, None, make(H // 2 - 1))
    for b in range(2):
        bank = read(m, act, f"l0o{b}")
        nc.scalar.activation(m.o_t[:, b * S:(b + 1) * S], bank[:, :], ACT.Copy).then_inc(emptied(m, f"l0o{b}"), 1)


def l0_attn_vector(nc, dve, m):
    w = m.w["l0a"]
    dve.wait_ge(m.x_in, 16)
    norm_to_turn(nc, dve, m, m.x)
    dve.wait_ge(m.loaded["l0a"], 16)
    for j in range(2):
        bank = read(m, dve, f"l0v{j}")
        nc.vector.tensor_tensor(m.v[:, 4 * j:4 * j + 4, :], bank[:, :].rearrange("p (t d) -> p t d", d=P),
                                w["bv"].rearrange("p (o d) -> p o d", o=1).broadcast_to([P, 4, P]),
                                ALU.add).then_inc(emptied(m, f"l0v{j}"), 1)
    for j in range(2):
        copied(m, dve, f"l0q{j}")

    def head_queries(p, head):
        nc.vector.tensor_scalar(m.head_qs[:, p, :], m.q_t[:, :], m.rows8[:, bass.ds(head, 1)] if not isinstance(head, int)
                                else m.rows8[:, head:head + 1], None, ALU.mult).then_inc(m.head_q, 1)

    head_queries(0, 0)

    def make(i):
        hooks = {0: lambda dve: head_queries(1, 2 * i + 1),
                 8: lambda dve: head_queries(0, 2 * i + 2)}
        return Attention(STEPS * i, STEPS // 2 * i, group=1, keys=lambda qt: (qt + 1) * P, vector_before=hooks,
                         group_done=lambda eng, g: wait(eng, m.pv_done, 4 * i + g + 1))

    attend_vector(nc, dve, m, make(0))
    with dve.Fori(1, H // 2) as i:
        attend_vector(nc, dve, m, make(i), make(i - 1))
    attend_vector(nc, dve, m, None, make(H // 2 - 1))
    m.dve.done(nc.vector.tensor_tensor(m.x[:, :, :], m.x[:, :, :],
                                       w["bo"].rearrange("p (o d) -> p o d", o=1).broadcast_to([P, NT, P]), ALU.add))
    add_to_x(nc, dve, m, "l0y")


def l0_attn_gpsimd(nc, pool, m):
    norm_gpsimd(nc, pool, m)
    for j in range(2):
        copied(m, pool, f"l0v{j}")

    def head_values(p, head):
        mask = m.cols8[:, head, :] if isinstance(head, int) else m.cols8[:, bass.ds(head, 1), :]
        mask = mask.rearrange("p d -> p () d") if isinstance(head, int) else mask
        nc.gpsimd.tensor_tensor(m.head_vals[:, p, :, :], m.v[:, :, :], mask.broadcast_to([P, NT, P]),
                                ALU.mult).then_inc(m.head_v, 1)

    head_values(0, 0)

    def one_pass(i):
        wait(pool, m.pv_done, 4 * i)
        head_values(1, 2 * i + 1)
        pool.wait_ge(m.pv_done, 4 * i + 2)
        head_values(0, 2 * i + 2)

    one_pass(0)
    with pool.Fori(1, H // 2) as i:
        one_pass(i)



XSTEPS = 2 * B * NQ


def cross_units():
    return [(b, half, qt) for b in range(B) for half in range(2) for qt in range(NQ)]


def cross_tensor(nc, pe, m, a):
    nk, units = a.nk, cross_units()
    for k in range(XSTEPS + 6):
        if k < XSTEPS:
            b, half, qt = units[k]
            wait(pe, m.negmax_ready, a.s0 + k - 1)
            for j in range(2):
                last = a.scores(m.ps[2 * (k % 2) + j], b, half, j, qt)
            last.then_inc(m.scores_ready, 1)
        j = k - 2
        if 0 <= j < XSTEPS:
            b, half, qt = units[j]
            pe.wait_ge(m.probs_ready, a.s0 + j + 1)
            wait(pe, m.cross_taken, a.x0 + j)
            for h in range(8):
                last = nc.tensor.transpose(m.ps[4 + h // 4][0:nk, (h % 4) * P:(h % 4 + 1) * P],
                                           m.xp[:, j % 3, h * nk:(h + 1) * nk], m.ident[:, :])
            last.then_inc(m.turned_ready, 1)
        j = k - 3 - (NQ - 1)
        if j >= 0:
            b, half, i = units[j]
            if i == 0:
                pe.wait_ge(m.cross_taken, a.x0 + j + NQ)
            a.values(pe, b, half, i)


def cross_vector(nc, dve, m, a):
    nk = a.nk
    view = lambda ap: ap.rearrange("p (g h k) -> p g h k", g=2, k=nk)
    spread = lambda ap: ap.rearrange("p (g h o) -> p g h o", g=2, o=1).broadcast_to([P, 2, 4, nk])
    for k in range(XSTEPS + 1):
        if k < XSTEPS:
            dve.wait_ge(m.scores_ready, a.s0 + k + 1)
            wait(dve, m.turned_ready, a.s0 + k - 2)
            scores = m.psum[:, 2 * (k % 2):2 * (k % 2) + 2, 0:4 * nk].rearrange("p g (h k) -> p g h k", k=nk)
            to = view(m.xp[:, k % 3, 0:8 * nk])
            if a.clip:
                m.dve.done(nc.vector.tensor_scalar(to, scores, a.clip, -a.clip, ALU.min, ALU.max))
                scores = to
            m.dve.done(nc.vector.tensor_reduce(m.xmax[:, k % 2, :].rearrange("p (g h) -> p g h", g=2), scores, AX.X, ALU.max))
            nc.vector.tensor_tensor(to, scores, spread(m.xmax[:, k % 2, :]), ALU.subtract).then_inc(m.negmax_ready, 1)
        j = k - 1
        if j >= 0:
            dve.wait_ge(m.exp_done, a.s0 + j + 1)
            sums = m.xsum[:, 8 * j:8 * j + 8]
            m.dve.done(nc.vector.tensor_reduce(sums, m.xp[:, j % 3, 0:8 * nk].rearrange("p (h k) -> p h k", k=nk),
                                               AX.X, ALU.add))
            wait(dve, m.probs_ready, a.s0 + j - 1)
            nc.vector.reciprocal(m.xrsum[:, j % 2, :], sums).then_inc(m.rsum_ready, 1)
        if k in a.vector_after:
            a.vector_after[k](dve)


def cross_scalar(nc, act, m, a):
    nk, units = a.nk, cross_units()
    for k in range(XSTEPS + 2):
        if k < XSTEPS:
            act.wait_ge(m.negmax_ready, a.s0 + k + 1)
            pr = m.xp[:, k % 3, 0:8 * nk]
            nc.scalar.activation(pr, pr, ACT.Exp).then_inc(m.exp_done, 1)
        j = k - 2
        if j >= 0:
            b, half, qt = units[j]
            act.wait_ge(m.turned_ready, a.s0 + j + 1)
            if b > 0 and qt == 0:
                a.unit_done(act, b - 1, half)
            nc.scalar.activation(m.xpt[0:nk, half, :, qt * P:(qt + 1) * P],
                                 m.psum[0:nk, 4:6, :].rearrange("p g (h q) -> p (g h) q", q=P),
                                 ACT.Copy).then_inc(m.cross_taken, 1)


def cross_gpsimd(nc, pool, m, a):
    nk = a.nk
    for k in range(XSTEPS):
        pool.wait_ge(m.rsum_ready, a.s0 + k + 1)
        pr = m.xp[:, k % 3, 0:8 * nk].rearrange("p (h k) -> p h k", k=nk)
        nc.gpsimd.tensor_tensor(pr, pr, m.xrsum[:, k % 2, :].rearrange("p (h o) -> p h o", o=1).broadcast_to([P, 8, nk]),
                                ALU.mult).then_inc(m.probs_ready, 1)


def project_turned_tensor(nc, pe, m, name, pairs, turn):
    for j in range(2):
        bank = fill(m, pe, f"{name}{j}")
        for n, (w, x_t) in enumerate(pairs):
            last = nc.tensor.matmul(bank[:, :], w, x_t(j), start=n == 0, stop=n == len(pairs) - 1)
        last.then_inc(filled(m, f"{name}{j}"), 1)
    turn_back_tensor(nc, pe, m, name, turn)


def turn_back_tensor(nc, pe, m, name, turn):
    for j in range(2):
        copied(m, pe, f"{name}{j}")
        bank = fill(m, pe, f"{turn}{j}")
        for t in range(4):
            last = nc.tensor.transpose(bank[:, t * P:(t + 1) * P], m.y_t[:, (4 * j + t) * P:(4 * j + t + 1) * P],
                                       m.ident[:, :])
        last.then_inc(filled(m, f"{turn}{j}"), 1)


def copy_out_scalar(nc, act, m, name, dst, scale=1.0, bias=0.0):
    for j in range(2):
        bank = read(m, act, f"{name}{j}")
        nc.scalar.activation(dst[:, j * S:(j + 1) * S], bank[:, :], ACT.Identity, scale=scale,
                             bias=bias).then_inc(emptied(m, f"{name}{j}"), 1)



L0X = Cross(SC + 1)
NPAIR = H // 2


def l0_cross_tensor(nc, pe, m):
    w, a = m.w["l0x"], L0X
    nk = a.nk
    a.s0, a.x0 = m.steps0["l0x"], m.cross0["l0x"]
    pe.wait_ge(m.loaded["l0x"], 16)
    pe.wait_ge(m.context_in, 16 * 5)
    for g in range(NPAIR):
        bank = fill(m, pe, f"l0xk{g}")
        nc.tensor.matmul(bank[:, 0:B * SC], w["wk"][0:DC, g * P:(g + 1) * P], m.context_t[0:DC, :], start=True,
                         stop=True).then_inc(filled(m, f"l0xk{g}"), 1)
    for n in range(2 * B):
        b, j = divmod(n, 2)
        bank = fill(m, pe, f"l0xv{n}")
        nc.tensor.matmul(bank[0:SC, :], m.context_t[0:DC, b * SC:(b + 1) * SC], w["wv"][0:DC, j * S:(j + 1) * S],
                         start=True, stop=True).then_inc(filled(m, f"l0xv{n}"), 1)
    turn_tensor(nc, pe, m, "l0xn")
    turned(m, pe, "l0xn")
    for n in range(2 * NPAIR):
        g, j = divmod(n, 2)
        bank = fill(m, pe, f"l0xq{n}")
        nc.tensor.matmul(bank[:, :], w["wq"][:, g * P:(g + 1) * P], m.xn_t[:, j * S:(j + 1) * S], start=True,
                         stop=True).then_inc(filled(m, f"l0xq{n}"), 1)
    for n in range(2 * NPAIR - 2, 2 * NPAIR):
        copied(m, pe, f"l0xq{n}")
    pe.wait_ge(m.cross_ready, 1)

    def scores(bank, b, half, j, qt):
        for i in range(2):
            g = 4 * half + 2 * j + i
            nc.tensor.matmul(bank[:, 2 * i * nk:2 * (i + 1) * nk], m.wide[:, g, b * S + qt * P:b * S + (qt + 1) * P],
                             m.keys_own[:, b, 2 * g * nk:2 * (g + 1) * nk], start=i == 0, stop=False,
                             skip_group_check=True)
        return nc.tensor.matmul(bank[:, 0:4 * nk], m.ones_bf[0:1, :], m.mask_row[0:1, b, :], start=False, stop=True,
                                skip_group_check=True)

    def values(pe, b, half, i):
        g = 4 * half + i
        name = f"l0xo{(b * 2 + half) * 4 + i}"
        bank = fill(m, pe, name)
        for e in range(2):
            last = nc.tensor.matmul(bank[64 * e:64 * e + 64, :],
                                    m.context_v[0:nk, b, (2 * g + e) * 64:(2 * g + e + 1) * 64],
                                    m.xpt[0:nk, half, 2 * i + e, :], start=True, stop=True)
        last.then_inc(filled(m, name), 1)

    a.scores, a.values = scores, values
    cross_tensor(nc, pe, m, a)
    for n in range(4 * NPAIR // 2 - 2, 4 * NPAIR // 2):
        copied(m, pe, f"l0xo{n}")
    project_turned_tensor(nc, pe, m, "l0xy",
                          [(w["wo"][:, g * P:(g + 1) * P], lambda j, g=g: m.wide[:, g, j * S:(j + 1) * S])
                           for g in range(NPAIR)], "l0xz")


def l0_cross_scalar(nc, act, m):
    w, a = m.w["l0x"], L0X
    a.s0, a.x0 = m.steps0["l0x"], m.cross0["l0x"]
    nk = a.nk
    act.wait_ge(m.keys_zero, 1)
    for g in range(NPAIR):
        bank = read(m, act, f"l0xk{g}")
        for e in range(2):
            at = (2 * g + e) * nk
            last = nc.scalar.activation(m.keys_own[64 * e:64 * e + 64, :, at:at + SC],
                                        bank[64 * e:64 * e + 64, 0:B * SC].rearrange("p (b k) -> p b k", k=SC), ACT.Copy)
        last.then_inc(emptied(m, f"l0xk{g}"), 1)
    turn_scalar(nc, act, m, "l0xn", scale=w["g_norm"])
    for g in range(NPAIR):
        bank = read(m, act, f"l0xq{2 * g}")
        nc.scalar.activation(m.wide[:, g, 0:S], bank[:, :], ACT.Copy,
                             scale=64 ** -0.5).then_inc(emptied(m, f"l0xq{2 * g}"), 1)
    a.unit_done = lambda eng, b, half: read(m, eng, f"l0xo{(b * 2 + half) * 4 + 3}")
    cross_scalar(nc, act, m, a)
    copy_out_scalar(nc, act, m, "l0xy", m.y_t)


def l0_cross_vector(nc, dve, m):
    w, a = m.w["l0x"], L0X
    a.s0, a.x0 = m.steps0["l0x"], m.cross0["l0x"]
    nk = a.nk
    dve.wait_ge(m.context_in, 16 * 5)
    dve.wait_ge(m.loaded["l0x"], 16)
    dve.wait_ge(m.keys_zero, 1)
    for e in range(2):
        null = m.keys_own[64 * e:64 * e + 64, :, :].rearrange("p b (g k) -> p b g k", k=2 * nk)[:, :, :, e * nk + SC]
        nc.vector.tensor_copy(null, w["null_k"][64 * e:64 * e + 64, :].broadcast_to([64, B * NPAIR]).rearrange(
            "p (b g) -> p b g", b=B))
    m.dve.done(nc.vector.tensor_scalar(m.mask_low[0:1, :], m.mask_u8[0:1, 0:2 * B * SC], -1.0, BIG, ALU.add, ALU.mult))
    nc.vector.tensor_copy(m.mask_row[0:1, :, :].rearrange("p b (h k) -> p b h k", k=nk)[:, :, :, 0:SC],
                          m.mask_low[0:1, 0:B * SC].rearrange("p (b o k) -> p b o k", o=1, k=SC).broadcast_to(
                              [1, B, 4, SC])).then_inc(m.cross_ready, 1)
    for n in range(2 * B):
        b, j = divmod(n, 2)
        bank = read(m, dve, f"l0xv{n}")
        nc.vector.tensor_copy(m.context_v[0:SC, b, j * S:(j + 1) * S],
                              bank[0:SC, :]).then_inc(emptied(m, f"l0xv{n}"), 1)
    m.dve.done(norm_vector(nc, dve, m, m.x, m.xn))
    norm_to_turn(nc, dve, m, m.xn)
    for g in range(NPAIR):
        bank = read(m, dve, f"l0xq{2 * g + 1}")
        nc.vector.tensor_scalar(m.wide[:, g, S:T], bank[:, :], float(64 ** -0.5), None,
                                ALU.mult).then_inc(emptied(m, f"l0xq{2 * g + 1}"), 1)

    def take_values(n):
        b, half, i = cross_units()[n]
        bank = read(m, dve, f"l0xo{n}")
        nc.vector.tensor_copy(m.wide[:, 4 * half + i, b * S:(b + 1) * S], bank[:, :]).then_inc(emptied(m, f"l0xo{n}"), 1)

    first = NQ + 3
    a.vector_after = {first + n: lambda dve, n=n: take_values(n) for n in range(XSTEPS - first + 1)}
    cross_vector(nc, dve, m, a)
    for n in range(XSTEPS - first + 1, XSTEPS):
        take_values(n)
    for j in range(2):
        bank = read(m, dve, f"l0xz{j}")
        last = nc.vector.tensor_copy(m.xn[:, 4 * j:4 * j + 4, :], bank[:, :].rearrange("p (t d) -> p t d", d=P))
        last.then_inc(emptied(m, f"l0xz{j}"), 1)
    for j in range(2):
        copied(m, dve, f"l0xz{j}")
    m.dve.done(norm_vector(nc, dve, m, m.xn, m.xn))
    m.dve.done(nc.vector.tensor_tensor(m.xn[:, :, :], m.xn[:, :, :], over_tiles(w["g_out"]), ALU.mult))
    m.dve.done(nc.vector.tensor_tensor(m.x[:, :, :], m.x[:, :, :], m.xn[:, :, :], ALU.add))


def over_tiles(row, tiles=NT):
    return row.rearrange("p (o d) -> p o d", o=1).broadcast_to([P, tiles, row.shape[1]])


def l0_cross_gpsimd(nc, pool, m):
    a = L0X
    a.s0 = m.steps0["l0x"]
    norm_gpsimd(nc, pool, m)
    norm_gpsimd(nc, pool, m)
    cross_gpsimd(nc, pool, m, a)
    norm_gpsimd(nc, pool, m)



def stream_sync(sp, m, dram, passes, free, slots=2, between=None):
    def one_pass(i):
        for s in range(slots):
            if not (isinstance(i, int) and i == 0):
                free(i, s)
            n = slots * i + s
            src = dram[n] if isinstance(n, int) else dram[bass.ds(n, 1)].rearrange("o p n -> (o p) n")
            sp.dma_start(m.slot[s][:, 0:dram.shape[2]], src).then_inc(m.slot_in[s], 16)

    one_pass(0)
    if between:
        between()
    with sp.Fori(1, passes) as i:
        one_pass(i)



E0, F0 = 8, 512
TOP_P = 0.8


def l0_ffn_sync(nc, sp, m, dram):
    def spread_gates():
        for j in range(2):
            copied(m, sp, f"l0fg{j}")
        sp.dma_start(dram["scratch_gates"], m.gate_t[0:E0, :]).then_inc(m.gates_out, 16)
        sp.wait_ge(m.gates_out, 16)
        for e in range(E0):
            sp.dma_start(m.wide[:, e, :], dram["scratch_gates"][e:e + 1, :].broadcast_to([P, T])).then_inc(
                m.gates_in[min(e // 2, 1)], 16)

    stream_sync(sp, m, dram["s_l0f"], E0 // 2,
                lambda i, s: sp.wait_ge(m.hidden_used, m.h0["l0f"] + 16 * (i - 1) + 8 * (s + 1)), between=spread_gates)


def l0_ffn_tensor(nc, pe, m):
    w = m.w["l0f"]
    pe.wait_ge(m.loaded["l0f"], 16)
    turn_tensor(nc, pe, m, "l0fn")
    turned(m, pe, "l0fn")
    bank = fill(m, pe, "l0fr")
    for t in range(NT):
        last = nc.tensor.matmul(bank[:, t * E0:(t + 1) * E0], m.xn_t[:, t * P:(t + 1) * P], w["wr"], start=True, stop=True)
    last.then_inc(filled(m, "l0fr"), 1)
    pe.wait_ge(m.gates_ready, 1)
    for j in range(2):
        bank = fill(m, pe, f"l0fg{j}")
        for t in range(4):
            last = nc.tensor.transpose(bank[0:E0, t * P:(t + 1) * P], m.gates[:, 4 * j + t, :], m.ident[:, :])
        last.then_inc(filled(m, f"l0fg{j}"), 1)
    for j in range(2):
        copied(m, pe, f"l0fg{j}")
    for j in range(2):
        bank = fill(m, pe, f"l0fy{j}")
        nc.tensor.matmul(bank[:, :], w["b2"][0:E0, :], m.gate_t[0:E0, j * S:(j + 1) * S], start=True, stop=False,
                         skip_group_check=True)
    g0, h0 = m.slot0["l0f"], m.h0["l0f"]

    def one_pass(i):
        base = h0 + 16 * i
        for k in range(16 + 2):
            if k < 16:
                s, fc, j = k // 8, k // 2 % 4, k % 2
                if k % 8 == 0:
                    pe.wait_ge(m.slot_in[s], 16 * (g0 + i + 1))
                if k >= 4:
                    pe.wait_ge(m.hidden_read, base + k - 3)
                nc.tensor.matmul(m.ps[k % 4][:, :], m.slots[:, s, fc * P:(fc + 1) * P], m.xn_t[:, j * S:(j + 1) * S],
                                 start=True, stop=True).then_inc(m.hidden_ready, 1)
            q = k - 2
            if q >= 0:
                s, fc, j = q // 8, q // 2 % 4, q % 2
                pe.wait_ge(m.hidden_gated, base + q + 1)
                last = nc.tensor.matmul(m.ps[6 + j][:, :], m.slots[:, s, F0 + fc * P:F0 + (fc + 1) * P], m.hidden[:, q % 4, :],
                                        start=False, stop=False, skip_group_check=True)
                last.then_inc(m.hidden_used, 1)

    with pe.Fori(0, E0 // 2) as i:
        one_pass(i)
    complete(nc, pe, m, "l0fy")
    turn_back_tensor(nc, pe, m, "l0fy", "l0fz")


def l0_ffn_scalar(nc, act, m):
    w = m.w["l0f"]
    act.wait_ge(m.loaded["l0f"], 16)
    turn_scalar(nc, act, m, "l0fn")
    act.wait_ge(m.router_less_max, 1)
    nc.scalar.activation(m.gates[:, :, :], m.gates[:, :, :], ACT.Exp).then_inc(m.router_exp, 1)
    for j in range(2):
        bank = read(m, act, f"l0fg{j}")
        nc.scalar.activation(m.gate_t[0:E0, j * S:(j + 1) * S], bank[0:E0, :], ACT.Copy).then_inc(emptied(m, f"l0fg{j}"), 1)
    h0 = m.h0["l0f"]

    def one_pass(i):
        for k in range(16):
            s, fc = k // 8, k // 2 % 4
            act.wait_ge(m.hidden_ready, h0 + 16 * i + k + 1)
            wait(act, m.hidden_used, h0 + 16 * i + k - 3)
            nc.scalar.activation(m.hidden[:, k % 4, :], m.ps[k % 4][:, :], ACT.Relu,
                                 bias=m.slots[:, s, 2 * F0 + fc:2 * F0 + fc + 1]).then_inc(m.hidden_read, 1)

    one_pass(0)
    with act.Fori(1, E0 // 2) as i:
        one_pass(i)
    copy_out_scalar(nc, act, m, "l0fy", m.y_t)


def l0_ffn_vector(nc, dve, m):
    w = m.w["l0f"]
    d = m.dve
    dve.wait_ge(m.loaded["l0f"], 16)
    norm_to_turn(nc, dve, m, m.x)
    gates = m.gates[:, :, :]
    bank = read(m, dve, "l0fr")
    nc.vector.tensor_tensor(gates, bank[:, 0:NT * E0].rearrange("p (t e) -> p t e", e=E0),
                            over_tiles(w["br"]), ALU.add).then_inc(emptied(m, "l0fr"), 1)
    copied(m, dve, "l0fr")
    last8 = lambda ap: ap.rearrange("p (t o) -> p t o", o=1).broadcast_to([P, NT, E0])
    d.done(nc.vector.tensor_reduce(m.per_token[:, 0, :], gates, AX.X, ALU.max))
    nc.vector.tensor_tensor(gates, gates, last8(m.per_token[:, 0, :]), ALU.subtract).then_inc(m.router_less_max, 1)
    dve.wait_ge(m.router_exp, 1)
    d.done(nc.vector.tensor_reduce(m.per_token[:, 1, :], gates, AX.X, ALU.add))
    d.done(nc.vector.reciprocal(m.per_token[:, 2, :], m.per_token[:, 1, :]))
    d.done(nc.vector.tensor_tensor(gates, gates, last8(m.per_token[:, 2, :]), ALU.mult))
    shape = [P, NT, E0, E0]
    mine = gates.rearrange("p t (e o) -> p t e o", o=1).broadcast_to(shape)
    other = gates.rearrange("p t (o e) -> p t o e", o=1).broadcast_to(shape)
    ahead, tie = m.pairs[:, 0, :, :, :], m.pairs[:, 1, :, :, :]
    not_after = w["not_after"].rearrange("p (o e j) -> p o e j", o=1, j=E0).broadcast_to(shape)
    d.done(nc.vector.tensor_tensor(tie, mine, other, ALU.is_equal))
    d.done(nc.vector.tensor_tensor(tie, tie, not_after, ALU.mult))
    d.done(nc.vector.tensor_tensor(ahead, other, mine, ALU.is_gt))
    d.done(nc.vector.tensor_tensor(ahead, ahead, tie, ALU.add))
    d.done(nc.vector.tensor_reduce(m.keep[:, 0, :, :], ahead, AX.X, ALU.add))
    d.done(nc.vector.tensor_tensor(ahead, ahead, other, ALU.mult))
    d.done(nc.vector.tensor_reduce(m.keep[:, 1, :, :], ahead, AX.X, ALU.add))
    d.done(nc.vector.tensor_scalar(m.keep[:, 0, :, :], m.keep[:, 0, :, :], 1.5, None, ALU.is_lt))
    d.done(nc.vector.tensor_scalar(m.keep[:, 1, :, :], m.keep[:, 1, :, :], TOP_P, None, ALU.is_lt))
    d.done(nc.vector.tensor_tensor(m.keep[:, 0, :, :], m.keep[:, 0, :, :], m.keep[:, 1, :, :], ALU.max))
    nc.vector.tensor_tensor(gates, gates, m.keep[:, 0, :, :], ALU.mult).then_inc(m.gates_ready, 1)
    h0 = m.h0["l0f"]

    def one_pass(i):
        for k in range(16):
            s, j = k // 8, k % 2
            dve.wait_ge(m.hidden_read, h0 + 16 * i + k + 1)
            at = slice(j * S, (j + 1) * S)
            gate = m.wide[:, s, at] if isinstance(i, int) else m.wide[:, bass.ds(2 * i + s, 1), at].rearrange("p o n -> p (o n)")
            nc.vector.tensor_tensor(m.hidden[:, k % 4, :], m.hidden[:, k % 4, :], gate, ALU.mult).then_inc(m.hidden_gated, 1)

    dve.wait_ge(m.gates_in[0], 16 * 2)
    one_pass(0)
    dve.wait_ge(m.gates_in[1], 16 * (E0 - 2))
    with dve.Fori(1, E0 // 2) as i:
        one_pass(i)
    add_to_x(nc, dve, m, "l0fz")


def l0_ffn_gpsimd(nc, pool, m):
    norm_gpsimd(nc, pool, m)



PROJECT_AT = LAG + NQ


class BankUses:

    def __init__(self, n):
        self.n, self.uses = n, NPAIR * (n + 1)

    def projection(self, g):
        first = isinstance(g, int) and g == 0
        return 0 if first else g * (self.n + 1) - 1

    def output(self, g):
        last = isinstance(g, int) and g == NPAIR - 1
        return g * (self.n + 1) + (self.n if last else 2 * self.n)


PAIR1, PAIR3 = BankUses(3), BankUses(4)
USES = {"l1aj": PAIR1, "l3fj": PAIR3}


def over_pairs(eng, one, drain):
    one(0, 0, None)
    with eng.Fori(1, NPAIR // 2) as i:
        one(i - 1, 1, (i - 1, 0))
        one(i, 0, (i - 1, 1))
    one(NPAIR // 2 - 1, 1, (NPAIR // 2 - 1, 0))
    drain(NPAIR // 2 - 1, 1)


def next_pair(r, s):
    if isinstance(r, int) and 2 * r + s == NPAIR - 1:
        return None
    return (r, 1) if s == 0 else (r + 1, 0)


def pair_project_tensor(nc, pe, m, name, r, s, what, weights):
    w_q, w_k, k_src, v_src, w_v = weights(s)
    for j in range(2):
        bank = fill(m, pe, f"{name}{j}", USES[name].projection(2 * r + s) + what)
        if what == 0:
            last = nc.tensor.matmul(bank[:, :], w_q, m.xn_t[:, j * S:(j + 1) * S], start=True, stop=True)
        elif what == 1:
            last = nc.tensor.matmul(bank[:, :], w_k, k_src[:, j * S:(j + 1) * S], start=True, stop=True)
        else:
            for t in range(4):
                last = nc.tensor.matmul(bank[:, t * P:(t + 1) * P], v_src[:, (4 * j + t) * P:(4 * j + t + 1) * P], w_v,
                                        start=True, stop=True)
        last.then_inc(filled(m, f"{name}{j}"), 1)


def pair_project_scalar(nc, act, m, name, r, s, what, scale):
    for j in range(2):
        bank = read(m, act, f"{name}{j}", USES[name].projection(2 * r + s) + what)
        if what == 0:
            last = nc.scalar.activation(m.pair_q[s][:, j * S:(j + 1) * S], bank[:, :], ACT.Copy, scale=scale)
        elif what == 1:
            for e in range(2):
                last = nc.scalar.activation(m.pair_k[64 * e:64 * e + 64, s, e, j * S:(j + 1) * S],
                                            bank[64 * e:64 * e + 64, :], ACT.Copy)
        else:
            last = nc.scalar.activation(m.pair_v[s][:, 4 * j:4 * j + 4, :],
                                        bank[:, :].rearrange("p (t d) -> p t d", d=P), ACT.Copy)
        last.then_inc(emptied(m, f"{name}{j}"), 1)


def first_projections(name, project):
    for what in range(USES[name].n):
        project(0, 0, what)


def next_projections(name, project, r, s, delay):
    after = next_pair(r, s)
    if after is None:
        return {}
    return {PROJECT_AT + delay + what: (lambda eng, what=what: project(*after, what)) for what in range(USES[name].n)}


def pair_attention(m, name, stage, r, s, causal, **parts):
    g = 2 * r + s

    def group_done(eng, b):
        if b >= 0:
            read(m, eng, f"{name}{b}", USES[name].output(g))
        elif not (isinstance(g, int) and g == 0):
            read(m, eng, f"{name}{b + 2}", USES[name].output(g - 1))

    return Attention(m.steps0[stage] + STEPS * g, m.half0[stage] + STEPS // 2 * g, group=2, causal=causal,
                     keys=(lambda qt: (qt + 1) * P) if causal else (lambda qt: S), group_done=group_done, **parts)


def pair_attend_tensor(nc, pe, m, name, stage, causal, project, projected):
    def make(r, s):
        def values(pe, b, kt):
            bank = fill(m, pe, f"{name}{b}", USES[name].output(2 * r + s)) if kt == 0 else m.ps[6 + b]
            q0 = kt * P if causal else 0
            for e in range(2):
                last = nc.tensor.matmul(bank[64 * e:64 * e + 64, q0:S],
                                        m.pair_v[s][:, b * NQ + kt, 64 * e:64 * e + 64],
                                        m.pt[:, 2 * b + e, kt, q0:S], start=kt == 0, stop=kt == NQ - 1,
                                        skip_group_check=True)
            if kt == NQ - 1:
                last.then_inc(filled(m, f"{name}{b}"), 1)

        return pair_attention(
            m, name, stage, r, s, causal, values=values,
            q=lambda u, qt: m.pair_q[s][:, (u // 2) * S + qt * P:(u // 2) * S + (qt + 1) * P],
            k=lambda u, keys: m.pair_k[:, s, u % 2, (u // 2) * S:(u // 2) * S + keys],
            before_scores={0: lambda pe: projected(r, s)},
            after=next_projections(name, project, r, s, 0))

    first_projections(name, project)
    over_pairs(pe, lambda r, s, before: attend_tensor(nc, pe, m, make(r, s), make(*before) if before else None),
               lambda r, s: attend_tensor(nc, pe, m, None, make(r, s)))


def pair_attend_scalar(nc, act, m, name, stage, causal, project):
    def make(r, s):
        return pair_attention(m, name, stage, r, s, causal, scalar_before=next_projections(name, project, r, s, 1))

    first_projections(name, project)
    over_pairs(act, lambda r, s, before: attend_scalar(nc, act, m, make(r, s), make(*before) if before else None),
               lambda r, s: attend_scalar(nc, act, m, None, make(r, s)))


def pair_attend_vector(nc, dve, m, name, stage, causal, project):
    def take_output(r, s, b):
        bank = read(m, dve, f"{name}{b}", USES[name].output(2 * r + s))
        to = m.wide[:, bass.ds(2 * r + s, 1), b * S:(b + 1) * S].rearrange("p o n -> p (o n)")
        nc.vector.tensor_scalar(to, bank[:, :], 1.0, None, ALU.mult).then_inc(emptied(m, f"{name}{b}"), 1)

    def make(r, s, before=None):
        hooks = next_projections(name, project, r, s, 1)
        hooks[STEPS - 1] = lambda dve: take_output(r, s, 0)
        if before:
            hooks[PROJECT_AT] = lambda dve: take_output(*before, 1)
        return pair_attention(m, name, stage, r, s, causal, vector_before=hooks)

    def drain(r, s):
        attend_vector(nc, dve, m, None, make(r, s))
        take_output(r, s, 1)

    first_projections(name, project)
    over_pairs(dve, lambda r, s, before: attend_vector(nc, dve, m, make(r, s, before), make(*before) if before else None),
               drain)



LATENT = 32
L1A_PARTS = ("wq", "wk", "wv")


def l1_attn_sync(nc, sp, m, dram):
    def free(i, s):
        sp.wait_ge(m.exp_done, m.steps0["l1a"] + STEPS * (2 * (i - 1) + s) + 1)

    sp.wait_ge(m.hidden_used, 8 * E0)
    stream_sync(sp, m, dram["s_l1a"], NPAIR // 2, free)


def l1_attn_tensor(nc, pe, m):
    w = m.w["l1a"]
    g0 = m.slot0["l1a"]
    pe.wait_ge(m.loaded["l1a"], 16)
    turn_tensor(nc, pe, m, "l1an")
    turned(m, pe, "l1an")
    for j in range(2):
        bank = fill(m, pe, f"l1al{j}")
        nc.tensor.matmul(bank[0:LATENT, :], w["down"], m.xn_t[:, j * S:(j + 1) * S], start=True,
                         stop=True).then_inc(filled(m, f"l1al{j}"), 1)
    for j in range(2):
        copied(m, pe, f"l1al{j}")

    def project(r, s, what):
        pe.wait_ge(m.slot_in[s], 16 * (g0 + r + 1))
        part = lambda n: m.slots[:, s, n * P:(n + 1) * P]
        pair_project_tensor(nc, pe, m, "l1aj", r, s, what, lambda s: (part(0), part(1), m.latent_t, m.latent_t, part(2)))

    def projected(r, s):
        for j in range(2):
            copied(m, pe, f"l1aj{j}", PAIR1.projection(2 * r + s) + PAIR1.n - 1)

    pair_attend_tensor(nc, pe, m, "l1aj", "l1a", True, project, projected)
    for j in range(2):
        copied(m, pe, f"l1aj{j}", PAIR1.uses - 1)
    project_turned_tensor(nc, pe, m, "l1ay",
                          [(w["wo"][:, g * P:(g + 1) * P], lambda j, g=g: m.wide[:, g, j * S:(j + 1) * S])
                           for g in range(NPAIR)], "l1az")


def l1_attn_scalar(nc, act, m):
    turn_scalar(nc, act, m, "l1an")
    act.wait_ge(m.pair_zero, 1)
    for j in range(2):
        bank = read(m, act, f"l1al{j}")
        nc.scalar.activation(m.latent_t[0:LATENT, j * S:(j + 1) * S], bank[0:LATENT, :],
                             ACT.Copy).then_inc(emptied(m, f"l1al{j}"), 1)
    pair_attend_scalar(nc, act, m, "l1aj", "l1a", True,
                       lambda r, s, what: pair_project_scalar(nc, act, m, "l1aj", r, s, what, 64 ** -0.5))
    copy_out_scalar(nc, act, m, "l1ay", m.y_t)


def l1_attn_vector(nc, dve, m):
    norm_to_turn(nc, dve, m, m.x)
    pair_attend_vector(nc, dve, m, "l1aj", "l1a", True, lambda r, s, what: None)
    add_to_x(nc, dve, m, "l1az")


def l1_attn_gpsimd(nc, pool, m):
    pool.wait_ge(m.stage_done, 3)
    nc.gpsimd.memset(m.latent_t[:, :], 0.0)
    nc.gpsimd.memset(m.pair_k[:, :, :, :], 0.0).then_inc(m.pair_zero, 1)
    norm_gpsimd(nc, pool, m)



RMS_EPS = 1e-8
ALLK = S + SC


def l1_cross_units():
    return [(b, h, qt) for b in range(B) for h in range(2) for qt in range(NQ)]


def l1_cross_tensor(nc, pe, m):
    w = m.w["l1x"]
    pe.wait_ge(m.loaded["l1x"], 16)
    turn_tensor(nc, pe, m, "l1xn")
    turned(m, pe, "l1xn")
    tokens_tensor(nc, pe, m, "l1xq", m.xn_t, w["wq"])
    tokens_tensor(nc, pe, m, "l1xk", m.xn_t, w["wlk"])
    tokens_tensor(nc, pe, m, "l1xv", m.xn_t, w["wlv"])
    pe.wait_ge(m.context_normed, 1)
    bank = fill(m, pe, "l1xc0")
    for b in range(B):
        last = nc.tensor.transpose(bank[0:DC, b * SC:(b + 1) * SC], m.context[:, b, :], m.ident[0:SC, 0:SC])
    last.then_inc(filled(m, "l1xc0"), 1)
    copied(m, pe, "l1xc0")
    for b in range(B):
        bank = fill(m, pe, f"l1xd{b}")
        nc.tensor.matmul(bank[0:SC, 0:2 * P], m.context_norm_t[0:DC, b * SC:(b + 1) * SC], w["wkv"][0:DC, :], start=True,
                         stop=True).then_inc(filled(m, f"l1xd{b}"), 1)
    pe.wait_ge(m.rms_done, 1)
    for name, src in (("l1xqt", m.q_tok), ("l1xkt", m.k_tok)):
        for j in range(2):
            bank = fill(m, pe, f"{name}{j}")
            for t in range(4):
                last = nc.tensor.transpose(bank[:, t * P:(t + 1) * P], src[:, 4 * j + t, :], m.ident[:, :])
            last.then_inc(filled(m, f"{name}{j}"), 1)
    bank = fill(m, pe, "l1xct0")
    for b in range(B):
        last = nc.tensor.transpose(bank[:, b * SC:(b + 1) * SC], m.context_kv[0:SC, b, 0:P], m.ident[0:SC, 0:SC])
    last.then_inc(filled(m, "l1xct0"), 1)
    for name in ("l1xqt0", "l1xqt1", "l1xkt0", "l1xkt1", "l1xct0"):
        copied(m, pe, name)
    pe.wait_ge(m.low_row_ready, 1)
    s0, x0, units = m.steps0["l1x"], m.cross0["l1x"], l1_cross_units()
    for k in range(XSTEPS + 3):
        if k < XSTEPS:
            b, h, qt = units[k]
            pe.wait_ge(m.exp_done, s0 + k - 1)
            q = m.q_t[:, b * S + qt * P:b * S + (qt + 1) * P]
            nc.tensor.matmul(m.ps[2 * (k % 2)], q, m.pair_k[:, 0, h, b * S:(b + 1) * S], start=True, stop=True)
            bank = m.ps[2 * (k % 2) + 1]
            nc.tensor.matmul(bank[:, 0:SC], q, m.pair_k[:, 1, h, b * SC:(b + 1) * SC], start=True, stop=False)
            nc.tensor.matmul(bank[:, 0:SC], m.ones_bf[0:1, :], m.low_row[0:1, b * SC:(b + 1) * SC], start=False,
                             stop=True).then_inc(m.scores_ready, 1)
        j = k - 2
        if 0 <= j < XSTEPS:
            pe.wait_ge(m.probs_ready, s0 + j + 1)
            pe.wait_ge(m.cross_taken, x0 + j)
            wait(pe, m.tail_taken, j)
            for n in range(NQ):
                nc.tensor.transpose(m.ps[4][:, n * P:(n + 1) * P], m.xp[:, j % 3, n * P:(n + 1) * P], m.ident[:, :])
            nc.tensor.transpose(m.ps[5][0:SC, 0:P], m.xp[:, j % 3, S:ALLK], m.ident[:, :]).then_inc(m.turned_ready, 1)
        j = k - 3
        if j >= 0 and (j + 1) % (2 * NQ) == 0:
            b = j // (2 * NQ)
            pe.wait_ge(m.cross_taken, x0 + j + 1)
            pe.wait_ge(m.tail_taken, j + 1)
            bank = fill(m, pe, f"l1xo{b}")
            for n in range(NQ + 1):
                for h in range(2):
                    hd = slice(64 * h, 64 * h + 64)
                    if n < NQ:
                        nc.tensor.matmul(bank[hd, :], m.v[:, b * NQ + n, hd], m.pt[:, 2 * b + h, n, :], start=n == 0,
                                         stop=False, skip_group_check=True)
                    else:
                        last = nc.tensor.matmul(bank[hd, :], m.context_kv[0:SC, b, P + 64 * h:P + 64 * h + 64],
                                                m.tail_pt[0:SC, 2 * b + h, :], start=False, stop=True,
                                                skip_group_check=True)
            last.then_inc(filled(m, f"l1xo{b}"), 1)
    project_out_tensor(nc, pe, m, "l1xo", "l1xy", w["wo"])


def l1_cross_scalar(nc, act, m):
    w = m.w["l1x"]
    act.wait_ge(m.loaded["l1x"], 16)
    turn_scalar(nc, act, m, "l1xn", scale=w["ln_l_g"], bias=w["ln_l_b"])
    for name, dst in (("l1xq", m.q_tok), ("l1xk", m.k_tok), ("l1xv", m.v)):
        for j in range(2):
            bank = read(m, act, f"{name}{j}")
            nc.scalar.activation(dst[:, 4 * j:4 * j + 4, :], bank[:, :].rearrange("p (t d) -> p t d", d=P),
                                 ACT.Copy).then_inc(emptied(m, f"{name}{j}"), 1)
    bank = read(m, act, "l1xc0")
    nc.scalar.activation(m.context_norm_t[0:DC, :], bank[0:DC, 0:B * SC], ACT.Copy).then_inc(emptied(m, "l1xc0"), 1)
    for b in range(B):
        bank = read(m, act, f"l1xd{b}")
        nc.scalar.activation(m.context_kv[0:SC, b, :], bank[0:SC, 0:2 * P], ACT.Copy).then_inc(emptied(m, f"l1xd{b}"), 1)
    act.wait_ge(m.rms_ready, 1)
    nc.scalar.activation(m.rms[:, :], m.rms[:, :], ACT.Sqrt).then_inc(m.rms_inverted, 1)
    for j in range(2):
        bank = read(m, act, f"l1xqt{j}")
        nc.scalar.activation(m.q_t[:, j * S:(j + 1) * S], bank[:, :], ACT.Copy,
                             scale=w["qn_g"]).then_inc(emptied(m, f"l1xqt{j}"), 1)
    for j in range(2):
        bank = read(m, act, f"l1xkt{j}")
        for h in range(2):
            own = slice(64 * h, 64 * h + 64)
            last = nc.scalar.activation(m.pair_k[own, 0, h, j * S:(j + 1) * S], bank[own, :], ACT.Copy,
                                        scale=w["kn_g"][own, :])
        last.then_inc(emptied(m, f"l1xkt{j}"), 1)
    bank = read(m, act, "l1xct0")
    for h in range(2):
        own = slice(64 * h, 64 * h + 64)
        last = nc.scalar.activation(m.pair_k[own, 1, h, 0:B * SC], bank[own, 0:B * SC], ACT.Copy, scale=w["kn_g"][own, :])
    last.then_inc(emptied(m, "l1xct0"), 1)
    s0, x0, units = m.steps0["l1x"], m.cross0["l1x"], l1_cross_units()
    for k in range(XSTEPS + 2):
        if k < XSTEPS:
            act.wait_ge(m.negmax_ready, s0 + k + 1)
            act.wait_ge(m.turned_ready, s0 + k - 2)
            nc.scalar.activation(m.xp[:, k % 3, 0:ALLK], scores_of(m, k), ACT.Exp, bias=m.negmax[:, k % 4:k % 4 + 1],
                                 accum_out=m.sum[:, k % 4:k % 4 + 1]).then_inc(m.exp_done, 1)
        j = k - 2
        if j >= 0:
            b, h, qt = units[j]
            act.wait_ge(m.turned_ready, s0 + j + 1)
            nc.scalar.activation(m.pt[:, 2 * b + h, :, qt * P:(qt + 1) * P],
                                 m.ps[4].rearrange("p (b q) -> p b q", q=P), ACT.Copy).then_inc(m.cross_taken, 1)
    copy_out_scalar(nc, act, m, "l1xo", m.o_t)


def scores_of(m, k):
    return m.psum[:, 2 * (k % 2):2 * (k % 2) + 2, :].rearrange("p g s -> p (g s)")[:, 0:ALLK]


def l1_cross_vector(nc, dve, m):
    w, d = m.w["l1x"], m.dve
    dve.wait_ge(m.loaded["l1x"], 16)
    nc.vector.memset(m.rms[:, :], 1.0)
    d.done(norm_vector(nc, dve, m, m.x, m.xn))
    norm_to_turn(nc, dve, m, m.xn)
    for b in range(B):
        last = nc.vector.bn_stats(m.stats[0:SC, b, :], m.context[:, b, :])
    d.done(last)
    for b in range(B):
        last = nc.vector.bn_aggr(m.moments[0:SC, b, :], m.stats[0:SC, b, :])
    d.done(last)
    nc.vector.tensor_scalar(m.var[0:SC, 0:B], m.moments[0:SC, 0:B, 1], 1e-5, None, ALU.add).then_inc(m.var_ready, 1)
    m.norms += 1
    dve.wait_ge(m.rstd_ready, m.norms)
    for b in range(B):
        last = nc.vector.tensor_scalar(m.context[:, b, :], m.context[:, b, :], m.moments[0:SC, b, 0:1], m.rstd[0:SC, b:b + 1],
                                       ALU.subtract, ALU.mult)
    d.done(last)
    each = lambda row: row[0:SC, :].rearrange("p (o d) -> p o d", o=1).broadcast_to([SC, B, DC])
    d.done(nc.vector.tensor_tensor(m.context[:, :, :], m.context[:, :, :], each(w["ln_x_g"]), ALU.mult))
    nc.vector.tensor_tensor(m.context[:, :, :], m.context[:, :, :], each(w["ln_x_b"]), ALU.add).then_inc(m.context_normed, 1)
    nc.vector.tensor_copy(m.low_row[0:1, :], m.mask_low[0:1, B * SC:2 * B * SC]).then_inc(m.low_row_ready, 1)
    heads = lambda ap: ap.rearrange("p t (h d) -> p (t h) d", d=64)
    for name, src, at in (("l1xq", m.q_tok, 0), ("l1xk", m.k_tok, 2 * NT)):
        for j in range(2):
            copied(m, dve, f"{name}{j}")
        d.done(nc.vector.tensor_tensor(m.squares, src, src, ALU.mult))
        d.done(nc.vector.tensor_reduce(m.rms[:, at:at + 2 * NT], heads(m.squares), AX.X, ALU.add))
    for b in range(B):
        copied(m, dve, f"l1xd{b}")
    ck = m.context_kv[0:SC, :, 0:P]
    d.done(nc.vector.tensor_tensor(m.squares[0:SC, 0:B, :], ck, ck, ALU.mult))
    d.done(nc.vector.tensor_reduce(m.rms[0:SC, 4 * NT:4 * NT + 2 * B], heads(m.squares[0:SC, 0:B, :]), AX.X, ALU.add))
    d.done(nc.vector.tensor_scalar(m.rms[:, :], m.rms[:, :], 1.0 / 64, RMS_EPS ** 2, ALU.mult, ALU.max))
    nc.vector.reciprocal(m.rms[:, :], m.rms[:, :]).then_inc(m.rms_ready, 1)
    dve.wait_ge(m.rms_inverted, 1)
    q_r = m.rms[:, 0:2 * NT]
    d.done(nc.vector.tensor_scalar(q_r, q_r, float(64 ** -0.5), None, ALU.mult))
    spread = lambda ap, n: ap.rearrange("p (t o) -> p t o", o=1).broadcast_to([ap.shape[0], n, 64])
    nc.vector.tensor_tensor(heads(m.q_tok), heads(m.q_tok), spread(q_r, 2 * NT), ALU.mult)
    nc.vector.tensor_tensor(heads(m.k_tok), heads(m.k_tok), spread(m.rms[:, 2 * NT:4 * NT], 2 * NT), ALU.mult)
    ckh = ck.rearrange("p b (h d) -> p b h d", d=64)
    nc.vector.tensor_tensor(ckh, ckh, m.rms[0:SC, 4 * NT:4 * NT + 2 * B].rearrange("p (b h o) -> p b h o", h=2, o=1)
                            .broadcast_to([SC, B, 2, 64]), ALU.mult).then_inc(m.rms_done, 1)
    d.done(nc.vector.tensor_tensor(m.x[:, :, :], m.x[:, :, :], over_tiles(w["bo"]), ALU.add))
    s0, units = m.steps0["l1x"], l1_cross_units()
    for k in range(XSTEPS + 3):
        if k < XSTEPS:
            dve.wait_ge(m.scores_ready, s0 + k + 1)
            nc.vector.tensor_reduce(m.negmax[:, k % 4:k % 4 + 1], scores_of(m, k), AX.X, ALU.max,
                                    negate=True).then_inc(m.negmax_ready, 1)
        j = k - 1
        if 0 <= j < XSTEPS:
            dve.wait_ge(m.exp_done, s0 + j + 1)
            nc.vector.reciprocal(m.rsum[:, j % 4:j % 4 + 1], m.sum[:, j % 4:j % 4 + 1]).then_inc(m.rsum_ready, 1)
            dve.wait_ge(m.rsum_ready, s0 + j + 1)
            pr = m.xp[:, j % 3, 0:ALLK]
            nc.vector.tensor_scalar(pr, pr, m.rsum[:, j % 4:j % 4 + 1], None, ALU.mult).then_inc(m.probs_ready, 1)
        j = k - 3
        if j >= 0:
            b, h, qt = units[j]
            dve.wait_ge(m.turned_ready, s0 + j + 1)
            nc.vector.tensor_copy(m.tail_pt[0:SC, 2 * b + h, qt * P:(qt + 1) * P], m.ps[5][0:SC, 0:P]).then_inc(m.tail_taken, 1)
    add_to_x(nc, dve, m, "l1xy")


def l1_cross_gpsimd(nc, pool, m):
    for _ in range(3):
        norm_gpsimd(nc, pool, m)



F1 = 384
INT_SCALE = 1.0 / 127.0


def l1_ffn_sync(nc, sp, m, dram):
    copied(m, sp, "l1aj1", PAIR1.uses - 1)
    sp.dma_start(m.ints[:, :], dram["ints"]).then_inc(m.ints_in, 16)


def l1_ffn_tensor(nc, pe, m):
    turn_tensor(nc, pe, m, "l1fn")
    turned(m, pe, "l1fn")
    pe.wait_ge(m.ints_cast, 1)
    n = F1 // P
    part = lambda what, c: m.cast_w[:, what * F1 + c * P:what * F1 + (c + 1) * P]
    for k in range(2 * n + 1):
        if k < 2 * n:
            c, j = divmod(k, 2)
            wait(pe, m.swiglu_done, k - 1)
            for what in range(2):
                last = nc.tensor.matmul(m.ps[2 * (k % 2) + what], part(what, c), m.xn_t[:, j * S:(j + 1) * S], start=True,
                                        stop=True)
            last.then_inc(m.swiglu_ready, 1)
        q = k - 1
        if q >= 0:
            c, j = divmod(q, 2)
            pe.wait_ge(m.swiglu_done, q + 1)
            bank = fill(m, pe, f"l1fy{j}") if c == 0 else m.ps[6 + j]
            last = nc.tensor.matmul(bank, part(2, c), m.hidden[:, q % 4, :], start=c == 0, stop=c == n - 1,
                                    skip_group_check=True)
            last.then_inc(filled(m, f"l1fy{j}") if c == n - 1 else m.swiglu_added, 1)
    turn_back_tensor(nc, pe, m, "l1fy", "l1fz")


def l1_ffn_scalar(nc, act, m):
    turn_scalar(nc, act, m, "l1fn")
    for k in range(2 * F1 // P):
        act.wait_ge(m.swiglu_ready, k + 1)
        wait(act, m.swiglu_added, k - 3)
        nc.scalar.activation(m.hidden[:, k % 4, :], m.ps[2 * (k % 2)], ACT.Exp, scale=-1.0).then_inc(m.swiglu_exp, 1)
    copy_out_scalar(nc, act, m, "l1fy", m.y_t)


def l1_ffn_vector(nc, dve, m):
    d = m.dve
    norm_to_turn(nc, dve, m, m.x)
    dve.wait_ge(m.ints_in, 16)
    nc.vector.tensor_scalar(m.cast_w, m.ints[:, :], float(INT_SCALE), None, ALU.mult).then_inc(m.ints_cast, 1)
    for k in range(2 * F1 // P):
        h = m.hidden[:, k % 4, :]
        gate, up = m.ps[2 * (k % 2)], m.ps[2 * (k % 2) + 1]
        dve.wait_ge(m.swiglu_exp, k + 1)
        d.done(nc.vector.tensor_scalar(h, h, 1.0, None, ALU.add))
        d.done(nc.vector.reciprocal(h, h))
        d.done(nc.vector.tensor_tensor(h, h, gate, ALU.mult))
        nc.vector.tensor_tensor(h, h, up, ALU.mult).then_inc(m.swiglu_done, 1)
    add_to_x(nc, dve, m, "l1fz")


def one_norm_gpsimd(nc, pool, m):
    norm_gpsimd(nc, pool, m)



def l2_attn_tensor(nc, pe, m):
    w = m.w["l2a"]
    pe.wait_ge(m.loaded["l2a"], 16)
    turn_tensor(nc, pe, m, "l2an")
    turned(m, pe, "l2an")
    for name, wt in (("l2aq", w["wq"]), ("l2ak", w["wk"])):
        for j in range(2):
            bank = fill(m, pe, f"{name}{j}")
            nc.tensor.matmul(bank[:, :], wt, m.xn_t[:, j * S:(j + 1) * S], start=True,
                             stop=True).then_inc(filled(m, f"{name}{j}"), 1)
    tokens_tensor(nc, pe, m, "l2av", m.xn_t, w["wv"])
    for name in ("l2aq", "l2ak", "l2av"):
        for j in range(2):
            copied(m, pe, f"{name}{j}")

    def values(pe, b, qt):
        bank = fill(m, pe, f"l2ao{b}") if qt == 0 else m.ps[6 + b]
        for kt in range(NQ):
            last = nc.tensor.matmul(bank[:, qt * P:(qt + 1) * P], m.pt[:, b, kt, qt * P:(qt + 1) * P],
                                    m.v[:, b * NQ + kt, :], start=kt == 0, stop=kt == NQ - 1)
        if qt == NQ - 1:
            last.then_inc(filled(m, f"l2ao{b}"), 1)

    a = Attention(m.steps0["l2a"], m.half0["l2a"], steps=B * NQ, group=1, keys=lambda qt: S,
                        q=lambda u, qt: m.q_t[:, u * S + qt * P:u * S + (qt + 1) * P],
                        k=lambda u, keys: m.k_t[:, u * S:(u + 1) * S], values=values)
    attend_tensor(nc, pe, m, a)
    attend_tensor(nc, pe, m, None, a)
    project_out_tensor(nc, pe, m, "l2ao", "l2ay", w["wo"])


def l2_attn_scalar(nc, act, m):
    turn_scalar(nc, act, m, "l2an")
    for name, dst, scale in (("l2aq", m.q_t, float(np.float32(1.0) / np.sqrt(np.float32(P // H)))), ("l2ak", m.k_t, 1.0)):
        for j in range(2):
            bank = read(m, act, f"{name}{j}")
            nc.scalar.activation(dst[:, j * S:(j + 1) * S], bank[:, :], ACT.Copy,
                                 scale=scale).then_inc(emptied(m, f"{name}{j}"), 1)
    for j in range(2):
        bank = read(m, act, f"l2av{j}")
        nc.scalar.activation(m.v[:, 4 * j:4 * j + 4, :], bank[:, :].rearrange("p (t d) -> p t d", d=P),
                             ACT.Copy).then_inc(emptied(m, f"l2av{j}"), 1)
    a = Attention(m.steps0["l2a"], m.half0["l2a"], steps=B * NQ, group=1, keys=lambda qt: S,
                  group_done=lambda eng, g: None)
    attend_scalar(nc, act, m, a)
    attend_scalar(nc, act, m, None, a)
    for b in range(B):
        bank = read(m, act, f"l2ao{b}")
        nc.scalar.activation(m.o_t[:, b * S:(b + 1) * S].rearrange("p (h q) -> p q h", q=NQ),
                             bank[:, :].rearrange("p (q h) -> p q h", q=NQ), ACT.Copy).then_inc(emptied(m, f"l2ao{b}"), 1)


def l2_attn_vector(nc, dve, m):
    w = m.w["l2a"]
    norm_to_turn(nc, dve, m, m.x)
    dve.wait_ge(m.loaded["l2a"], 16)
    dve.wait_ge(m.xn_ready, m.turns_dve)
    m.dve.done(nc.vector.tensor_tensor(m.x[:, :, :], m.x[:, :, :], over_tiles(w["bo"]), ALU.add))
    a = Attention(m.steps0["l2a"], m.half0["l2a"], steps=B * NQ, group=1, keys=lambda qt: S,
                  group_done=lambda eng, g: None)
    attend_vector(nc, dve, m, a)
    attend_vector(nc, dve, m, None, a)
    add_to_x(nc, dve, m, "l2ay")



def narrow_cross(stage, clip=None):
    a = Cross(SC, clip)

    def start(m):
        a.s0, a.x0, a.v0 = m.steps0[stage], m.cross0[stage], m.values0[stage]
        return m.w[stage]

    def tensor(nc, pe, m):
        w = start(m)
        pe.wait_ge(m.loaded[stage], 16)
        bank = fill(m, pe, f"{stage}k0")
        nc.tensor.matmul(bank[:, 0:B * SC], w["wk"][0:DC, :], m.context_t[0:DC, :], start=True,
                         stop=True).then_inc(filled(m, f"{stage}k0"), 1)
        bank = fill(m, pe, f"{stage}v0")
        for b in range(B):
            last = nc.tensor.matmul(bank[0:SC, b * P:(b + 1) * P], m.context_t[0:DC, b * SC:(b + 1) * SC], w["wv"][0:DC, :],
                                    start=True, stop=True)
        last.then_inc(filled(m, f"{stage}v0"), 1)
        turn_tensor(nc, pe, m, f"{stage}n")
        turned(m, pe, f"{stage}n")
        for j in range(2):
            bank = fill(m, pe, f"{stage}q{j}")
            nc.tensor.matmul(bank, w["wq"], m.xn_t[:, j * S:(j + 1) * S], start=True,
                             stop=True).then_inc(filled(m, f"{stage}q{j}"), 1)
        for j in range(2):
            copied(m, pe, f"{stage}q{j}")
        pe.wait_ge(m.narrow_keys, a.v0 // 2 + 1)

        def scores(bank, b, half, j, qt):
            at = (8 * half + 4 * j) * SC
            return nc.tensor.matmul(bank[:, 0:4 * SC], m.q_t[:, b * S + qt * P:b * S + (qt + 1) * P],
                                    m.keys_own[:, b, at:at + 4 * SC], start=True, stop=True)

        def values(pe, b, half, i):
            if i == 0:
                pe.wait_ge(m.narrow_values, a.v0 // 2 + 1)
            bank = fill(m, pe, f"{stage}o{b}") if half == 0 and i == 0 else m.ps[6 + b]
            for h in (2 * i, 2 * i + 1):
                last = nc.tensor.matmul(bank, m.values_own[0:SC, b, 8 * half + h, :], m.xpt[0:SC, half, h, :],
                                        start=half == 0 and h == 0, stop=half == 1 and h == 7, skip_group_check=True)
            if i == 3:
                last.then_inc(filled(m, f"{stage}o{b}") if half else m.pv_done, 1)

        a.scores, a.values = scores, values
        cross_tensor(nc, pe, m, a)
        if clip:
            bank = fill(m, pe, f"{stage}g0")
            for b in range(B):
                nc.tensor.matmul(bank[:, b:b + 1], m.context_kv[0:SC, b, 0:P], m.share[0:SC, :], start=True, stop=True)
            pe.wait_ge(m.sums_are_numbers, 1)
            nc.tensor.transpose(bank[0:1, P:2 * P], m.number[:, 0:1], m.ident[:, :]).then_inc(filled(m, f"{stage}g0"), 1)
            pe.wait_ge(m.sums_are_numbers, 2)
            bank = fill(m, pe, f"{stage}h0")
            nc.tensor.matmul(bank[:, 0:1], m.ones_row[0:1, :], m.number[0:1, 1:2], start=True,
                             stop=True).then_inc(filled(m, f"{stage}h0"), 1)
            pe.wait_ge(m.sums_are_numbers, 3)
        project_out_tensor(nc, pe, m, f"{stage}o", f"{stage}y", w["wo"])

    def scalar(nc, act, m):
        w = start(m)
        act.wait_ge(m.loaded[stage], 16)
        bank = read(m, act, f"{stage}k0")
        nc.scalar.activation(m.context_k[:, :], bank[:, 0:B * SC], ACT.Identity,
                             bias=w["bk"]).then_inc(emptied(m, f"{stage}k0"), 1)
        turn_scalar(nc, act, m, f"{stage}n")
        for j in range(2):
            bank = read(m, act, f"{stage}q{j}")
            nc.scalar.activation(m.q_t[:, j * S:(j + 1) * S], bank, ACT.Identity,
                                 bias=w["bq"]).then_inc(emptied(m, f"{stage}q{j}"), 1)

        def unit_done(act, b, half):
            if half:
                read(m, act, f"{stage}o{b}")
            else:
                act.wait_ge(m.pv_done, m.pv0 + a.v0 + b + 1)

        a.unit_done = unit_done
        cross_scalar(nc, act, m, a)
        copy_out_scalar(nc, act, m, f"{stage}o", m.o_t)

    def vector(nc, dve, m):
        w, d = start(m), m.dve
        dve.wait_ge(m.loaded[stage], 16)
        norm_to_turn(nc, dve, m, m.x)
        copied(m, dve, f"{stage}k0")
        for b in range(B):
            shape = [P, H, SC]
            last = nc.vector.tensor_tensor(
                m.keys_own[:, b, 0:H * SC].rearrange("p (h k) -> p h k", k=SC),
                m.context_k[:, b * SC:(b + 1) * SC].rearrange("p (o k) -> p o k", o=1).broadcast_to(shape),
                m.rows8[:, 0:H].rearrange("p (h o) -> p h o", o=1).broadcast_to(shape), ALU.mult)
        last.then_inc(m.narrow_keys, 1)
        bank = read(m, dve, f"{stage}v0")
        nc.vector.tensor_tensor(m.context_kv[0:SC, :, 0:P], bank[0:SC, 0:B * P].rearrange("p (b d) -> p b d", b=B),
                                over_tiles(w["bv"], B)[0:SC], ALU.add).then_inc(emptied(m, f"{stage}v0"), 1)
        dve.wait_ge(m.xn_ready, m.turns_dve)
        d.done(nc.vector.tensor_tensor(m.x[:, :, :], m.x[:, :, :], over_tiles(w["bo"]), ALU.add))
        cross_vector(nc, dve, m, a)
        if clip:
            d.done(nc.vector.tensor_tensor(m.numbers[:, :], m.xsum[:, :], m.xsum[:, :], ALU.is_equal))
            nc.vector.tensor_reduce(m.number[:, 0:1], m.numbers[:, :], AX.X, ALU.min).then_inc(m.sums_are_numbers, 1)
            bank = read(m, dve, f"{stage}g0")
            nc.vector.tensor_copy(m.average[:, :], bank[:, 0:B])
            d.done(nc.vector.tensor_reduce(m.number[0:1, 1:2], bank[0:1, P:2 * P], AX.X, ALU.min))
            nc.vector.engine_nop().then_inc(emptied(m, f"{stage}g0"), 1)
            nc.vector.engine_nop().then_inc(m.sums_are_numbers, 1)
            bank = read(m, dve, f"{stage}h0")
            nc.vector.tensor_scalar(m.number[:, 2:3], bank[:, 0:1], 0.5, None, ALU.is_lt).then_inc(emptied(m, f"{stage}h0"), 1)
            copied(m, dve, f"{stage}h0")
            for b in range(B):
                copied(m, dve, f"{stage}o{b}")
            for b in range(B):
                last = nc.vector.copy_predicated(m.o_t[:, b * S:(b + 1) * S],
                                                 m.number[:, 2:3].bitcast(U32).broadcast_to([P, S]),
                                                 m.average[:, b:b + 1].broadcast_to([P, S]))
            last.then_inc(m.sums_are_numbers, 1)
        add_to_x(nc, dve, m, f"{stage}y")

    def gpsimd(nc, pool, m):
        start(m)
        norm_gpsimd(nc, pool, m)
        copied(m, pool, f"{stage}v0")
        for b in range(B):
            last = nc.gpsimd.tensor_tensor(m.values_own[0:SC, b, :, :],
                                           m.context_kv[0:SC, b, 0:P].rearrange("p (o d) -> p o d", o=1).broadcast_to([SC, H, P]),
                                           m.cols8[0:SC, 0:H, :], ALU.mult)
        last.then_inc(m.narrow_values, 1)
        cross_gpsimd(nc, pool, m, a)

    return stage, tensor, scalar, vector, gpsimd, None



E2, F2 = 16, 512
CAP = T // E2
LAG2 = 2
HIDDEN_BANKS = (0, 1, 4, 5)
SLOT_W = 2 * F2 + F2 // P + P


def l2_ffn_sync(nc, sp, m, dram):
    sp.wait_ge(m.ints_cast, 1)
    stream_sync(sp, m, dram["s_l2f"], E2 // 4, lambda i, s: sp.wait_ge(m.expert_taken, 4 * (i - 1) + s + 1), slots=4)


def l2_ffn_tensor(nc, pe, m):
    w = m.w["l2f"]
    pe.wait_ge(m.loaded["l2f"], 16)
    turn_tensor(nc, pe, m, "l2fn")
    turned(m, pe, "l2fn")
    for j in range(2):
        bank = fill(m, pe, f"l2fr{j}")
        nc.tensor.matmul(bank[0:E2, :], w["router"], m.xn_t[:, j * S:(j + 1) * S], start=True,
                         stop=True).then_inc(filled(m, f"l2fr{j}"), 1)
    for name, src in (("l2fl0", m.logits), ("l2fp0", m.places)):
        if name == "l2fl0":
            for j in range(2):
                copied(m, pe, f"l2fr{j}")
        else:
            pe.wait_ge(m.places_ready, 1)
        bank = fill(m, pe, name)
        for t in range(NT):
            last = nc.tensor.transpose(bank[:, t * E2:(t + 1) * E2], src[0:E2, t * P:(t + 1) * P], m.ident[0:E2, 0:E2])
        last.then_inc(filled(m, name), 1)
    for j in range(2):
        fill(m, pe, f"l2fx{j}")
    for t in range(NT):
        pe.wait_ge(m.chosen_ready, t + 1)
        for j in range(2):
            last = nc.tensor.matmul(m.ps[m.items[f"l2fx{j}"][0]], m.xn[:, t, :], m.wide[:, t, j * S:(j + 1) * S],
                                    start=t == 0, stop=t == NT - 1, skip_group_check=True)
            if t == NT - 1:
                last.then_inc(filled(m, f"l2fx{j}"), 1)
    for j in range(2):
        copied(m, pe, f"l2fx{j}")
    g0 = m.slot0["l2f"]

    with pe.Fori(0, E2 // 4) as i:
        for k in range(4 + LAG2):
            s = k
            if s < 4:
                pe.wait_ge(m.slot_in[s], 16 * (i + 1 + (g0 if s < 2 else 0)))
                for c in range(F2 // P):
                    last = nc.tensor.matmul(m.ps[HIDDEN_BANKS[s]][:, c * CAP:(c + 1) * CAP], m.slot[s][:, c * P:(c + 1) * P],
                                            m.chosen_t[:, bass.ds((4 * i + s) * CAP, CAP)], start=True, stop=True)
                last.then_inc(m.expert_hidden, 1)
            s = k - LAG2
            if s >= 0:
                pe.wait_ge(m.expert_gelu, 4 * i + s + 1)
                if s >= 2:
                    pe.wait_ge(m.expert_taken, 4 * i + s - 1)
                half = 64 * (s % 2)
                for c in range(F2 // P):
                    last = nc.tensor.matmul(m.ps[2 + s % 2][half:half + CAP, 0:P], m.expert_h[:, s, c * CAP:(c + 1) * CAP],
                                            m.slot[s][:, F2 + c * P:F2 + (c + 1) * P], start=c == 0, stop=c == F2 // P - 1)
                last.then_inc(m.expert_y_ready, 1)
        pe.wait_ge(m.expert_taken, 4 * (i + 1) - 1)
    for n in range(2 * NT):
        t, j = divmod(n, 2)
        pe.wait_ge(m.weighted_ready, NT)
        bank = fill(m, pe, f"l2fw{n}")
        for g in range(4):
            last = nc.tensor.transpose(bank[:, g * P:(g + 1) * P], m.weighted[:, t, (4 * j + g) * P:(4 * j + g + 1) * P],
                                       m.ident[:, :])
        last.then_inc(filled(m, f"l2fw{n}"), 1)
    for n in (2 * NT - 2, 2 * NT - 1):
        copied(m, pe, f"l2fw{n}")
    pe.wait_ge(m.expert_taken, E2)
    for j in range(2):
        bank = fill(m, pe, f"l2fy{j}")
        for g in range(E2 // 2):
            last = nc.tensor.matmul(bank, m.v[:, g, :], m.wide[:, g, j * S:(j + 1) * S], start=g == 0,
                                    stop=g == E2 // 2 - 1)
        last.then_inc(filled(m, f"l2fy{j}"), 1)
    turn_back_tensor(nc, pe, m, "l2fy", "l2fz")


def l2_ffn_scalar(nc, act, m):
    w = m.w["l2f"]
    act.wait_ge(m.loaded["l2f"], 16)
    turn_scalar(nc, act, m, "l2fn")
    for j in range(2):
        bank = read(m, act, f"l2fr{j}")
        nc.scalar.activation(m.logits[0:E2, j * S:(j + 1) * S], bank[0:E2, :], ACT.Identity,
                             bias=w["router_b"][0:E2, :]).then_inc(emptied(m, f"l2fr{j}"), 1)
    act.wait_ge(m.router_less_max, 2)
    nc.scalar.activation(m.probs16[:, :, :], m.probs16[:, :, :], ACT.Exp).then_inc(m.router_exp, 1)
    for j in range(2):
        bank = read(m, act, f"l2fx{j}")
        nc.scalar.activation(m.chosen_t[:, j * S:(j + 1) * S], bank, ACT.Copy).then_inc(emptied(m, f"l2fx{j}"), 1)

    with act.Fori(0, E2 // 4) as i:
        for s in range(4):
            act.wait_ge(m.expert_biased, 4 * i + s + 1)
            h = m.expert_h[:, s, :]
            nc.scalar.activation(h, h, ACT.Gelu).then_inc(m.expert_gelu, 1)
    for n in range(0, 2 * NT, 2):
        take_weighted(lambda out, in_: nc.scalar.activation(out, in_, ACT.Copy), act, m, n)
    copy_out_scalar(nc, act, m, "l2fy", m.y_t)


def take_weighted(copy, eng, m, n):
    t, j = divmod(n, 2)
    bank = read(m, eng, f"l2fw{n}")
    copy(m.wide[:, 4 * j:4 * j + 4, t * P:(t + 1) * P],
         bank.rearrange("p (g q) -> p g q", q=P)).then_inc(emptied(m, f"l2fw{n}"), 1)


def l2_ffn_vector(nc, dve, m):
    w, d = m.w["l2f"], m.dve
    dve.wait_ge(m.loaded["l2f"], 16)
    d.done(norm_vector(nc, dve, m, m.x, m.xn))
    d.done(nc.vector.tensor_tensor(m.squares, m.xn[:, :, :], m.xn[:, :, :], ALU.mult))
    d.done(nc.vector.tensor_reduce(m.per_token[:, 0, :], m.squares, AX.X, ALU.add))
    nc.vector.tensor_scalar(m.var[:, :], m.per_token[:, 0, :], 1.0 / P, 1e-5, ALU.mult, ALU.add).then_inc(m.var_ready, 1)
    m.norms += 1
    dve.wait_ge(m.rstd_ready, m.norms)
    d.done(nc.vector.tensor_tensor(m.xn[:, :, :], m.xn[:, :, :],
                                   m.rstd[:, :].rearrange("p (t o) -> p t o", o=1).broadcast_to([P, NT, P]), ALU.mult))
    nc.vector.tensor_tensor(m.xn[:, :, :], m.xn[:, :, :], over_tiles(w["norm_w"]), ALU.mult).then_inc(m.xn_ready, 2)
    m.turns_dve += 2
    for j in range(2):
        copied(m, dve, f"l2fr{j}")
    src = m.logits[0:E2, :]
    for r in range(CAP // 8):
        d.done(nc.vector.max(m.top8[0:E2, r % 2, :], src))
        if r < CAP // 8 - 1:
            d.done(nc.vector.match_replace(m.left[0:E2, :], m.top8[0:E2, r % 2, :], src, -BIG))
            src = m.left[0:E2, :]
    limit = m.top8[0:E2, (CAP // 8 - 1) % 2, 7:8]
    above, level, count = m.left[0:E2, :], m.places[0:E2, :], m.running[0:E2, :]
    one = m.ones_col[0:E2, 0:1].broadcast_to([E2, T])
    d.done(nc.vector.tensor_scalar(above, m.logits[0:E2, :], limit, None, ALU.is_gt))
    d.done(nc.vector.tensor_reduce(m.needed[0:E2, 0:1], above, AX.X, ALU.add))
    d.done(nc.vector.tensor_scalar(m.needed[0:E2, 1:2], m.needed[0:E2, 0:1], -1.0, float(CAP), ALU.mult, ALU.add))
    d.done(nc.vector.tensor_scalar(level, m.logits[0:E2, :], limit, None, ALU.is_equal))
    d.done(nc.vector.tensor_tensor_scan(count, one, level, 0.0, ALU.mult, ALU.add))
    d.done(nc.vector.tensor_scalar(count, count, m.needed[0:E2, 1:2], None, ALU.is_le))
    d.done(nc.vector.tensor_tensor(level, level, count, ALU.mult))
    d.done(nc.vector.tensor_tensor(above, above, level, ALU.add))
    d.done(nc.vector.tensor_tensor_scan(count, one, above, 0.0, ALU.mult, ALU.add))
    nc.vector.tensor_tensor(level, count, above, ALU.mult).then_inc(m.places_ready, 1)
    probs = m.probs16[:, :, :]
    last16 = lambda ap: ap.rearrange("p (t o) -> p t o", o=1).broadcast_to([P, NT, E2])
    bank = read(m, dve, "l2fl0")
    logits = bank[:, 0:NT * E2].rearrange("p (t e) -> p t e", e=E2)
    d.done(nc.vector.tensor_reduce(m.per_token[:, 1, :], logits, AX.X, ALU.max))
    nc.vector.tensor_tensor(probs, logits, last16(m.per_token[:, 1, :]), ALU.subtract).then_inc(emptied(m, "l2fl0"), 1)
    copied(m, dve, "l2fl0")
    nc.vector.engine_nop().then_inc(m.router_less_max, 1)
    bank = read(m, dve, "l2fp0")
    nc.vector.tensor_copy(m.place[:, :, :], bank[:, 0:NT * E2].rearrange("p (t e) -> p t e", e=E2)).then_inc(
        emptied(m, "l2fp0"), 1)
    copied(m, dve, "l2fp0")
    for t in range(NT):
        shape = [P, E2, CAP]
        nc.vector.tensor_tensor(m.wide[:, t, :].rearrange("p (e s) -> p e s", s=CAP),
                                w["one_to_cap"].rearrange("p (o s) -> p o s", o=1).broadcast_to(shape),
                                m.place[:, t, :].rearrange("p (e o) -> p e o", o=1).broadcast_to(shape),
                                ALU.is_equal).then_inc(m.chosen_ready, 1)
    dve.wait_ge(m.router_exp, 2)
    d.done(nc.vector.tensor_reduce(m.per_token[:, 2, :], probs, AX.X, ALU.add))
    d.done(nc.vector.reciprocal(m.per_token[:, 3, :], m.per_token[:, 2, :]))
    d.done(nc.vector.tensor_tensor(probs, probs, last16(m.per_token[:, 3, :]), ALU.mult))
    d.done(nc.vector.tensor_scalar(m.place[:, :, :], m.place[:, :, :], 0.5, None, ALU.is_gt))
    nc.vector.tensor_tensor(m.place[:, :, :], m.place[:, :, :], probs, ALU.mult).then_inc(m.gates_ready, 1)
    dve.wait_ge(m.gates_ready, 2)
    d.done(nc.vector.tensor_reduce(m.per_token[:, 0, :], m.place[:, :, :], AX.X, ALU.add))
    d.done(nc.vector.tensor_scalar(m.per_token[:, 1, :], m.per_token[:, 0, :], 0.0, None, ALU.is_le))
    d.done(nc.vector.tensor_tensor(m.per_token[:, 0, :], m.per_token[:, 0, :], m.per_token[:, 1, :], ALU.add))
    d.done(nc.vector.reciprocal(m.per_token[:, 1, :], m.per_token[:, 0, :]))

    with dve.Fori(0, E2 // 4) as i:
        for k in range(4 + LAG2):
            s = k
            if s < 4:
                dve.wait_ge(m.expert_hidden, 4 * i + s + 1)
                bias = m.slot[s][:, 2 * F2:2 * F2 + F2 // P].rearrange("p (c o) -> p c o", o=1)
                nc.vector.tensor_tensor(m.expert_h[:, s, :].rearrange("p (c n) -> p c n", n=CAP),
                                        m.ps[HIDDEN_BANKS[s]][:, 0:F2 // P * CAP].rearrange("p (c n) -> p c n", n=CAP),
                                        bias.broadcast_to([P, F2 // P, CAP]), ALU.add).then_inc(m.expert_biased, 1)
            s = k - LAG2
            if s >= 0:
                dve.wait_ge(m.expert_y_ready, 4 * i + s + 1)
                own = slice(64 * (s % 2), 64 * (s % 2) + CAP)
                nc.vector.tensor_tensor(m.v[own, bass.ds(2 * i + s // 2, 1), :].rearrange("p o d -> p (o d)"),
                                        m.ps[2 + s % 2][own, 0:P], m.slot[s][own, SLOT_W - P:SLOT_W],
                                        ALU.add).then_inc(m.expert_taken, 1)
    for n in range(1, 2 * NT, 2):
        take_weighted(nc.vector.tensor_copy, dve, m, n)
    for j in range(2):
        bank = read(m, dve, f"l2fz{j}")
        tiles = slice(4 * j, 4 * j + 4)
        nc.vector.tensor_tensor(m.xn[:, tiles, :], bank.rearrange("p (t d) -> p t d", d=P),
                                m.per_token[:, 1, tiles].rearrange("p (t o) -> p t o", o=1).broadcast_to([P, 4, P]),
                                ALU.mult).then_inc(emptied(m, f"l2fz{j}"), 1)
    for j in range(2):
        copied(m, dve, f"l2fz{j}")
    d.done(nc.vector.tensor_tensor(m.x[:, :, :], m.x[:, :, :], m.xn[:, :, :], ALU.add))


def l2_ffn_gpsimd(nc, pool, m):
    norm_gpsimd(nc, pool, m)
    norm_gpsimd(nc, pool, m)
    pool.wait_ge(m.gates_ready, 2)
    for t in range(NT):
        shape = [P, E2, CAP]
        pool.wait_ge(m.chosen_ready, t + 1)
        split = lambda ap: ap.rearrange("p (e s) -> p e s", s=CAP)
        nc.gpsimd.tensor_tensor(split(m.weighted[:, t, :]), split(m.wide[:, t, :]),
                                m.place[:, t, :].rearrange("p (e o) -> p e o", o=1).broadcast_to(shape),
                                ALU.mult).then_inc(m.weighted_ready, 1)



DK, DV = 4, 8
QKVG = 2 * H * DK + 2 * P
TAPS = 4
FAR = -87.0


def per_head(ap, width):
    return ap.rearrange("p t (h d) -> p t h d", d=width)


def over_head(ap, width):
    t = ap.shape[1]
    return ap.rearrange("p t (h o) -> p t h o", o=1).broadcast_to([P, t, H, width])


def l3_attn_tensor(nc, pe, m):
    w = m.w["l3a"]
    pe.wait_ge(m.loaded["l3a"], 16)
    turn_tensor(nc, pe, m, "l3an")
    pe.wait_ge(m.conv_done, 1)
    for t in range(NT):
        bank = fill(m, pe, f"l3ap{t}")
        nc.tensor.matmul(bank[:, 0:QKVG], m.k_t[:, t * P:(t + 1) * P], w["wqkvg"], start=True,
                         stop=True).then_inc(filled(m, f"l3ap{t}"), 1)
    turn_tensor(nc, pe, m, "l3am")
    turned(m, pe, "l3am")
    tokens_tensor(nc, pe, m, "l3ay", m.xn_t, w["wo"])


def l3_attn_scalar(nc, act, m):
    turn_scalar(nc, act, m, "l3an")
    act.wait_ge(m.gla_ready, 1)
    nc.scalar.activation(m.q_t[:, :], m.q_t[:, :], ACT.Exp, scale=-1.0).then_inc(m.gla_exp, 1)
    for t in range(NT):
        bank = read(m, act, f"l3ap{t}")
        nc.scalar.activation(m.wide[:, t, 0:QKVG], bank[:, 0:QKVG], ACT.Copy).then_inc(emptied(m, f"l3ap{t}"), 1)
    decay = m.gla["decay"]
    act.wait_ge(m.gla_ready, 2)
    nc.scalar.activation(decay, decay, ACT.Exp, scale=-1.0).then_inc(m.gla_exp, 1)
    act.wait_ge(m.gla_exp, 2)
    nc.scalar.activation(decay, decay, ACT.Ln, bias=m.ones_col[:, :]).then_inc(m.gla_exp, 1)
    act.wait_ge(m.gla_ready, 3)
    nc.scalar.activation(decay, decay, ACT.Exp, scale=1.0 / 16.0).then_inc(m.gla_exp, 1)
    act.wait_ge(m.gla_ready, 4)
    nc.scalar.activation(m.gla["sig_g"], m.gla["sig_g"], ACT.Exp, scale=-1.0).then_inc(m.gla_exp, 1)
    act.wait_ge(m.gla_ready, 5)
    nc.scalar.activation(m.gla["aug"], m.gla["aug"], ACT.Exp, scale=-1.0).then_inc(m.gla_exp, 1)
    act.wait_ge(m.head_var_ready, 1)
    nc.scalar.activation(m.probs16[:, :, :], m.probs16[:, :, :], ACT.Sqrt).then_inc(m.head_rstd_ready, 1)
    turn_scalar(nc, act, m, "l3am")


def l3_attn_vector(nc, dve, m):
    w, d, g = m.w["l3a"], m.dve, m.gla
    tt, ts = nc.vector.tensor_tensor, nc.vector.tensor_scalar
    dve.wait_ge(m.loaded["l3a"], 16)
    norm_to_turn(nc, dve, m, m.x)
    for j in range(2):
        copied(m, dve, f"l3an{j}")
    y, e = m.k_t, m.q_t
    d.done(ts(y[:, :], m.xn_t[:, :], w["conv"][:, TAPS - 1:TAPS], None, ALU.mult))
    d.done(ts(e[:, 0:S], m.xn_t[:, 0:S], w["conv"][:, TAPS - 2:TAPS - 1], None, ALU.mult))
    d.done(tt(y[:, S:T], y[:, S:T], e[:, 0:S], ALU.add))
    ts(e[:, :], y[:, :], FAR, None, ALU.max).then_inc(m.gla_ready, 1)
    dve.wait_ge(m.gla_exp, 1)
    d.done(ts(e[:, :], e[:, :], 1.0, None, ALU.add))
    d.done(nc.vector.reciprocal(e[:, :], e[:, :]))
    tt(y[:, :], y[:, :], e[:, :], ALU.mult).then_inc(m.conv_done, 1)
    for t in range(NT):
        copied(m, dve, f"l3ap{t}")
    q, gate, v, decay, k = g["q"], g["gate"], g["v"], g["decay"], g["k"]
    d.done(ts(k, gate, -1.0, None, ALU.mult))
    tt(decay, gate, k, ALU.max).then_inc(m.gla_ready, 1)
    dve.wait_ge(m.gla_ready, 2)
    d.done(ts(k, gate, 0.0, None, ALU.min))
    dve.wait_ge(m.gla_exp, 3)
    tt(decay, k, decay, ALU.subtract).then_inc(m.gla_ready, 1)
    d.done(tt(g["g"], g["g"], over_tiles(w["bg"]), ALU.add))
    ts(g["sig_g"], g["g"], FAR, None, ALU.max).then_inc(m.gla_ready, 1)
    dve.wait_ge(m.gla_exp, 4)
    d.done(ts(k, decay, -1.0, 1.0, ALU.mult, ALU.add))
    qk, own, past = g["qk"], m.place[:, :, :], m.probs16[:, NQ:NT, :]
    d.done(tt(qk, q, k, ALU.mult))
    d.done(nc.vector.tensor_reduce(own, per_head(qk, DK), AX.X, ALU.add))
    d.done(tt(qk, qk, over_tiles(w["aug_balance"]), ALU.mult))
    d.done(nc.vector.tensor_reduce(m.probs16[:, :, :], per_head(qk, DK), AX.X, ALU.add))
    d.done(tt(per_head(g["aug"], DV), over_head(m.probs16[:, :, :], DV), per_head(v, DV), ALU.mult))
    ts(g["aug"], g["aug"], FAR, None, ALU.max).then_inc(m.gla_ready, 1)
    dve.wait_ge(m.gla_ready, 5)
    d.done(ts(own, own, DK ** -0.5, None, ALU.mult))
    d.done(tt(per_head(g["o"], DV), over_head(own, DV), per_head(v, DV), ALU.mult))
    second = slice(NQ, NT)
    d.done(tt(qk[:, second], q[:, second], decay[:, second], ALU.mult))
    d.done(tt(qk[:, second], qk[:, second], k[:, 0:NQ], ALU.mult))
    d.done(nc.vector.tensor_reduce(past, per_head(qk[:, second], DK), AX.X, ALU.add))
    d.done(ts(past, past, DK ** -0.5, None, ALU.mult))
    d.done(tt(per_head(g["tmp"][:, second], DV), over_head(past, DV), per_head(v[:, 0:NQ], DV), ALU.mult))
    d.done(tt(g["o"][:, second], g["o"][:, second], g["tmp"][:, second], ALU.add))
    dve.wait_ge(m.gla_exp, 6)
    for part in ("aug", "sig_g"):
        d.done(ts(g[part], g[part], 1.0, None, ALU.add))
        d.done(nc.vector.reciprocal(g[part], g[part]))
    o = g["o"]
    d.done(tt(o, o, g["aug"], ALU.add))
    mean, var = m.place[:, :, :], m.probs16[:, :, :]
    d.done(nc.vector.tensor_reduce(mean, per_head(o, DV), AX.X, ALU.add))
    d.done(ts(mean, mean, 1.0 / DV, None, ALU.mult))
    d.done(tt(per_head(o, DV), per_head(o, DV), over_head(mean, DV), ALU.subtract))
    d.done(tt(g["tmp"], o, o, ALU.mult))
    d.done(nc.vector.tensor_reduce(var, per_head(g["tmp"], DV), AX.X, ALU.add))
    d.done(ts(var, var, 1.0 / DV, 1e-5, ALU.mult, ALU.add))
    nc.vector.reciprocal(var, var).then_inc(m.head_var_ready, 1)
    d.done(tt(g["sig_g"], g["sig_g"], g["g"], ALU.mult))
    d.done(tt(o, o, g["sig_g"], ALU.mult))
    dve.wait_ge(m.head_rstd_ready, 1)
    tt(per_head(m.xn[:, :, :], DV), per_head(o, DV), over_head(var, DV), ALU.mult).then_inc(m.xn_ready, 2)
    m.turns_dve += 2
    add_to_x(nc, dve, m, "l3ay")


def l3_attn_gpsimd(nc, pool, m):
    norm_gpsimd(nc, pool, m)



E3, ROT, F3 = 8, 32, 512
GROUPS3 = 4
MIXES = 2 * NT
SPREADS = B * E3


def l3_ffn_sync(nc, sp, m, dram):
    sp.wait_ge(m.expert_taken, E2)
    stream_sync(sp, m, dram["s_l3v"], NPAIR // 2,
                lambda i, s: sp.wait_ge(m.mixed_taken, MIXES * (2 * (i - 1) + s + 1)))
    weights = dram["s_l3q"]

    def one_pass(i):
        for s in range(2):
            if isinstance(i, int):
                sp.wait_ge(m.mixed_gated, MIXES * NPAIR // 2)
                sp.wait_ge(m.mixed_added, MIXES * NPAIR // 2)
                src, values = weights[2 * i + s], m.wide[:, 2 * i + s, :]
            else:
                src = weights[bass.ds(2 * i + s, 1)].rearrange("o p n -> (o p) n")
                values = m.wide[:, bass.ds(2 * i + s, 1), :].rearrange("p o n -> p (o n)")
                sp.wait_ge(m.exp_done, m.steps0["l3f"] + STEPS * (2 * (i - 1) + s) + 1)
            sp.dma_start(m.slots[:, s, 0:S], src).then_inc(m.slot_in[s], 16)
            if not isinstance(i, int):
                read(m, sp, "l3fj1", PAIR3.output(2 * (i - 1) + s))
            sp.dma_start(m.pair_v[s].rearrange("p t d -> p (t d)"), values).then_inc(m.values_in[s], 16)

    one_pass(0)
    with sp.Fori(1, NPAIR // 2) as i:
        one_pass(i)
    sp.wait_ge(m.rope_added, 6 * NPAIR)
    stream_sync(sp, m, dram["s_l3o"], NPAIR // 2,
                lambda i, s: sp.wait_ge(m.spread_used, SPREADS * (2 * (i - 1) + s + 1)))


def l3_ffn_tensor(nc, pe, m):
    w = m.w["l3f"]
    pe.wait_ge(m.loaded["l3f"], 16)
    turn_tensor(nc, pe, m, "l3fn")
    turned(m, pe, "l3fn")
    for n in range(4):
        bank = fill(m, pe, f"l3fs{n}")
        for k in range(2):
            last = nc.tensor.matmul(bank[:, k * 2 * P:(k + 1) * 2 * P], m.xn_t[:, (2 * n + k) * P:(2 * n + k + 1) * P],
                                    w["wsel"], start=True, stop=True)
        last.then_inc(filled(m, f"l3fs{n}"), 1)
    g0 = m.slot0["l3v"]

    with pe.Fori(0, NPAIR // 2) as i:
        for s in range(2):
            pe.wait_ge(m.slot_in[s], 16 * (g0 + i + 1))
            for n in range(MIXES):
                t, h = divmod(n, 2)
                if s > 0 or n >= 4:
                    pe.wait_ge(m.mixed_taken, 2 * MIXES * i + MIXES * s + n - 3)
                nc.tensor.matmul(m.ps[n % 4], m.xn_t[:, t * P:(t + 1) * P], m.slots[:, s, h * S:(h + 1) * S], start=True,
                                 stop=True).then_inc(m.mixed_ready, 1)
        pe.wait_ge(m.mixed_taken, 2 * MIXES * (i + 1))
    pe.wait_ge(m.parts_ready, 1)
    for q in range(GROUPS3):
        for j in range(2):
            bank = fill(m, pe, f"l3fg{2 * q + j}")
            for t in range(4):
                last = nc.tensor.matmul(bank[:, t * P:(t + 1) * P],
                                        m.gate_parts[:, 4 * j + t, q, :, :].rearrange("p c g -> p (c g)"),
                                        m.ident_bf[:, :], start=True, stop=True)
            last.then_inc(filled(m, f"l3fg{2 * q + j}"), 1)
    q0 = m.slot0["l3q"]

    def project(r, s, what):
        pe.wait_ge(m.slot_in[s], 16 * (q0 + r + 1))
        for j in range(2):
            bank = fill(m, pe, f"l3fj{j}", PAIR3.projection(2 * r + s) + what)
            nc.tensor.matmul(bank, m.slots[:, s, what * P:(what + 1) * P], m.xn_t[:, j * S:(j + 1) * S], start=True,
                             stop=True).then_inc(filled(m, f"l3fj{j}"), 1)

    def projected(r, s):
        pe.wait_ge(m.rope_added, 6 * (2 * r + s + 1))
        pe.wait_ge(m.values_in[s], 16 * (r + 1))

    pair_attend_tensor(nc, pe, m, "l3fj", "l3f", False, project, projected)
    for j in range(2):
        copied(m, pe, f"l3fj{j}", PAIR3.uses - 1)
    for j in range(2):
        bank = fill(m, pe, f"l3fy{j}")
        nc.tensor.matmul(bank, m.zeros[:, :], m.xn_t[:, j * S:(j + 1) * S], start=True, stop=False, skip_group_check=True)
    o0 = m.slot0["l3o"]

    with pe.Fori(0, NPAIR // 2) as i:
        base = 2 * SPREADS * i
        for k in range(2 * SPREADS + 2):
            if k < 2 * SPREADS:
                s, e, b = k // SPREADS, k % SPREADS // 2, k % 2
                if k % SPREADS == 0:
                    pe.wait_ge(m.slot_in[s], 16 * (o0 + i + 1))
                if k >= 4:
                    pe.wait_ge(m.spread_gated, base + k - 3)
                nc.tensor.matmul(m.ps[k % 4], m.select[:, s * E3 + e, :],
                                 m.gate_rows[:, bass.ds(i, 1), b * S:(b + 1) * S].rearrange("p o n -> p (o n)"), start=True,
                                 stop=True).then_inc(m.spread_ready, 1)
            q = k - 2
            if q >= 0:
                s, e, b = q // SPREADS, q % SPREADS // 2, q % 2
                pe.wait_ge(m.spread_gated, base + q + 1)
                nc.tensor.matmul(m.ps[6 + b], m.slots[:, s, e * P:(e + 1) * P], m.gated[:, q % 4, :], start=False,
                                 stop=False, skip_group_check=True).then_inc(m.spread_used, 1)
    complete(nc, pe, m, "l3fy")
    turn_back_tensor(nc, pe, m, "l3fy", "l3fz")
    turn_tensor(nc, pe, m, "l3fm")
    turned(m, pe, "l3fm")
    h0, chunks = m.h0["l3f"], F3 // P
    for k in range(2 * chunks + 2):
        if k < 2 * chunks:
            c, j = divmod(k, 2)
            if k >= 4:
                pe.wait_ge(m.hidden_read, h0 + k - 3)
            nc.tensor.matmul(m.ps[k % 4], w["w1"][:, c * P:(c + 1) * P], m.xn_t[:, j * S:(j + 1) * S], start=True,
                             stop=True).then_inc(m.hidden_ready, 1)
        q = k - 2
        if q >= 0:
            c, j = divmod(q, 2)
            pe.wait_ge(m.hidden_read, h0 + q + 1)
            bank = fill(m, pe, f"l3fu{j}") if c == 0 else m.ps[6 + j]
            last = nc.tensor.matmul(bank, w["w2"][:, c * P:(c + 1) * P], m.hidden[:, q % 4, :], start=c == 0,
                                    stop=c == chunks - 1, skip_group_check=True)
            last.then_inc(filled(m, f"l3fu{j}") if c == chunks - 1 else m.hidden_used, 1)
    turn_back_tensor(nc, pe, m, "l3fu", "l3fw")


def l3_ffn_scalar(nc, act, m):
    w = m.w["l3f"]
    act.wait_ge(m.loaded["l3f"], 16)
    turn_scalar(nc, act, m, "l3fn")
    for n in range(4):
        act.wait_ge(m.pick_ready, n + 1)
        part = m.pick[:, n * S:(n + 1) * S]
        nc.scalar.activation(part, part, ACT.Exp, scale=-1.0).then_inc(m.pick_exp, 1)
    for n in range(2 * GROUPS3):
        q, j = divmod(n, 2)
        bank = read(m, act, f"l3fg{n}")
        nc.scalar.activation(m.gate_rows[:, q, j * S:(j + 1) * S], bank, ACT.Copy).then_inc(emptied(m, f"l3fg{n}"), 1)
    pair_attend_scalar(nc, act, m, "l3fj", "l3f", False, lambda r, s, what: None)
    copy_out_scalar(nc, act, m, "l3fy", m.y_t)
    turn_scalar(nc, act, m, "l3fm")
    h0 = m.h0["l3f"]
    for k in range(2 * F3 // P):
        c = k // 2
        act.wait_ge(m.hidden_ready, h0 + k + 1)
        if k >= 4:
            act.wait_ge(m.hidden_used, h0 + k - 3)
        nc.scalar.activation(m.hidden[:, k % 4, :], m.ps[k % 4], ACT.Relu, bias=w["b1"][:, c:c + 1]).then_inc(
            m.hidden_read, 1)
    copy_out_scalar(nc, act, m, "l3fu", m.y_t)


def l3_ffn_vector(nc, dve, m):
    w, d = m.w["l3f"], m.dve
    tt, ts, reduce = nc.vector.tensor_tensor, nc.vector.tensor_scalar, nc.vector.tensor_reduce
    dve.wait_ge(m.loaded["l3f"], 16)
    norm_to_turn(nc, dve, m, m.x)
    for n in range(4):
        bank = read(m, dve, f"l3fs{n}")
        ts(m.pick[:, n * S:(n + 1) * S], bank, FAR, None, ALU.max).then_inc(emptied(m, f"l3fs{n}"), 1)
        copied(m, dve, f"l3fs{n}")
        nc.vector.engine_nop().then_inc(m.pick_ready, 1)
    dve.wait_ge(m.pick_exp, 4)
    u, tmp, first = m.pick, m.pick_tmp, m.pick_first
    experts = lambda ap: ap.rearrange("p (h e) -> p h e", e=E3)
    spread = lambda ap: ap.rearrange("p (h o) -> p h o", o=1).broadcast_to([P, NT * 2 * H, E3])
    falling = w["falling"].rearrange("p (o e) -> p o e", o=1).broadcast_to([P, NT * 2 * H, E3])
    d.done(ts(u, u, 1.0, None, ALU.add))

    def choose(hot, best):
        rank = m.pick_best[:, 0:NT * 2 * H]
        d.done(reduce(best, experts(u), AX.X, ALU.min))
        d.done(tt(experts(hot), experts(u), spread(best), ALU.is_equal))
        d.done(tt(experts(hot), experts(hot), falling, ALU.mult))
        d.done(reduce(rank, experts(hot), AX.X, ALU.max))
        d.done(tt(experts(hot), experts(hot), spread(rank), ALU.is_equal))
        d.done(nc.vector.reciprocal(best, best))

    best1, best2 = (m.pick_best[:, n * NT * 2 * H:(n + 1) * NT * 2 * H] for n in (1, 2))
    choose(first, best1)
    d.done(ts(tmp, first, BIG, None, ALU.mult))
    d.done(tt(u, u, tmp, ALU.max))
    choose(tmp, best2)
    s = u
    d.done(tt(experts(first), experts(first), spread(best1), ALU.mult))
    d.done(tt(experts(tmp), experts(tmp), spread(best2), ALU.mult))
    d.done(tt(s, first, tmp, ALU.add))
    gates = s.rearrange("p (t w g) -> p t w g", w=2, g=P)
    out_gates = gates[:, :, 1, :].rearrange("p t (q g) -> p t q g", q=GROUPS3)
    part = lambda c: m.gate_parts[:, :, :, c, :]
    rest = tmp[:, 0:T].rearrange("p (t q g) -> p t q g", t=NT, q=GROUPS3)
    dve.wait_ge(m.parts_zero, 1)
    d.done(nc.vector.tensor_copy(part(0), out_gates))
    d.done(tt(rest, out_gates, part(0), ALU.subtract))
    d.done(nc.vector.tensor_copy(part(1), rest))
    tt(part(2), rest, part(1), ALU.subtract).then_inc(m.parts_ready, 1)
    dve.wait_ge(m.parts_ready, 1)

    mixed = tmp.rearrange("p (n s) -> p n s", s=S)
    with dve.Fori(0, NPAIR // 2) as i:
        def gather(n):
            s, k = divmod(n, MIXES)
            t, h = divmod(k, 2)
            dve.wait_ge(m.mixed_taken, 2 * MIXES * i + n + 1)
            to = m.wide[:, bass.ds(2 * i + s, 1), t * P + 64 * h:t * P + 64 * h + 64].rearrange("p o d -> p (o d)")
            reduce(to, mixed[:, n % 4, :].rearrange("p (e d) -> p d e", e=E3), AX.X, ALU.add).then_inc(m.mixed_gated, 1)

        for n in range(2 * MIXES):
            s, k = divmod(n, MIXES)
            t, h = divmod(k, 2)
            dve.wait_ge(m.mixed_ready, 2 * MIXES * i + n + 1)
            if n >= 4:
                dve.wait_ge(m.mixed_gated if n % 2 == 0 else m.mixed_added, MIXES * i + n // 2 - 1)
            gate = gates[:, t, 0, bass.ds((2 * (2 * i + s) + h) * E3, E3)]
            tt(mixed[:, n % 4, :].rearrange("p (e d) -> p e d", e=E3), m.ps[n % 4].rearrange("p (e d) -> p e d", e=E3),
               gate.rearrange("p (e o) -> p e o", o=1).broadcast_to([P, E3, 64]), ALU.mult).then_inc(m.mixed_taken, 1)
            if n % 2 == 1:
                gather(n - 1)
        dve.wait_ge(m.mixed_gated, MIXES * (i + 1))
        dve.wait_ge(m.mixed_added, MIXES * (i + 1))
    dve.wait_ge(m.pair_zero, 2)

    def rope(r, s, what):
        keys, partner = divmod(what, 2)
        table = w[("cos_q", "sin_q", "cos", "sin")[what]]
        use, added = PAIR3.projection(2 * r + s) + what, 6 * (2 * r + s)
        for j in range(2):
            bank = read(m, dve, f"l3fj{j}", use)
            tt(m.rope_tmp[:, j, partner, :], bank, table, ALU.mult).then_inc(emptied(m, f"l3fj{j}"), 1)
        if not partner:
            return
        for j in range(2):
            copied(m, dve, f"l3fj{j}", use)
            at = slice(j * S, (j + 1) * S)
            if not keys:
                tt(m.pair_q[s][:, at], m.rope_tmp[:, j, 0, :], m.rope_tmp[:, j, 1, :], ALU.add).then_inc(m.rope_added, 1)
            else:
                for e in range(2):
                    own = slice(64 * e, 64 * e + 64)
                    tt(m.pair_k[own, s, e, at], m.rope_tmp[own, j, 0, :], m.rope_tmp[own, j, 1, :],
                       ALU.add).then_inc(m.rope_added, 1)
        dve.wait_ge(m.rope_added, added + (6 if keys else 2))

    pair_attend_vector(nc, dve, m, "l3fj", "l3f", False, rope)
    with dve.Fori(0, NPAIR // 2) as i:
        for k in range(2 * SPREADS):
            s, b = k // SPREADS, k % 2
            dve.wait_ge(m.spread_ready, 2 * SPREADS * i + k + 1)
            out = m.wide[:, bass.ds(2 * i + s, 1), b * S:(b + 1) * S].rearrange("p o n -> p (o n)")
            tt(m.gated[:, k % 4, :], m.ps[k % 4], out, ALU.mult).then_inc(m.spread_gated, 1)
    add_to(nc, dve, m, "l3fz", m.xn)
    affine_norm(nc, dve, m, w["ln1_g"], w["ln1_b"]).then_inc(m.xn_ready, 2)
    m.turns_dve += 2
    dve.wait_ge(m.xn_ready, m.turns_dve)
    d.done(tt(m.q_tok, m.xn[:, :, :], over_tiles(w["b2"]), ALU.add))
    for j in range(2):
        read(m, dve, f"l3fm{j}")
    d.done(nc.vector.tensor_copy(m.xn[:, :, :], m.q_tok))
    add_to(nc, dve, m, "l3fw", m.xn)
    d.done(affine_norm(nc, dve, m, w["ln2_g"], w["ln2_b"]))
    d.done(tt(m.x[:, :, :], m.x[:, :, :], m.xn[:, :, :], ALU.add))


def affine_norm(nc, dve, m, gain, offset):
    m.dve.done(norm_vector(nc, dve, m, m.xn, m.xn))
    m.dve.done(nc.vector.tensor_tensor(m.xn[:, :, :], m.xn[:, :, :], over_tiles(gain), ALU.mult))
    return nc.vector.tensor_tensor(m.xn[:, :, :], m.xn[:, :, :], over_tiles(offset), ALU.add)


def l3_ffn_gpsimd(nc, pool, m):
    pool.wait_ge(m.stage_done, 11)
    nc.gpsimd.memset(m.gate_parts[:, :, :, :, :], 0.0).then_inc(m.parts_zero, 1)
    nc.gpsimd.memset(m.pair_k[:, :, :, :], 0.0).then_inc(m.pair_zero, 1)
    norm_gpsimd(nc, pool, m)
    mixed = m.pick_tmp.rearrange("p (n s) -> p n s", s=S)
    pairs, fours = m.pick_first[:, 0:4 * 64], m.pick_first[:, 4 * 64:6 * 64]
    add = lambda to, of, n: nc.gpsimd.tensor_tensor(to, of[:, 0:n], of[:, n:2 * n], ALU.add)
    with pool.Fori(0, NPAIR // 2) as i:
        for n in range(1, 2 * MIXES, 2):
            s, t = n // MIXES, n % MIXES // 2
            done = 2 * (MIXES * i + n // 2)
            pool.wait_ge(m.mixed_taken, 2 * MIXES * i + n + 1)
            add(pairs, mixed[:, n % 4, :], 4 * 64).then_inc(m.mixed_halved, 1)
            pool.wait_ge(m.mixed_halved, done + 1)
            add(fours, pairs, 2 * 64).then_inc(m.mixed_halved, 1)
            pool.wait_ge(m.mixed_halved, done + 2)
            to = m.wide[:, bass.ds(2 * i + s, 1), t * P + 64:(t + 1) * P].rearrange("p o d -> p (o d)")
            add(to, fours, 64).then_inc(m.mixed_added, 1)
        pool.wait_ge(m.mixed_added, MIXES * (i + 1))
    for _ in range(2):
        norm_gpsimd(nc, pool, m)



def plan(m):
    m.pv0 = 4 * NPAIR
    m.values0 = {}

    def pair(name):
        item(m, f"{name}0", 6)
        item(m, f"{name}1", 7)

    def narrow(stage, values):
        m.values0[stage] = values
        for name, times in (("k", 1), ("v", 1), ("n", 2), ("q", 2), ("o", 2)):
            run(stage + name, times)
        if stage == "l2x":
            run("l2xg", 1)
            run("l2xh", 1)
        run(stage + "y", 2)

    def run(name, times):
        for n in range(times):
            item(m, f"{name}{n}", 6 + n % 2)

    for name in ("l0n", "l0q", "l0k", "l0v", "l0o", "l0y"):
        pair(name)
    for name, times in (("l0xk", NPAIR), ("l0xv", 2 * B), ("l0xn", 2), ("l0xq", 2 * NPAIR), ("l0xo", 2 * NPAIR),
                        ("l0xy", 2), ("l0xz", 2)):
        run(name, times)
    run("l0fn", 2)
    item(m, "l0fr", 6)
    item(m, "l0fg0", 7)
    item(m, "l0fg1", 6)
    run("l0fy", 2)
    run("l0fz", 2)
    run("l1an", 2)
    run("l1al", 2)
    item(m, "l1aj0", 6, PAIR1.uses)
    item(m, "l1aj1", 7, PAIR1.uses)
    run("l1ay", 2)
    run("l1az", 2)
    for name, times in (("l1xn", 2), ("l1xq", 2), ("l1xk", 2), ("l1xv", 2), ("l1xc", 1), ("l1xd", 2), ("l1xqt", 2),
                        ("l1xkt", 2), ("l1xct", 1), ("l1xo", 2), ("l1xy", 2)):
        run(name, times)
    run("l1fn", 2)
    run("l1fy", 2)
    run("l1fz", 2)
    for name in ("n", "q", "k", "v", "o", "y"):
        run(f"l2a{name}", 2)
    narrow("l2x", 0)
    for name, times in (("l2fn", 2), ("l2fr", 2), ("l2fl", 1), ("l2fp", 1), ("l2fx", 2), ("l2fw", 2 * NT), ("l2fy", 2),
                        ("l2fz", 2)):
        run(name, times)
    run("l3an", 2)
    run("l3ap", NT)
    run("l3am", 2)
    run("l3ay", 2)
    narrow("l3x", 2)
    run("l3fn", 2)
    run("l3fs", 4)
    run("l3fg", 2 * GROUPS3)
    item(m, "l3fj0", 6, PAIR3.uses)
    item(m, "l3fj1", 7, PAIR3.uses)
    for name in ("y", "z", "m", "u", "w"):
        run(f"l3f{name}", 2)
    m.slot0 = {"l0f": 0, "l1a": E0 // 2, "l2f": E0 // 2 + NPAIR // 2}
    at = m.slot0["l2f"] + E2 // 4
    for name in ("l3v", "l3q", "l3o"):
        m.slot0[name] = at
        at += NPAIR // 2
    m.h0 = {"l0f": 0, "l3f": 8 * E0}
    m.steps0, m.half0, m.cross0 = {}, {}, {}
    own = cross = 0
    for stage, kind, steps in (("l0a", "self", 8 * STEPS), ("l0x", "cross", XSTEPS), ("l1a", "self", 8 * STEPS),
                               ("l1x", "cross", XSTEPS), ("l2a", "self", B * NQ), ("l2x", "cross", XSTEPS),
                               ("l3x", "cross", XSTEPS), ("l3f", "self", 8 * STEPS)):
        m.steps0[stage], m.half0[stage], m.cross0[stage] = own + cross, own // 2, cross
        if kind == "self":
            own += steps
        else:
            cross += steps
def build(nc, shapes, dram, out):
    m = Core()
    with ExitStack() as ctx:
        def sb(name, shape, dt=F32):
            return ctx.enter_context(nc.sbuf_tensor(name, shape, dt))

        def sem(name):
            return ctx.enter_context(nc.semaphore(name))

        m.psum = ctx.enter_context(nc.psum_tensor("psum", [P, 8, S], F32))
        m.ps = [m.psum[:, b, :] for b in range(8)]
        m.x = sb("x", [P, NT, P])
        m.xn = sb("xn", [P, NT, P])
        m.xn_t = sb("xn_t", [P, T])
        m.q_t = sb("q_t", [P, T])
        m.k_t = sb("k_t", [P, T])
        m.v = sb("v", [P, NT, P])
        m.o_t = sb("o_t", [P, T])
        m.y_t = m.o_t
        heads = sb("heads", [P, 4, T])
        m.head_qs = heads[:, 0:2, :]
        m.head_vals = heads[:, 2:4, :].rearrange("p n (t d) -> p n t d", d=P)
        m.wide = sb("wide", [P, NPAIR, T])
        m.p = sb("p", [P, 4, S])
        m.xp = m.p[:, :, :].rearrange("p a s -> p (a s)")[:, 0:3 * 8 * (SC + 1)].rearrange("p (n s) -> p n s", n=3)
        m.pt = sb("pt", [P, 4, NQ, S])
        m.xpt = m.pt[:, :, :, :].rearrange("p (n a) h s -> p n (a h) s", a=2)
        m.keys_own = sb("keys_own", [P, B, H * (SC + 1)])
        m.context_t = sb("context_t", [P, B * SC])
        m.context_v = sb("context_v", [P, B, H * 64])
        m.mask_words = sb("mask_words", [1, 2 * B * SC // 4], I32)
        m.mask_u8 = m.mask_words[:, :].bitcast(U8)
        m.mask_low = sb("mask_low", [1, 2 * B * SC])
        m.mask_row = sb("mask_row", [1, B, 4 * (SC + 1)], BF16)
        m.ones_bf = sb("ones_bf", [1, P], BF16)
        m.pair_q = [m.q_t, m.k_t]
        m.pair_k = heads[:, :, :].rearrange("p (s e) n -> p s e n", e=2)
        m.pair_v = [m.v, m.o_t[:, :].rearrange("p (t d) -> p t d", d=P)]
        m.latent_t = m.keys_own[:, 0, 0:T]
        m.slots_all = sb("slots", [P, 2 * SLOT_W])
        m.slots = m.slots_all[:, :].rearrange("p (s n) -> p s n", s=2)
        more = m.keys_own[:, :, :].rearrange("p a b -> p (a b)")
        m.slot = [m.slots[:, 0, :], m.slots[:, 1, :], more[:, 0:SLOT_W], more[:, SLOT_W:2 * SLOT_W]]
        m.context = sb("context", [SC, B, DC])
        m.context_norm_t = sb("context_norm_t", [P, B * SC])
        m.context_kv = m.context_v[:, :, 0:2 * P]
        tiles = lambda ap: ap.rearrange("p (t d) -> p t d", d=P)
        m.q_tok, m.k_tok, m.squares = (tiles(m.wide[:, n, :]) for n in range(3))
        m.tail_pt = m.wide[:, 4:8, 0:S]
        m.ints = m.slots_all[:, 0:3 * F1].bitcast(I32)
        m.cast_w = m.keys_own[:, 0, 0:3 * F1]
        m.context_k = m.context_norm_t
        m.values_own = heads[:, :, :].rearrange("p (b n) (h d) -> p b (n h) d", b=B, d=P)
        m.numbers = sb("numbers", [P, 8 * XSTEPS])
        m.number = sb("number", [P, 3])
        m.average = sb("average", [P, B])
        m.share = sb("share", [P, 1])
        m.ones_row = sb("ones_row", [1, P])
        m.logits, m.left, m.places, m.running = m.q_t, m.k_t, m.o_t, heads[:, 0, :]
        m.probs16 = sb("probs16", [P, NT, E2])
        m.place = sb("place", [P, NT, E2])
        m.top8 = sb("top8", [P, 2, 8])
        m.needed = sb("needed", [P, 2])
        m.ones_col = sb("ones_col", [P, 1])
        m.chosen_t = m.xn_t
        m.weighted = m.pt[:, :, :, :].rearrange("p n (a b) s -> p (n a) (b s)", b=2)
        m.expert_h = sb("expert_h", [P, 4, F2 // P * CAP])
        m.rms = sb("rms", [P, 4 * NT + 2 * B])
        m.low_row = sb("low_row", [1, B * SC], BF16)
        m.hidden = m.p
        columns = {"q": 64, "gate": 64, "v": P, "g": P, "decay": 64, "k": 64, "qk": 64, "aug": P, "sig_g": P, "o": P}
        m.gla, at = {"tmp": m.v[:, :, :]}, 0
        for name, n in columns.items():
            m.gla[name] = m.wide[:, :, at:at + n]
            at += n
        m.select = sb("select", [P, 16, P], BF16)
        m.pick = m.p[:, :, :].rearrange("p a s -> p (a s)")
        flat = m.pt[:, :, :, :].rearrange("p a b s -> p (a b s)")
        m.pick_tmp, m.pick_first = flat[:, 2048:4096], flat[:, 4096:6144]
        m.pick_best = flat[:, 6144:6144 + 3 * NT * 2 * H]
        m.gate_parts = flat[:, 0:2048].bitcast(BF16).rearrange("p (t q c g) -> p t q c g", q=GROUPS3, c=4, g=32)
        m.gated = flat[:, 0:2048].rearrange("p (n s) -> p n s", s=S)
        m.gate_rows = m.keys_own[:, :, :].rearrange("p a b -> p (a b)")[:, 0:2048].bitcast(BF16).rearrange(
            "p (q n) -> p q n", q=GROUPS3)
        m.rope_tmp = m.context_v[:, :, :].rearrange("p s (r n) -> p s r n", n=S)
        m.gates = sb("gates", [P, NT, E0])
        m.gate_t = m.q_t
        m.pairs = m.pt[:, 0:2, 0, :].rearrange("p n (t e j) -> p n t e j", e=E0, j=E0)
        m.keep = sb("keep", [P, 2, NT, E0])
        m.per_token = sb("per_token", [P, 4, NT])
        m.xmax = sb("xmax", [P, 2, 8])
        m.xsum = sb("xsum", [P, 8 * XSTEPS])
        m.xrsum = sb("xrsum", [P, 2, 8])
        m.negmax = sb("negmax", [P, 4])
        m.sum = sb("sum", [P, 4])
        m.rsum = sb("rsum", [P, 4])
        m.stats = sb("stats", [P, NT, nc.vector.BN_STATS_DIM])
        m.moments = sb("moments", [P, NT, 2])
        m.var = sb("var", [P, NT])
        m.rstd = sb("rstd", [P, NT])
        m.minus_half = sb("minus_half", [P, NT])
        m.zeros = sb("zeros", [P, P])
        m.ident = sb("ident", [P, P])
        m.ident_bf = sb("ident_bf", [P, P], BF16)
        m.future_bf = sb("future", [P, P], BF16)
        m.rows8 = sb("rows8", [P, H + 1])
        m.cols8 = sb("cols8", [P, H + 1, P])
        m.weights, m.w, m.loaded = {}, {}, {}
        widths = [sum(n for _, n in parts) for parts in shapes.values()]
        arenas = [sb(f"weights{n}", [P, max(widths[n::2], default=1)]) for n in range(2)]
        for stage, parts in shapes.items():
            width = sum(n for _, n in parts)
            m.weights[stage] = arenas[len(m.weights) % 2][:, 0:width]
            m.loaded[stage] = sem(f"loaded_{stage}")
            at, m.w[stage] = 0, {}
            for name, n in parts:
                m.w[stage][name] = m.weights[stage][:, at:at + n]
                at += n
        m.consts = [("ident", m.ident[:, :]), ("future", m.wide[:, 2, 0:P]),
                    ("rows8", m.rows8[:, :]), ("cols8", m.cols8[:, :, :]), ("zeros", m.zeros[:, :]),
                    ("share", m.share[:, :]), ("ones_col", m.ones_col[:, :]), ("select", m.wide[:, 0:2, :].rearrange("p a (e o) -> p (a e) o", o=P)), ("ones_row", m.ones_row[:, :]), ("minus_half", m.minus_half[:, :])]
        m.n_consts = len(m.consts)
        m.filled = {b: sem(f"filled{b}") for b in (6, 7)}
        m.emptied = {b: sem(f"emptied{b}") for b in (6, 7)}
        m.conv_done = sem("conv_done")
        m.gla_ready = sem("gla_ready")
        m.gla_exp = sem("gla_exp")
        m.head_var_ready = sem("head_var_ready")
        m.head_rstd_ready = sem("head_rstd_ready")
        m.pick_exp = sem("pick_exp")
        m.pick_ready = sem("pick_ready")
        m.parts_zero = sem("parts_zero")
        m.parts_ready = sem("parts_ready")
        m.mixed_ready = sem("mixed_ready")
        m.mixed_taken = sem("mixed_taken")
        m.mixed_gated = sem("mixed_gated")
        m.mixed_halved = sem("mixed_halved")
        m.mixed_added = sem("mixed_added")
        m.rope_added = sem("rope_added")
        m.spread_ready = sem("spread_ready")
        m.spread_gated = sem("spread_gated")
        m.spread_used = sem("spread_used")
        m.x_in = sem("x_in")
        m.consts_in = sem("consts_in")
        m.out_done = sem("out_done")
        m.var_ready = sem("var_ready")
        m.rstd_ready = sem("rstd_ready")
        m.consts_cast = sem("consts_cast")
        m.xn_ready = sem("xn_ready")
        m.scores_ready = sem("scores_ready")
        m.negmax_ready = sem("negmax_ready")
        m.exp_done = sem("exp_done")
        m.rsum_ready = sem("rsum_ready")
        m.probs_ready = sem("probs_ready")
        m.turned_ready = sem("turned_ready")
        m.pv_done = sem("pv_done")
        m.head_q = sem("head_q")
        m.head_v = sem("head_v")
        m.cross_taken = sem("cross_taken")
        m.keys_zero = sem("keys_zero")
        m.cross_ready = sem("cross_ready")
        m.context_in = sem("context_in")
        m.stage_done = sem("stage_done")
        m.gates_out = sem("gates_out")
        m.places_ready = sem("places_ready")
        m.chosen_ready = sem("chosen_ready")
        m.weighted_ready = sem("weighted_ready")
        m.expert_hidden = sem("expert_hidden")
        m.expert_biased = sem("expert_biased")
        m.expert_gelu = sem("expert_gelu")
        m.expert_y_ready = sem("expert_y_ready")
        m.expert_taken = sem("expert_taken")
        m.ints_in = sem("ints_in")
        m.ints_cast = sem("ints_cast")
        m.swiglu_ready = sem("swiglu_ready")
        m.swiglu_exp = sem("swiglu_exp")
        m.swiglu_done = sem("swiglu_done")
        m.swiglu_added = sem("swiglu_added")
        m.narrow_keys = sem("narrow_keys")
        m.narrow_values = sem("narrow_values")
        m.sums_are_numbers = sem("sums_are_numbers")
        m.context_normed = sem("context_normed")
        m.low_row_ready = sem("low_row_ready")
        m.rms_ready = sem("rms_ready")
        m.rms_inverted = sem("rms_inverted")
        m.rms_done = sem("rms_done")
        m.tail_taken = sem("tail_taken")
        m.pair_zero = sem("pair_zero")
        m.gates_in = [sem("gates_in0"), sem("gates_in1")]
        m.gates_ready = sem("gates_ready")
        m.router_less_max = sem("router_less_max")
        m.router_exp = sem("router_exp")
        m.hidden_ready = sem("hidden_ready")
        m.hidden_read = sem("hidden_read")
        m.hidden_gated = sem("hidden_gated")
        m.hidden_used = sem("hidden_used")
        m.turned_taken = [sem("turned_taken0"), sem("turned_taken1")]
        m.values_in = [sem("values_in0"), sem("values_in1")]
        m.slot_in = [sem(f"slot_in{n}") for n in range(4)]
        plan(m)
        block = ctx.enter_context(nc.Block())

        @block.sync
        def _(sp):
            sp.dma_start(m.x[:, :, :], dram["x"]).then_inc(m.x_in, 16)
            for name, dst in m.consts:
                sp.dma_start(dst, dram[name]).then_inc(m.consts_in, 16)
            sp.dma_start(m.context_t[0:DC, :], dram["context_t"]).then_inc(m.context_in, 16)
            sp.dma_start(m.context[:, :, :], dram["context"]).then_inc(m.context_in, 16)
            sp.dma_start(m.mask_words[:, :], dram["masks"]).then_inc(m.context_in, 16)
            for b in range(B):
                sp.dma_start(m.context_v[SC:SC + 1, b, :], dram["null_v"]).then_inc(m.context_in, 16)
            stages = [stage[0] for stage in STAGES]
            for n in range(2):
                sp.dma_start(m.weights[stages[n]], dram[f"w_{stages[n]}"]).then_inc(m.loaded[stages[n]], 16)
            for n, stage in enumerate(STAGES):
                if 0 < n < len(stages) - 1:
                    sp.wait_ge(m.stage_done, n)
                    sp.dma_start(m.weights[stages[n + 1]], dram[f"w_{stages[n + 1]}"]).then_inc(
                        m.loaded[stages[n + 1]], 16)
                if stage[5]:
                    stage[5](nc, sp, m, dram)
            sp.wait_ge(m.stage_done, len(STAGES))
            sp.dma_start(out, m.x[:, :, :]).then_inc(m.out_done, 16)
            sp.wait_ge(m.out_done, 16)

        @block.gpsimd
        def _(pool):
            pool.wait_ge(m.consts_in, 16 * m.n_consts)
            nc.gpsimd.memset(m.mask_row[:, :, :], 0.0)
            nc.gpsimd.memset(m.ones_bf[:, :], 1.0)
            nc.gpsimd.memset(m.keys_own[:, :, :], 0.0).then_inc(m.keys_zero, 1)
            for stage in STAGES:
                stage[4](nc, pool, m)

        @block.scalar
        def _(act):
            act.wait_ge(m.consts_in, 16 * m.n_consts)
            nc.scalar.activation(m.ident_bf[:, :], m.ident[:, :], ACT.Copy).then_inc(m.consts_cast, 1)
            nc.scalar.activation(m.future_bf[:, :], m.wide[:, 2, 0:P], ACT.Copy).then_inc(m.consts_cast, 1)
            nc.scalar.activation(m.select[:, :, :], m.wide[:, 0:2, :].rearrange("p a (e o) -> p (a e) o", o=P),
                                 ACT.Copy).then_inc(m.consts_cast, 1)
            for stage in STAGES:
                stage[2](nc, act, m)

        @block.vector
        def _(dve):
            m.dve = Chain(dve, ctx.enter_context(nc.semaphore("vector_chain")))
            dve.wait_ge(m.consts_in, 16 * m.n_consts)
            for stage in STAGES:
                stage[3](nc, dve, m)
                dve.sem_inc(m.stage_done, 1)

        @block.tensor
        def _(pe):
            for stage in STAGES:
                stage[1](nc, pe, m)


STAGES = [
    ("l0a", l0_attn_tensor, l0_attn_scalar, l0_attn_vector, l0_attn_gpsimd, None),
    ("l0x", l0_cross_tensor, l0_cross_scalar, l0_cross_vector, l0_cross_gpsimd, None),
    ("l0f", l0_ffn_tensor, l0_ffn_scalar, l0_ffn_vector, l0_ffn_gpsimd, l0_ffn_sync),
    ("l1a", l1_attn_tensor, l1_attn_scalar, l1_attn_vector, l1_attn_gpsimd, l1_attn_sync),
    ("l1x", l1_cross_tensor, l1_cross_scalar, l1_cross_vector, l1_cross_gpsimd, None),
    ("l1f", l1_ffn_tensor, l1_ffn_scalar, l1_ffn_vector, one_norm_gpsimd, l1_ffn_sync),
    ("l2a", l2_attn_tensor, l2_attn_scalar, l2_attn_vector, one_norm_gpsimd, None),
    narrow_cross("l2x", clip=10000.0),
    ("l2f", l2_ffn_tensor, l2_ffn_scalar, l2_ffn_vector, l2_ffn_gpsimd, l2_ffn_sync),
    ("l3a", l3_attn_tensor, l3_attn_scalar, l3_attn_vector, l3_attn_gpsimd, None),
    narrow_cross("l3x"),
    ("l3f", l3_ffn_tensor, l3_ffn_scalar, l3_ffn_vector, l3_ffn_gpsimd, l3_ffn_sync),
]



def rows(a):
    out = np.zeros((P, a.shape[1]), a.dtype)
    out[:a.shape[0]] = a
    return out


def column(a):
    return a.reshape(-1, 1)


def every(a):
    return np.tile(a.reshape(1, -1), (P, 1))


def layout(v):
    w = v["L0_attn_c_attn_kernel"]
    bias = v["L0_attn_c_attn_bias"]
    packs = {
        "l0a": [("wq", w[0:P].T), ("wk", w[P:2 * P].T), ("wv", w[2 * P:].T),
                ("wo", v["L0_attn_c_proj_kernel"].T), ("bq", column(bias[0:P])), ("bk", column(bias[P:2 * P])),
                ("bv", every(bias[2 * P:])), ("bo", every(v["L0_attn_c_proj_bias"]))],
        "l0x": [("wq", v["L0_xattn_Wq"]), ("wk", v["L0_xattn_Wkv"][:, 0:H * 64]), ("wv", v["L0_xattn_Wkv"][:, H * 64:]),
                ("wo", v["L0_xattn_Wout"].reshape(NPAIR, P, P).transpose(1, 0, 2).reshape(P, NPAIR * P)),
                ("g_norm", column(v["L0_xattn_g_norm"])), ("g_out", every(v["L0_xattn_g_out"])),
                ("null_k", column(np.tile(v["L0_xattn_null_kv"][0], 2)))],
        "l0f": [("wr", v["L0_ffn_Wr"]), ("br", every(v["L0_ffn_br"])), ("b2", v["L0_ffn_b2"]),
                ("not_after", every(np.tril(np.ones((E0, E0), np.float32))))],
        "l1a": [("down", v["L1_attn_Wkv_down"]),
                ("wo", v["L1_attn_Wout"].reshape(NPAIR, P, P).transpose(1, 0, 2).reshape(P, NPAIR * P))],
    }
    packs["l1x"] = [
        ("wq", v["L1_xattn_Wq"].T), ("wkv", v["L1_xattn_Wkv"].T), ("wlk", v["L1_xattn_Wlkv"][0:P].T),
        ("wlv", v["L1_xattn_Wlkv"][P:].T), ("wo", v["L1_xattn_Wo"].T), ("ln_l_g", column(v["L1_xattn_ln_l_g"])),
        ("ln_l_b", column(v["L1_xattn_ln_l_b"])), ("ln_x_g", every(v["L1_xattn_ln_x_g"])),
        ("ln_x_b", every(v["L1_xattn_ln_x_b"])), ("qn_g", column(np.tile(v["L1_xattn_qn_g"], 2))),
        ("kn_g", column(np.tile(v["L1_xattn_kn_g"], 2))), ("bo", every(v["L1_xattn_bo"]))]
    w = v["L2_attn_w_qkv"]
    packs["l1f"] = [("none", np.zeros((P, 1), np.float32))]
    packs["l2a"] = [("wq", w[0:P].T), ("wk", w[P:2 * P].T), ("wv", w[2 * P:].T), ("wo", v["L2_attn_w_proj"].T),
                    ("bo", every(v["L2_attn_b_proj"]))]
    packs["l2x"] = [("wq", v["L2_xattn_Wq"]), ("wk", v["L2_xattn_Wk"]), ("wv", v["L2_xattn_Wv"]), ("wo", v["L2_xattn_Wo"]),
                    ("bq", column(v["L2_xattn_bq"])), ("bk", column(v["L2_xattn_bk"])), ("bv", every(v["L2_xattn_bv"])),
                    ("bo", every(v["L2_xattn_bo"]))]
    packs["l2f"] = [("router", v["L2_ffn_router_weight"].T), ("router_b", column(v["L2_ffn_router_bias"])),
                    ("norm_w", every(v["L2_ffn_norm_weight"])),
                    ("one_to_cap", every(np.arange(1, CAP + 1, dtype=np.float32)))]
    split = lambda g: np.concatenate(g, axis=1)
    packs["l3a"] = [("wqkvg", split([v["L3_attn_Wq"], v["L3_attn_Wkg"], v["L3_attn_Wv"], v["L3_attn_Wg"]])),
                    ("wo", v["L3_attn_Wout"]), ("bg", every(v["L3_attn_bg"])),
                    ("aug_balance", every(v["L3_attn_aug_balance"])), ("conv", v["L3_attn_conv_w"])]
    packs["l3x"] = [("wq", v["L3_xattn_w_q"]), ("wk", v["L3_xattn_w_k"]), ("wv", v["L3_xattn_w_v"]),
                    ("wo", v["L3_xattn_w_o"]), ("bq", column(v["L3_xattn_b_q"])), ("bk", column(v["L3_xattn_b_k"])),
                    ("bv", every(v["L3_xattn_b_v"])), ("bo", every(v["L3_xattn_b_o"]))]
    cos, sin = rope_tables()
    packs["l3f"] = [("wsel", split([v["L3_ffn_Wsel_v"].reshape(P, P).T, v["L3_ffn_Wsel_o"].reshape(P, P).T])),
                    ("w1", v["L3_ffn_W1"]), ("w2", v["L3_ffn_W2"].reshape(F3 // P, P, P).transpose(1, 0, 2).reshape(P, F3)),
                    ("b1", v["L3_ffn_b1"].reshape(F3 // P, P).T), ("falling", every(np.arange(E3, 0, -1, dtype=np.float32))),
                    ("cos", cos), ("sin", sin), ("cos_q", cos * np.float32(64 ** -0.5)), ("sin_q", sin * np.float32(64 ** -0.5))]
    packs["l3f"] += [(name, every(v["L3_ffn_" + name])) for name in ("ln1_g", "ln1_b", "ln2_g", "ln2_b", "b2")]
    return packs


def rope_tables():
    inverse = (10000.0 ** (-np.arange(ROT // 2) / (ROT // 2))).astype(np.float32)
    angle = np.arange(S, dtype=np.float32)[None, :] * inverse[:, None]
    head_cos, head_sin = np.ones((64, S), np.float32), np.zeros((64, S), np.float32)
    head_cos[0:ROT // 2], head_cos[ROT // 2:ROT] = np.cos(angle), np.cos(angle)
    head_sin[0:ROT // 2], head_sin[ROT // 2:ROT] = -np.sin(angle), np.sin(angle)
    return np.tile(head_cos, (2, 1)), np.tile(head_sin, (2, 1))


def turned_features(w):
    partner = np.arange(64)
    partner[0:ROT] = np.roll(partner[0:ROT], ROT // 2)
    return w.reshape(P, H, 64)[:, :, partner].reshape(P, H * 64)


def streams(v):
    return {
        "l0f": np.concatenate([v["L0_ffn_W1"], v["L0_ffn_W2"].reshape(E0, 4, P, P).transpose(0, 2, 1, 3).reshape(E0, P, F0),
                               v["L0_ffn_b1"].reshape(E0, 4, P).transpose(0, 2, 1)], axis=2),
        "l2f": np.concatenate([v["L2_ffn_fc1_weight"].transpose(0, 2, 1),
                               v["L2_ffn_fc2_weight"].reshape(E2, P, F2 // P, P).transpose(0, 3, 2, 1).reshape(E2, P, F2),
                               v["L2_ffn_fc1_bias"].reshape(E2, F2 // P, P).transpose(0, 2, 1),
                               np.broadcast_to(v["L2_ffn_fc2_bias"][:, None, :], (E2, P, P))], axis=2),
        "l1a": np.concatenate([by_pair(v["L1_attn_Wq"].reshape(P, H * 64)),
                               by_pair(rows(v["L1_attn_Wk_up"].reshape(LATENT, H * 64))),
                               by_pair(rows(v["L1_attn_Wv_up"].reshape(LATENT, H * 64)))], axis=2),
        "l3v": v["L3_ffn_Wv"].reshape(NPAIR, 2, E3, P, 64).transpose(0, 3, 1, 2, 4).reshape(NPAIR, P, 2 * E3 * 64),
        "l3q": np.concatenate([by_pair(turn(v[name].transpose(1, 0, 2).reshape(P, H * 64)))
                               for name in ("L3_ffn_Wq", "L3_ffn_Wk") for turn in (lambda w: w, turned_features)], axis=2),
        "l3o": v["L3_ffn_Wo"].reshape(NPAIR, 2, E3, 64, P).transpose(0, 1, 3, 2, 4).reshape(NPAIR, P, E3 * P),
    }


def by_pair(w):
    return w.reshape(P, NPAIR, P).transpose(1, 0, 2)


def constants():
    head = np.arange(P) // (P // H)
    own = (head[:, None] == np.arange(H + 1)[None, :]).astype(np.float32)
    select = np.zeros((4, 32, 2, E3, 2, 64), np.float32)
    for pair in range(2):
        for h in range(2):
            for e in range(E3):
                select[0:3, (2 * pair + h) * E3 + e, pair, e, h, :] = 1
    return {
        "select": select.reshape(P, 16, P),
        "ident": np.eye(P, dtype=np.float32),
        "future": np.where(np.arange(P)[None, :] > np.arange(P)[:, None], np.float32(-BIG), np.float32(0)),
        "rows8": own * np.float32((P // H) ** -0.5),
        "cols8": np.ascontiguousarray(np.broadcast_to(own.T[None], (P, H + 1, P))),
        "zeros": np.zeros((P, P), np.float32),
        "ones_col": np.ones((P, 1), np.float32),
        "share": np.full((P, 1), 1.0 / SC, np.float32),
        "ones_row": np.ones((1, P), np.float32),
        "minus_half": np.full((P, NT), -0.5, np.float32),
    }


def kernel(**inputs):
    import concourse.bacc as bacc
    from concourse.bass_utils import run_bass_kernel_spmd

    v = {name: np.asarray(a) for name, a in inputs.items()}
    packs = layout(v)
    arrays = {"x": np.ascontiguousarray(v["x"].reshape(NT, P, P).transpose(1, 0, 2))}
    arrays |= constants()
    arrays["context_t"] = np.ascontiguousarray(v["ctx_768"].transpose(2, 0, 1).reshape(DC, B * SC))
    arrays["context"] = np.ascontiguousarray(v["ctx_768"].transpose(1, 0, 2))
    arrays["ints"] = np.concatenate([v["L1_ffn_w_gate"].T, v["L1_ffn_w_up"].T, v["L1_ffn_w_down"].reshape(P, F1 // P, P)
                                     .transpose(2, 1, 0).reshape(P, F1)], axis=1)
    arrays["masks"] = np.stack([v["mask_BxS2_bf1"], v["mask_BxS2_bk0"]]).reshape(1, -1).view(np.int32)
    arrays["null_v"] = np.tile(v["L0_xattn_null_kv"][1], H).reshape(1, -1)
    for stage, parts in packs.items():
        arrays[f"w_{stage}"] = np.concatenate([rows(a) for _, a in parts], axis=1)
    arrays |= {f"s_{stage}": np.ascontiguousarray(a) for stage, a in streams(v).items()}
    shapes = {stage: [(name, a.shape[1]) for name, a in parts] for stage, parts in packs.items()}

    nc = bacc.Bacc("TRN2", target_bir_lowering=False, num_devices=1)
    dram = {name: nc.dram_tensor(f"in_{name}", a.shape, mybir.dt.from_np(a.dtype), kind="ExternalInput").ap()
            for name, a in arrays.items()}
    dram["scratch_gates"] = nc.dram_tensor("scratch_gates", (E0, T), F32, kind="Internal").ap()
    out = nc.dram_tensor("out", (P, NT, P), F32, kind="ExternalOutput").ap()
    build(nc, shapes, dram, out)
    got = run_bass_kernel_spmd(nc, [{f"in_{name}": a for name, a in arrays.items()}], core_ids=[0])
    return got.results[0]["out"].transpose(1, 0, 2).reshape(B, S, P)
```
